# Optimizing a Trainium2 kernel written in Bass

```python
import numpy as np
import jax
import jax.numpy as jnp

def _softmax(x, axis=-1):
    return jax.nn.softmax(x, axis=axis)

def _gelu(x):
    return jax.nn.gelu(x, approximate=True)

def _silu(x):
    return jax.nn.silu(x)

def _sigmoid(x):
    return jax.nn.sigmoid(x)

def _layernorm(x, axis=-1, eps=1e-05):
    m = jnp.mean(x, axis=axis, keepdims=True)
    v = jnp.var(x, axis=axis, keepdims=True)
    return (x - m) / jnp.sqrt(v + eps)

def _scatter_add(tgt, idx, src, axis=0):
    return tgt.at[idx].add(src)

def _segment_sum(src, seg, n):
    return jax.ops.segment_sum(src, seg, n)
kernel_name = 'mk_vit_tower_cls_d4_tok_img1024_r4_60f518'

def setup_inputs(seed: int=0):
    np.random.seed(seed)
    _w = jnp.asarray

    def _rec_inputs():
        import jax
        import jax.numpy as jnp
        _rk = jax.random.key(seed)
        x = -0.00011082 + 0.999858 * jax.random.normal(jax.random.fold_in(_rk, 1), (4, 5, 128, 128), jnp.float32)
        cls_tok = 0.02 * jax.random.normal(jax.random.fold_in(_rk, 5), (1, 1, 256), jnp.float32)
        return (x, cls_tok)
    x, cls_tok = _rec_inputs()

    def _L0_tok_setup():
        import jax, jax.numpy as jnp
        import numpy as np
        PATCH = 8
        EPS = 1e-05

        def _patchify(x):
            B, C, H, Wd = x.shape
            p = PATCH
            x = x.reshape(B, C, H // p, p, Wd // p, p)
            x = x.transpose(0, 2, 4, 1, 3, 5)
            return x.reshape(B, H // p * (Wd // p), C * p * p)
        key = jax.random.key(seed)
        k1, k2 = jax.random.split(key)
        B, C, H, W_ = (32, 5, 128, 128)
        in_feat, embed_dim = (C * PATCH * PATCH, 256)
        x = jax.random.normal(k1, (B, C, H, W_), dtype=jnp.float32)
        W = jax.random.normal(k2, (in_feat, embed_dim), dtype=jnp.float32) * (1.0 / np.sqrt(in_feat))
        gamma = jnp.ones((embed_dim,), dtype=jnp.float32)
        return {'x': x, 'W': W, 'gamma': gamma}
    _L0_tok_all = _L0_tok_setup()
    _L0_tok_in = {k: v for k, v in _L0_tok_all.items() if k in ('W', 'gamma')}
    del _L0_tok_all

    def _L0_attn_setup():
        import jax, jax.numpy as jnp
        import numpy as np
        D_MODEL = 256
        D_HEAD = 64
        N_HEADS = 16
        STATE = 64
        D_INNER = D_HEAD * N_HEADS
        B, T = (4, 512)
        LN_EPS = 1e-05

        def _linear_params(key, fan_out, fan_in):
            k1, k2 = jax.random.split(key)
            s = 1.0 / np.sqrt(fan_in)
            W = jax.random.uniform(k1, (fan_out, fan_in), jnp.float32, -s, s)
            b = jax.random.uniform(k2, (fan_out,), jnp.float32, -s, s)
            return (W, b)

        def _layer_norm(x, gamma, beta):
            mu = jnp.mean(x, axis=-1, keepdims=True)
            var = jnp.mean(jnp.square(x - mu), axis=-1, keepdims=True)
            return (x - mu) * jax.lax.rsqrt(var + LN_EPS) * gamma + beta
        key = jax.random.key(seed)
        ks = jax.random.split(key, 8)
        WQ, bQ = _linear_params(ks[0], D_INNER, D_MODEL)
        WK, bK = _linear_params(ks[1], D_INNER, D_MODEL)
        WV, bV = _linear_params(ks[2], D_INNER, D_MODEL)
        WO, bO = _linear_params(ks[3], D_MODEL, D_INNER)
        Wg, bg = _linear_params(ks[4], D_INNER, D_MODEL)
        alpha_logit = jax.random.normal(ks[5], (N_HEADS, STATE), jnp.float32) * 0.1
        ln_gamma = jnp.ones((D_MODEL,), jnp.float32)
        ln_beta = jnp.zeros((D_MODEL,), jnp.float32)
        x = jax.random.normal(ks[6], (B, T, D_MODEL), jnp.float32)
        return {'x': x, 'WQ': WQ, 'bQ': bQ, 'WK': WK, 'bK': bK, 'WV': WV, 'bV': bV, 'WO': WO, 'bO': bO, 'Wg': Wg, 'bg': bg, 'alpha_logit': alpha_logit, 'ln_gamma': ln_gamma, 'ln_beta': ln_beta}
    _L0_attn_all = _L0_attn_setup()
    _L0_attn_in = {k: v for k, v in _L0_attn_all.items() if k in ('WQ', 'bQ', 'WK', 'bK', 'WV', 'bV', 'WO', 'bO', 'Wg', 'bg', 'alpha_logit', 'ln_gamma', 'ln_beta')}
    del _L0_attn_all

    def _L0_ffn_setup():
        import jax, jax.numpy as jnp
        import numpy as np
        H = 256
        I = 4 * H
        E = 8
        TOP_K = 2
        key = jax.random.key(seed)
        ks = jax.random.split(key, 6)
        s = 0.02
        hidden_states = jax.random.normal(ks[0], (4, 1024, H), dtype=jnp.float32)
        w1_shared = jax.random.normal(ks[1], (H, I), dtype=jnp.float32) * s
        w2_shared = jax.random.normal(ks[2], (I, H), dtype=jnp.float32) * s
        w1_routed = jax.random.normal(ks[3], (E, H, I), dtype=jnp.float32) * s
        w2_routed = jax.random.normal(ks[4], (E, I, H), dtype=jnp.float32) * s
        w_router = jax.random.normal(ks[5], (H, E), dtype=jnp.float32) * s
        return {'hidden_states': hidden_states, 'w1_shared': w1_shared, 'w2_shared': w2_shared, 'w1_routed': w1_routed, 'w2_routed': w2_routed, 'w_router': w_router}
    _L0_ffn_all = _L0_ffn_setup()
    _L0_ffn_in = {k: v for k, v in _L0_ffn_all.items() if k in ('w1_shared', 'w2_shared', 'w1_routed', 'w2_routed', 'w_router')}
    del _L0_ffn_all

    def _L1_attn_setup():
        import jax, jax.numpy as jnp
        import numpy as np
        D_MODEL = 256
        N_HEADS = 16
        D_HEAD = 64
        B, S = (8, 256)
        EPS = 1.1920929e-07
        key = jax.random.key(seed)
        k1, k2, k3 = jax.random.split(key, 3)
        x = jax.random.normal(k1, (B, S, D_MODEL), dtype=jnp.float32)
        W_qkv = jax.random.normal(k2, (3 * N_HEADS * D_HEAD, D_MODEL), dtype=jnp.float32) * 0.02
        b_qkv = jnp.zeros((3 * N_HEADS * D_HEAD,), dtype=jnp.float32)
        W_o = jax.random.normal(k3, (D_MODEL, N_HEADS * D_HEAD), dtype=jnp.float32) * 0.02
        b_o = jnp.zeros((D_MODEL,), dtype=jnp.float32)
        return {'x': x, 'W_qkv': W_qkv, 'b_qkv': b_qkv, 'W_o': W_o, 'b_o': b_o}
    _L1_attn_all = _L1_attn_setup()
    _L1_attn_in = {k: v for k, v in _L1_attn_all.items() if k in ('W_qkv', 'b_qkv', 'W_o', 'b_o')}
    del _L1_attn_all

    def _L1_ffn_setup():
        import jax, jax.numpy as jnp
        import numpy as np
        TOPK = 4
        N_GROUPS = 4
        TOPK_GROUPS = 2
        ROUTE_SCALE = 2.5

        def _gate(x2, Wg):
            T = x2.shape[0]
            E = Wg.shape[0]
            scores = x2 @ Wg.T
            s = jax.nn.sigmoid(scores)
            g = s.reshape(T, N_GROUPS, E // N_GROUPS)
            group_scores = g.max(axis=-1)
            _, gidx = jax.lax.top_k(group_scores, TOPK_GROUPS)
            group_mask = jnp.any(jax.nn.one_hot(gidx, N_GROUPS, dtype=jnp.bool_), axis=1)
            masked = jnp.where(group_mask[:, :, None], g, -jnp.inf).reshape(T, E)
            _, idx = jax.lax.top_k(masked, TOPK)
            w = jnp.take_along_axis(s, idx, axis=1)
            w = w / jnp.sum(w, axis=-1, keepdims=True)
            w = w * ROUTE_SCALE
            return (w.astype(x2.dtype), idx)
        key = jax.random.key(seed)
        ks = jax.random.split(key, 6)
        B, S, D, I, E = (2, 512, 256, 256, 16)
        scale = 0.02
        return {'x': jax.random.normal(ks[0], (B, S, D), dtype=jnp.float32), 'Wg': jax.random.normal(ks[1], (E, D), dtype=jnp.float32) * scale, 'W1': jax.random.normal(ks[2], (E, I, D), dtype=jnp.float32) * scale, 'b1': jnp.zeros((E, I), dtype=jnp.float32), 'W2': jax.random.normal(ks[3], (E, D, I), dtype=jnp.float32) * scale, 'b2': jnp.zeros((E, D), dtype=jnp.float32), 'W3': jax.random.normal(ks[4], (E, I, D), dtype=jnp.float32) * scale, 'b3': jnp.zeros((E, I), dtype=jnp.float32)}
    _L1_ffn_all = _L1_ffn_setup()
    _L1_ffn_in = {k: v for k, v in _L1_ffn_all.items() if k in ('Wg', 'W1', 'b1', 'W2', 'b2', 'W3', 'b3')}
    del _L1_ffn_all

    def _L2_attn_setup():
        import jax, jax.numpy as jnp
        import numpy as np
        DIM = 256
        HEADS = 16
        HEAD_DIM = DIM // HEADS

        def _xavier(key, shape):
            fan_out, fan_in = shape
            limit = float(np.sqrt(6.0 / (fan_in + fan_out)))
            return jax.random.uniform(key, shape, jnp.float32, -limit, limit)
        key = jax.random.key(seed)
        kx, kv, kk, kq = jax.random.split(key, 4)
        x = jax.random.normal(kx, (4, 512, DIM), jnp.float32)
        Wv = _xavier(kv, (DIM, DIM))
        Wk = _xavier(kk, (DIM, DIM))
        Wq = _xavier(kq, (DIM, DIM))
        return {'x': x, 'Wq': Wq, 'Wk': Wk, 'Wv': Wv}
    _L2_attn_all = _L2_attn_setup()
    _L2_attn_in = {k: v for k, v in _L2_attn_all.items() if k in ('Wq', 'Wk', 'Wv')}
    del _L2_attn_all

    def _L2_ffn_setup():
        import jax, jax.numpy as jnp
        import numpy as np
        B, S, H = (2, 512, 256)
        I = 128
        E_R, E_Z = (32, 8)
        E_T = E_R + E_Z
        K = 6
        SCALE = 2.5
        W_INIT = 0.02
        key = jax.random.key(seed)
        k0, k1, k2, k3 = jax.random.split(key, 4)
        return {'hidden_states': jax.random.normal(k0, (B, S, H), jnp.float32), 'classifier_weight': jax.random.normal(k1, (E_T, H), jnp.float32) * W_INIT, 'e_score_correction_bias': jnp.zeros((E_T,), jnp.float32), 'gate_up_proj': jax.random.normal(k2, (E_T, 2 * I, H), jnp.float32) * W_INIT, 'down_proj': jax.random.normal(k3, (E_R, H, I), jnp.float32) * W_INIT}
    _L2_ffn_all = _L2_ffn_setup()
    _L2_ffn_in = {k: v for k, v in _L2_ffn_all.items() if k in ('classifier_weight', 'e_score_correction_bias', 'gate_up_proj', 'down_proj')}
    del _L2_ffn_all

    def _L3_attn_setup():
        import jax, jax.numpy as jnp
        import numpy as np
        key = jax.random.key(seed)
        B, L, d_model, d_state, expand = (2, 512, 256, 16, 2)
        d_inner = expand * d_model
        ks = jax.random.split(key, 8)
        s = lambda k, shape, scale: jax.random.normal(k, shape, dtype=jnp.float32) * scale
        x = s(ks[0], (B, L, d_model), 1.0)
        W_in = s(ks[1], (d_model, 2 * d_inner), 0.02)
        W_delta = s(ks[2], (d_inner, d_inner), 0.02)
        b_delta = s(ks[3], (d_inner,), 0.02)
        W_B = s(ks[4], (d_inner, d_state), 0.02)
        W_C = s(ks[5], (d_inner, d_state), 0.02)
        A_log = jnp.log(jnp.broadcast_to(jnp.arange(1, d_state + 1, dtype=jnp.float32), (d_inner, d_state)))
        D_param = jnp.ones((d_inner,), dtype=jnp.float32)
        W_out = s(ks[6], (d_inner, d_model), 0.02)
        return dict(x=x, W_in=W_in, W_delta=W_delta, b_delta=b_delta, W_B=W_B, W_C=W_C, A_log=A_log, D_param=D_param, W_out=W_out)
    _L3_attn_all = _L3_attn_setup()
    _L3_attn_in = {k: v for k, v in _L3_attn_all.items() if k in ('W_in', 'W_delta', 'b_delta', 'W_B', 'W_C', 'A_log', 'D_param', 'W_out')}
    del _L3_attn_all

    def _L3_ffn_setup():
        import jax, jax.numpy as jnp
        import numpy as np
        B, S, D, H, E = (4, 512, 256, 1024, 8)
        key = jax.random.key(seed)
        ks = jax.random.split(key, 8)
        s_d = 1.0 / np.sqrt(D)
        s_h = 1.0 / np.sqrt(H)
        return {'x': jax.random.normal(ks[0], (B, S, D), dtype=jnp.float32), 'gate_w': jax.random.uniform(ks[1], (E, D), jnp.float32, -s_d, s_d), 'gate_b': jax.random.uniform(ks[2], (E,), jnp.float32, -s_d, s_d), 'w1': jax.random.uniform(ks[3], (E, H, D), jnp.float32, -s_d, s_d), 'b1': jax.random.uniform(ks[4], (E, H), jnp.float32, -s_d, s_d), 'w2': jax.random.uniform(ks[5], (E, D, H), jnp.float32, -s_h, s_h), 'b2': jax.random.uniform(ks[6], (E, D), jnp.float32, -s_h, s_h)}
    _L3_ffn_all = _L3_ffn_setup()
    _L3_ffn_in = {k: v for k, v in _L3_ffn_all.items() if k in ('gate_w', 'gate_b', 'w1', 'b1', 'w2', 'b2')}
    del _L3_ffn_all
    return {'x': x, 'cls_tok': cls_tok, 'L0_tok_W': _L0_tok_in['W'], 'L0_tok_gamma': _L0_tok_in['gamma'], 'L0_attn_WQ': _L0_attn_in['WQ'], 'L0_attn_bQ': _L0_attn_in['bQ'], 'L0_attn_WK': _L0_attn_in['WK'], 'L0_attn_bK': _L0_attn_in['bK'], 'L0_attn_WV': _L0_attn_in['WV'], 'L0_attn_bV': _L0_attn_in['bV'], 'L0_attn_WO': _L0_attn_in['WO'], 'L0_attn_bO': _L0_attn_in['bO'], 'L0_attn_Wg': _L0_attn_in['Wg'], 'L0_attn_bg': _L0_attn_in['bg'], 'L0_attn_alpha_logit': _L0_attn_in['alpha_logit'], 'L0_attn_ln_gamma': _L0_attn_in['ln_gamma'], 'L0_attn_ln_beta': _L0_attn_in['ln_beta'], 'L0_ffn_w1_shared': _L0_ffn_in['w1_shared'], 'L0_ffn_w2_shared': _L0_ffn_in['w2_shared'], 'L0_ffn_w1_routed': _L0_ffn_in['w1_routed'], 'L0_ffn_w2_routed': _L0_ffn_in['w2_routed'], 'L0_ffn_w_router': _L0_ffn_in['w_router'], 'L1_attn_W_qkv': _L1_attn_in['W_qkv'], 'L1_attn_b_qkv': _L1_attn_in['b_qkv'], 'L1_attn_W_o': _L1_attn_in['W_o'], 'L1_attn_b_o': _L1_attn_in['b_o'], 'L1_ffn_Wg': _L1_ffn_in['Wg'], 'L1_ffn_W1': _L1_ffn_in['W1'], 'L1_ffn_b1': _L1_ffn_in['b1'], 'L1_ffn_W2': _L1_ffn_in['W2'], 'L1_ffn_b2': _L1_ffn_in['b2'], 'L1_ffn_W3': _L1_ffn_in['W3'], 'L1_ffn_b3': _L1_ffn_in['b3'], 'L2_attn_Wq': _L2_attn_in['Wq'], 'L2_attn_Wk': _L2_attn_in['Wk'], 'L2_attn_Wv': _L2_attn_in['Wv'], 'L2_ffn_classifier_weight': _L2_ffn_in['classifier_weight'], 'L2_ffn_e_score_correction_bias': _L2_ffn_in['e_score_correction_bias'], 'L2_ffn_gate_up_proj': _L2_ffn_in['gate_up_proj'], 'L2_ffn_down_proj': _L2_ffn_in['down_proj'], 'L3_attn_W_in': _L3_attn_in['W_in'], 'L3_attn_W_delta': _L3_attn_in['W_delta'], 'L3_attn_b_delta': _L3_attn_in['b_delta'], 'L3_attn_W_B': _L3_attn_in['W_B'], 'L3_attn_W_C': _L3_attn_in['W_C'], 'L3_attn_A_log': _L3_attn_in['A_log'], 'L3_attn_D_param': _L3_attn_in['D_param'], 'L3_attn_W_out': _L3_attn_in['W_out'], 'L3_ffn_gate_w': _L3_ffn_in['gate_w'], 'L3_ffn_gate_b': _L3_ffn_in['gate_b'], 'L3_ffn_w1': _L3_ffn_in['w1'], 'L3_ffn_b1': _L3_ffn_in['b1'], 'L3_ffn_w2': _L3_ffn_in['w2'], 'L3_ffn_b2': _L3_ffn_in['b2']}

def reference(x, cls_tok, L0_tok_W, L0_tok_gamma, L0_attn_WQ, L0_attn_bQ, L0_attn_WK, L0_attn_bK, L0_attn_WV, L0_attn_bV, L0_attn_WO, L0_attn_bO, L0_attn_Wg, L0_attn_bg, L0_attn_alpha_logit, L0_attn_ln_gamma, L0_attn_ln_beta, L0_ffn_w1_shared, L0_ffn_w2_shared, L0_ffn_w1_routed, L0_ffn_w2_routed, L0_ffn_w_router, L1_attn_W_qkv, L1_attn_b_qkv, L1_attn_W_o, L1_attn_b_o, L1_ffn_Wg, L1_ffn_W1, L1_ffn_b1, L1_ffn_W2, L1_ffn_b2, L1_ffn_W3, L1_ffn_b3, L2_attn_Wq, L2_attn_Wk, L2_attn_Wv, L2_ffn_classifier_weight, L2_ffn_e_score_correction_bias, L2_ffn_gate_up_proj, L2_ffn_down_proj, L3_attn_W_in, L3_attn_W_delta, L3_attn_b_delta, L3_attn_W_B, L3_attn_W_C, L3_attn_A_log, L3_attn_D_param, L3_attn_W_out, L3_ffn_gate_w, L3_ffn_gate_b, L3_ffn_w1, L3_ffn_b1, L3_ffn_w2, L3_ffn_b2):
    import jax
    import jax.numpy as jnp

    def _L0_tok_ref(x, W, gamma):
        import jax, jax.numpy as jnp
        import numpy as np
        PATCH = 8
        EPS = 1e-05

        def _patchify(x):
            B, C, H, Wd = x.shape
            p = PATCH
            x = x.reshape(B, C, H // p, p, Wd // p, p)
            x = x.transpose(0, 2, 4, 1, 3, 5)
            return x.reshape(B, H // p * (Wd // p), C * p * p)
        tokens = _patchify(x)
        h = jnp.einsum('bnf,fd->bnd', tokens, W)
        mu = jnp.mean(h, axis=-1, keepdims=True)
        var = jnp.mean(jnp.square(h - mu), axis=-1, keepdims=True)
        out = (h - mu) * jax.lax.rsqrt(var + EPS) * gamma
        return out

    def _L0_attn_ref(x, WQ, bQ, WK, bK, WV, bV, WO, bO, Wg, bg, alpha_logit, ln_gamma, ln_beta):
        import jax, jax.numpy as jnp
        import numpy as np
        D_MODEL = 256
        D_HEAD = 64
        N_HEADS = 16
        STATE = 64
        D_INNER = D_HEAD * N_HEADS
        B, T = (4, 512)
        LN_EPS = 1e-05

        def _linear_params(key, fan_out, fan_in):
            k1, k2 = jax.random.split(key)
            s = 1.0 / np.sqrt(fan_in)
            W = jax.random.uniform(k1, (fan_out, fan_in), jnp.float32, -s, s)
            b = jax.random.uniform(k2, (fan_out,), jnp.float32, -s, s)
            return (W, b)

        def _layer_norm(x, gamma, beta):
            mu = jnp.mean(x, axis=-1, keepdims=True)
            var = jnp.mean(jnp.square(x - mu), axis=-1, keepdims=True)
            return (x - mu) * jax.lax.rsqrt(var + LN_EPS) * gamma + beta
        batch, seq_len, _ = x.shape
        residual = x
        xn = _layer_norm(x, ln_gamma, ln_beta)
        Q = (xn @ WQ.T + bQ).reshape(batch, seq_len, N_HEADS, D_HEAD)
        K = (xn @ WK.T + bK).reshape(batch, seq_len, N_HEADS, D_HEAD)
        V = (xn @ WV.T + bV).reshape(batch, seq_len, N_HEADS, D_HEAD)
        gate = jax.nn.silu(xn @ Wg.T + bg).reshape(batch, seq_len, N_HEADS, D_HEAD)
        alpha = jax.nn.sigmoid(alpha_logit)
        Qs = Q[..., :STATE]
        Ks = K[..., :STATE]

        def step(h, qkv):
            q, k, v = qkv
            h = alpha[None, :, :, None] * h + k[:, :, :, None] * v[:, :, None, :]
            o = jnp.einsum('bhi,bhij->bhj', q, h)
            return (h, o)
        h0 = jnp.zeros((batch, N_HEADS, STATE, D_HEAD), x.dtype)
        qkv_t = (jnp.moveaxis(Qs, 1, 0), jnp.moveaxis(Ks, 1, 0), jnp.moveaxis(V, 1, 0))
        _, o = jax.lax.scan(step, h0, qkv_t)
        o = jnp.moveaxis(o, 0, 1)
        o = o * gate
        y = o.reshape(batch, seq_len, D_INNER) @ WO.T + bO
        return residual + y

    def _L0_ffn_ref(hidden_states, w1_shared, w2_shared, w1_routed, w2_routed, w_router):
        import jax, jax.numpy as jnp
        import numpy as np
        H = 256
        I = 4 * H
        E = 8
        TOP_K = 2
        bsz, seq_len, hidden_dim = hidden_states.shape
        flat = hidden_states.reshape(-1, hidden_dim)
        shared_out = jax.nn.silu(flat @ w1_shared) @ w2_shared
        router_logits = flat @ w_router
        routing_weights = jax.nn.softmax(router_logits, axis=-1)
        topk_w, topk_idx = jax.lax.top_k(routing_weights, TOP_K)
        topk_w = topk_w / jnp.sum(topk_w, axis=-1, keepdims=True)
        one_hot = jax.nn.one_hot(topk_idx, E, dtype=topk_w.dtype)
        cw = jnp.einsum('tk,tke->te', topk_w, one_hot)
        routed_out = jnp.zeros_like(flat)
        for e in range(E):
            expert_out = jax.nn.silu(flat @ w1_routed[e]) @ w2_routed[e]
            routed_out = routed_out + cw[:, e:e + 1] * expert_out
        total = shared_out + routed_out
        return total.reshape(bsz, seq_len, hidden_dim)

    def _L1_attn_ref(x, W_qkv, b_qkv, W_o, b_o):
        import jax, jax.numpy as jnp
        import numpy as np
        D_MODEL = 256
        N_HEADS = 16
        D_HEAD = 64
        B, S = (8, 256)
        EPS = 1.1920929e-07
        normed = x * jax.lax.rsqrt(jnp.mean(x * x, axis=-1, keepdims=True) + EPS)
        qkv = normed @ W_qkv.T + b_qkv
        qkv = qkv.reshape(*qkv.shape[:-1], N_HEADS, D_HEAD, 3)
        q, k, v = (qkv[..., 0], qkv[..., 1], qkv[..., 2])
        scores = jnp.einsum('bqhd,bkhd->bhqk', q, k)
        seq = x.shape[-2]
        causal_mask = jnp.triu(jnp.ones((seq, seq), dtype=bool), k=1)
        scores = jnp.where(causal_mask, -jnp.inf, scores)
        attn = jax.nn.softmax(scores, axis=-2)
        z = jnp.einsum('bhqk,bkhd->bqhd', attn, v)
        z = z.reshape(*z.shape[:-2], N_HEADS * D_HEAD)
        return z @ W_o.T + b_o

    def _L1_ffn_ref(x, Wg, W1, b1, W2, b2, W3, b3):
        import jax, jax.numpy as jnp
        import numpy as np
        TOPK = 4
        N_GROUPS = 4
        TOPK_GROUPS = 2
        ROUTE_SCALE = 2.5

        def _gate(x2, Wg):
            T = x2.shape[0]
            E = Wg.shape[0]
            scores = x2 @ Wg.T
            s = jax.nn.sigmoid(scores)
            g = s.reshape(T, N_GROUPS, E // N_GROUPS)
            group_scores = g.max(axis=-1)
            _, gidx = jax.lax.top_k(group_scores, TOPK_GROUPS)
            group_mask = jnp.any(jax.nn.one_hot(gidx, N_GROUPS, dtype=jnp.bool_), axis=1)
            masked = jnp.where(group_mask[:, :, None], g, -jnp.inf).reshape(T, E)
            _, idx = jax.lax.top_k(masked, TOPK)
            w = jnp.take_along_axis(s, idx, axis=1)
            w = w / jnp.sum(w, axis=-1, keepdims=True)
            w = w * ROUTE_SCALE
            return (w.astype(x2.dtype), idx)
        shape = x.shape
        D = shape[-1]
        x2 = x.reshape(-1, D)
        weights, indices = _gate(x2, Wg)
        E = Wg.shape[0]
        y = jnp.zeros_like(x2)
        for e in range(E):
            we = jnp.sum(weights * (indices == e), axis=-1)
            h = jax.nn.silu(x2 @ W1[e].T + b1[e]) * (x2 @ W3[e].T + b3[e])
            y = y + (h @ W2[e].T + b2[e]) * we[:, None]
        return y.reshape(shape)

    def _L2_attn_ref(x, Wq, Wk, Wv):
        import jax, jax.numpy as jnp
        import numpy as np
        DIM = 256
        HEADS = 16
        HEAD_DIM = DIM // HEADS

        def _xavier(key, shape):
            fan_out, fan_in = shape
            limit = float(np.sqrt(6.0 / (fan_in + fan_out)))
            return jax.random.uniform(key, shape, jnp.float32, -limit, limit)
        B, S, D = x.shape
        H, Hd = (HEADS, HEAD_DIM)
        q = (x @ Wq.T).reshape(B, S, H, Hd)
        k = (x @ Wk.T).reshape(B, S, H, Hd)
        v = (x @ Wv.T).reshape(B, S, H, Hd)
        energy = jnp.einsum('bqhd,bkhd->bhqk', q, k)
        attn = jax.nn.softmax(energy / jnp.sqrt(jnp.float32(D)), axis=-1)
        out = jnp.einsum('bhqk,bkhd->bqhd', attn, v).reshape(B, S, D)
        return out

    def _L2_ffn_ref(hidden_states, classifier_weight, e_score_correction_bias, gate_up_proj, down_proj):
        import jax, jax.numpy as jnp
        import numpy as np
        B, S, H = (2, 512, 256)
        I = 128
        E_R, E_Z = (32, 8)
        E_T = E_R + E_Z
        K = 6
        SCALE = 2.5
        W_INIT = 0.02
        orig_shape = hidden_states.shape
        x = hidden_states.reshape(-1, H).astype(jnp.float32)
        T = x.shape[0]
        logits = x @ classifier_weight.T
        scores = jax.nn.softmax(logits, axis=-1)
        _, topk_idx = jax.lax.top_k(scores + e_score_correction_bias[None, :], K)
        topk_w = jnp.take_along_axis(scores, topk_idx, axis=1) * SCALE
        w_full = jnp.zeros((T, E_T), jnp.float32).at[jnp.arange(T)[:, None], topk_idx].add(topk_w)
        zero_w = w_full[:, E_R:].sum(axis=-1, keepdims=True)
        out0 = x * zero_w
        routed_w = w_full[:, :E_R].T

        def body(out, xs):
            Wgu, Wd, we = xs
            gate, up = jnp.split(x @ Wgu.T, 2, axis=-1)
            y = jax.nn.silu(gate) * up @ Wd.T
            return (out + we[:, None] * y, None)
        out, _ = jax.lax.scan(body, out0, (gate_up_proj[:E_R], down_proj, routed_w))
        return out.reshape(orig_shape).astype(hidden_states.dtype)

    def _L3_attn_ref(x, W_in, W_delta, b_delta, W_B, W_C, A_log, D_param, W_out):
        import jax, jax.numpy as jnp
        import numpy as np
        d_inner = W_delta.shape[0]
        x_and_res = x @ W_in
        u, res = (x_and_res[..., :d_inner], x_and_res[..., d_inner:])
        u = jax.nn.silu(u)
        delta = jax.nn.softplus(u @ W_delta + b_delta)
        Bm = u @ W_B
        Cm = u @ W_C
        A = -jnp.exp(A_log)

        def step(h, inp):
            d_t, B_t, C_t, u_t = inp
            dA = jnp.exp(d_t[..., None] * A)
            h = dA * h + d_t[..., None] * B_t[:, None, :] * u_t[..., None]
            y_t = jnp.einsum('bdn,bn->bd', h, C_t)
            return (h, y_t)
        Bsz = x.shape[0]
        h0 = jnp.zeros((Bsz, d_inner, A.shape[1]), dtype=x.dtype)
        xs = (jnp.swapaxes(delta, 0, 1), jnp.swapaxes(Bm, 0, 1), jnp.swapaxes(Cm, 0, 1), jnp.swapaxes(u, 0, 1))
        _, ys = jax.lax.scan(step, h0, xs)
        y = jnp.swapaxes(ys, 0, 1) + u * D_param
        y = y * jax.nn.silu(res)
        return y @ W_out

    def _L3_ffn_ref(x, gate_w, gate_b, w1, b1, w2, b2):
        import jax, jax.numpy as jnp
        import numpy as np
        B, S, D, H, E = (4, 512, 256, 1024, 8)
        b, s, d = x.shape
        xf = x.reshape(-1, d)
        logits = xf @ gate_w.T + gate_b
        top1 = jnp.argmax(logits, axis=-1)
        out = jnp.zeros_like(xf)
        n_experts = w1.shape[0]
        for e in range(n_experts):
            h = jax.nn.relu(xf @ w1[e].T + b1[e])
            y = h @ w2[e].T + b2[e]
            out = out + jnp.where((top1 == e)[:, None], y, jnp.zeros((), y.dtype))
        return out.reshape(b, s, d)
    h = _L0_tok_ref(x, L0_tok_W, L0_tok_gamma)
    h = jnp.concatenate([jnp.broadcast_to(cls_tok, (h.shape[0], 1, h.shape[2])), h], axis=1)
    h = h + _L0_attn_ref(_layernorm(h, axis=-1), L0_attn_WQ, L0_attn_bQ, L0_attn_WK, L0_attn_bK, L0_attn_WV, L0_attn_bV, L0_attn_WO, L0_attn_bO, L0_attn_Wg, L0_attn_bg, L0_attn_alpha_logit, L0_attn_ln_gamma, L0_attn_ln_beta)
    h = h + _L0_ffn_ref(_layernorm(h, axis=-1), L0_ffn_w1_shared, L0_ffn_w2_shared, L0_ffn_w1_routed, L0_ffn_w2_routed, L0_ffn_w_router)
    h = h + _L1_attn_ref(_layernorm(h, axis=-1), L1_attn_W_qkv, L1_attn_b_qkv, L1_attn_W_o, L1_attn_b_o)
    h = h + _L1_ffn_ref(_layernorm(h, axis=-1), L1_ffn_Wg, L1_ffn_W1, L1_ffn_b1, L1_ffn_W2, L1_ffn_b2, L1_ffn_W3, L1_ffn_b3)
    h = h + _L2_attn_ref(_layernorm(h, axis=-1), L2_attn_Wq, L2_attn_Wk, L2_attn_Wv)
    h = h + _L2_ffn_ref(_layernorm(h, axis=-1), L2_ffn_classifier_weight, L2_ffn_e_score_correction_bias, L2_ffn_gate_up_proj, L2_ffn_down_proj)
    h = h + _L3_attn_ref(_layernorm(h, axis=-1), L3_attn_W_in, L3_attn_W_delta, L3_attn_b_delta, L3_attn_W_B, L3_attn_W_C, L3_attn_A_log, L3_attn_D_param, L3_attn_W_out)
    h = h + _L3_ffn_ref(_layernorm(h, axis=-1), L3_ffn_gate_w, L3_ffn_gate_b, L3_ffn_w1, L3_ffn_b1, L3_ffn_w2, L3_ffn_b2)
    return h

_drawn_inputs = setup_inputs


def setup_inputs(seed=0):
    import zlib

    import numpy as np

    out = dict(_drawn_inputs(seed))
    spreads = {'L0_tok_gamma': (1.0, 0.2),
     'L0_attn_ln_gamma': (1.0, 0.2),
     'L0_attn_ln_beta': (0.0, 0.1),
     'L1_attn_b_qkv': (0.0, 0.1),
     'L1_attn_b_o': (0.0, 0.1),
     'L1_ffn_b1': (0.0, 0.8),
     'L1_ffn_b2': (0.0, 0.1),
     'L1_ffn_b3': (0.0, 0.8),
     'L2_ffn_e_score_correction_bias': (0.0, 0.1),
     'L3_attn_D_param': (1.0, 0.6)}
    factors = {'L0_attn_bQ': 3.491,
     'L0_attn_bK': 3.047,
     'L0_attn_bV': 3.141,
     'L0_attn_bO': 3.101,
     'L0_attn_bg': 3.282,
     'L0_attn_alpha_logit': 4.502,
     'L1_ffn_W1': 4.038,
     'L1_ffn_W2': 3.63,
     'L1_ffn_W3': 3.712,
     'L2_ffn_classifier_weight': 4.148,
     'L2_ffn_gate_up_proj': 8.0,
     'L2_ffn_down_proj': 8.0,
     'L3_attn_W_in': 5.713,
     'L3_attn_W_delta': 8.0,
     'L3_attn_b_delta': 8.0,
     'L3_attn_W_B': 8.0,
     'L3_attn_W_C': 8.0,
     'L3_attn_A_log': 8.0,
     'L3_attn_W_out': 6.446,
     'L3_ffn_b1': 200.0,
     'L3_ffn_b2': 200.0,
     'L3_ffn_gate_w': 24.926,
     'L3_ffn_gate_b': 64.0,
     'L3_ffn_w1': 31.079,
     'L3_ffn_w2': 23.635}
    for name, (base, spread) in spreads.items():
        noise = np.random.default_rng([zlib.crc32(name.encode()), seed]).standard_normal(out[name].shape)
        drawn = base * np.exp(spread * noise) if base else spread * noise
        out[name] = jnp.asarray(drawn.astype(out[name].dtype))
    for name, factor in factors.items():
        out[name] = (out[name] * factor).astype(out[name].dtype)
    return out
```

```python
from contextlib import ExitStack

import numpy as np
import concourse.bass as bass
from concourse import mybir

P = 128
D = 256
C = D // P
B = 4
N = 257
T = B * N
PF = 320
EPS = 1e-5
RMS_EPS = 1.1920929e-07
BANK = 512
CHUNKS = [(0, 344), (344, 342), (686, 342)]
CW = 344
NC = len(CHUNKS)
TILES = [128 * j for j in range(8)] + [T - 128]
NT = len(TILES)
SC0, SC1 = N, N - P
SCW = SC0 + SC1
EMIN, EMAX = -8, 128
NEXP = EMAX - EMIN + 1
BIG = 1e30


class Ffn:
    def __init__(self, name, units, mt, gated, act, has_bias):
        self.name, self.units, self.mt, self.gated, self.act, self.has_bias = name, units, mt, gated, act, has_bias
        self.up_mats = 2 if gated else 1
        self.up_w = self.up_mats * C * mt * P
        self.up_words = self.up_w + (self.up_mats * mt if has_bias else 0)
        self.dn_w = mt * D
        self.dn_words = self.dn_w + (C if has_bias else 0)
        self.psums = self.up_mats
        self.depth = 4 // self.psums


FFNS = [Ffn("f0", 9, 8, False, "Silu", False), Ffn("f1", 16, 2, True, "Silu", True),
        Ffn("f2", 32, 1, True, "Silu", False), Ffn("f3", 8, 8, False, "Relu", True)]

CONSTS = {}
_at = 0
for _n, _w in (("ident", P), ("mean", P), ("headones", P), ("expo", NEXP), ("expo_r", NEXP), ("causal", SCW), ("hide", SCW),
               ("unpad", 2 * 64), ("block4", 4)):
    CONSTS[_n] = (_at, _at + _w)
    _at += _w
CONST_W = _at


VECS = {}
_at = 0
for _n, _w in (("cls", C), ("tok_gamma", C), ("ln_gamma", C), ("ln_beta", C), ("bO0", C), ("bO1", C), ("alpha", 8),
               ("b_delta", 4), ("A_log", 64), ("D_param", 4), ("gate_b", 8), ("score_b", 40)):
    VECS[_n] = (_at, _at + _w)
    _at += _w
VEC_W = _at
HP = 8
A0_W = 4 * C * P + D + 4
A1_W = 3 * C * P + D + 3
A2_W = 3 * C * P
ARENA_W = 29700


def build(nc, dram, out):
    f32 = mybir.dt.float32
    u32 = mybir.dt.uint32
    ALU = mybir.AluOpType
    ACT = mybir.ActivationFunctionType
    AX = mybir.AxisListType
    ctx = ExitStack()
    with ctx:
        def sb(name, shape):
            return ctx.enter_context(nc.sbuf_tensor(name, shape, f32))

        sems = {}

        def sem(name):
            if name not in sems:
                sems[name] = ctx.enter_context(nc.semaphore(name))
            return sems[name]

        HT = sb("HT", [P, C, T])
        XN = sb("XN", [P, C, T])
        XN2 = sb("XN2", [P, C, T])
        XC = sb("XC", [P, C, T])
        SQ = sb("SQ", [P, C, T])
        consts = sb("consts", [P, CONST_W])
        vecs = sb("vecs", [P, VEC_W])
        wup = [sb(f"wup{s}", [P, max(f.up_words for f in FFNS)]) for s in range(2)]
        wdn = [sb(f"wdn{s}", [P, max(f.dn_words for f in FFNS)]) for s in range(2)]
        watt = [sb(f"watt{s}", [P, A0_W]) for s in range(2)]
        arena = sb("arena", [P, ARENA_W])
        ps = ctx.enter_context(nc.psum_tensor("ps", [P, 8, BANK], f32))

        class Arena:
            def __init__(self):
                self.at = 0

            def take(self, *shape, rows=P):
                w = int(np.prod(shape))
                v = arena[0:rows, self.at:self.at + w]
                self.at += w
                assert self.at <= ARENA_W, self.at
                if len(shape) == 2:
                    v = v.rearrange("p (a b) -> p a b", b=shape[1])
                elif len(shape) == 3:
                    v = v.rearrange("p (a b c) -> p a b c", b=shape[1], c=shape[2])
                return v

        def const(name):
            a, b = CONSTS[name]
            return consts[:, a:b]

        def vec(name):
            a, b = VECS[name]
            return vecs[:, a:b]

        ident, mean_mat = const("ident"), const("mean")

        def spread(col, w):
            return col.unsqueeze(2).broadcast_to([col.shape[0], col.shape[1], w])

        def over(row, n):
            return row.unsqueeze(1).broadcast_to([row.shape[0], n, row.shape[1]])

        class Norm:
            count = 0

            def __init__(self, src, dst, ready, centred=True, eps=EPS, gamma=None, beta=None):
                self.src, self.dst, self.ready = src, dst, ready
                self.centred, self.eps, self.gamma, self.beta = centred, eps, gamma, beta
                self.base = NC * Norm.count
                self.cbase = NC * Norm.centred_before if centred else None
                Norm.count += 1
                Norm.centred_before += centred
                self.gbase = 2 * NC * Norm.gamma_before
                Norm.gamma_before += gamma is not None

            centred_before = 0
            gamma_before = 0

            def done(self, c=NC - 1):
                return sem("ln_out"), self.base + c + 1

            def pe(self, pe):
                if self.centred:
                    for c, (t0, w) in enumerate(CHUNKS):
                        for s, v in self.ready(c):
                            pe.wait_ge(s, v)
                        for k in range(C):
                            mm = pe.matmul(ps[:, c, 0:w], mean_mat, self.src[:, k, t0:t0 + w], start=(k == 0), stop=(k == C - 1))
                        mm.then_inc(sem("ln_mean"), 1)
                for c, (t0, w) in enumerate(CHUNKS):
                    pe.wait_ge(sem("ln_sq"), self.base + c + 1)
                    for k in range(C):
                        mm = pe.matmul(ps[:, NC + c, 0:w], mean_mat, SQ[:, k, t0:t0 + w], start=(k == 0), stop=(k == C - 1))
                    mm.then_inc(sem("ln_var"), 1)

            def act(self, act):
                for c, (t0, w) in enumerate(CHUNKS):
                    if self.centred:
                        act.wait_ge(sem("ln_cent"), self.cbase + c + 1)
                        x = XC
                    else:
                        for s, v in self.ready(c):
                            act.wait_ge(s, v)
                        x = self.src
                    act.activation(SQ[:, :, t0:t0 + w], x[:, :, t0:t0 + w], ACT.Square).then_inc(sem("ln_sq"), 1)
                for c, (t0, w) in enumerate(CHUNKS):
                    act.wait_ge(sem("ln_var"), self.base + c + 1)
                    act.wait_ge(sem("ln_eps"), 2)
                    eps = epsc[:, 0:1] if self.eps == EPS else epsc[:, 1:2]
                    act.activation(SQ[:, 0, t0:t0 + w], ps[:, NC + c, 0:w], ACT.Sqrt, bias=eps).then_inc(sem("ln_std"), 1)

            def dve(self, dve):
                if self.centred:
                    for c, (t0, w) in enumerate(CHUNKS):
                        dve.wait_ge(sem("ln_mean"), self.cbase + c + 1)
                        dve.tensor_tensor(XC[:, :, t0:t0 + w], self.src[:, :, t0:t0 + w], over(ps[:, c, 0:w], C),
                                          ALU.subtract).then_inc(sem("ln_cent"), 1)
                x = XC if self.centred else self.src
                for c, (t0, w) in enumerate(CHUNKS):
                    n = self.base + c + 1
                    dve.wait_ge(sem("ln_std"), n)
                    dve.reciprocal(SQ[:, 1, t0:t0 + w], SQ[:, 0, t0:t0 + w]).then_inc(sem("ln_rstd"), 1)
                    dve.wait_ge(sem("ln_rstd"), n)
                    last = dve.tensor_tensor(self.dst[:, :, t0:t0 + w], x[:, :, t0:t0 + w], over(SQ[:, 1, t0:t0 + w], C), ALU.mult)
                    if self.gamma is not None:
                        for k in range(C):
                            last.then_inc(sem("ln_scaled"), 1)
                            dve.wait_ge(sem("ln_scaled"), self.gbase + C * c + k + 1)
                            v = self.dst[:, k, t0:t0 + w]
                            if self.beta is None:
                                last = dve.tensor_scalar(v, v, self.gamma[:, k:k + 1], None, ALU.mult)
                            else:
                                last = dve.tensor_scalar(v, v, self.gamma[:, k:k + 1], self.beta[:, k:k + 1], ALU.mult, ALU.add)
                    last.then_inc(sem("ln_out"), 1)

        epsc = sb("epsc", [P, 2])

        ar = Arena()
        xt = ar.take(3, B * D)
        wtok = ar.take(3, D)

        def tok_sp(sp):
            sp.dma_start(xt, dram["xt"]).then_inc(sem("tok_in"), 16)
            sp.dma_start(wtok, dram["wtok"]).then_inc(sem("tok_in"), 16)
            sp.dma_start(consts[:, :], dram["consts"]).then_inc(sem("const_in"), 16)
            sp.dma_start(vecs[:, :], dram["vecs"]).then_inc(sem("const_in"), 16)

        def tok_pe(pe):
            pe.wait_ge(sem("tok_in"), 32)
            for b in range(B):
                for d in range(C):
                    for k in range(3):
                        r = min(P, PF - k * P)
                        mm = pe.matmul(ps[:, 2 * b + d, 0:D], wtok[0:r, k, d * P:(d + 1) * P], xt[0:r, k, b * D:(b + 1) * D],
                                       start=(k == 0), stop=(k == 2))
                mm.then_inc(sem("tok_ps"), 1)
            pe.wait_ge(sem("const_in"), 32)

        def cls_columns(dve):
            return dve.tensor_copy(HT[:, :, :].rearrange("p c (b n) -> p c b n", n=N)[:, :, :, 0], spread(vec("cls"), B))

        def tok_dve(dve):
            dve.memset(epsc[:, 0:1], EPS).then_inc(sem("ln_eps"), 1)
            dve.memset(epsc[:, 1:2], RMS_EPS).then_inc(sem("ln_eps"), 1)
            dve.wait_ge(sem("const_in"), 32)
            cls_columns(dve).then_inc(sem("tok_h"), 1)
            for b in range(B):
                dve.wait_ge(sem("tok_ps"), b + 1)
                dve.tensor_copy(HT[:, :, b * N + 1:(b + 1) * N], ps[:, 2 * b:2 * b + 2, 0:D]).then_inc(sem("tok_h"), 1)

        tok_norm = Norm(HT, HT, lambda c: [(sem("tok_h"), B + 1)], gamma=vec("tok_gamma"))

        def tok_cls(dve):
            dve.wait_ge(*tok_norm.done())
            cls_columns(dve).then_inc(sem("h0"), 1)

        n0a = Norm(HT, XN, lambda c: [(sem("h0"), 1)])
        n0b = Norm(XN, XN2, lambda c: [n0a.done(c)], gamma=vec("ln_gamma"), beta=vec("ln_beta"))
        ar = Arena()
        w0 = [w[:, 0:A0_W] for w in watt]
        powt = ar.take(HP, NEXP)
        powr = ar.take(HP, NEXP)
        tab = ar.take(2, NEXP)
        lga = ar.take(4, HP)
        q0, k0, v0, g0 = ([ar.take(N) for _ in range(2)] for _ in range(4))
        q16, kA, kB = ar.take(16, 16), ar.take(8, 16), ar.take(8, 32)
        q32, k32 = ar.take(4, 32), ar.take(4, 32)
        q64, k64 = ar.take(2, 64), ar.take(2, 64)
        q128, k128 = ar.take(P + 1), ar.take(2, P)
        at0 = [ar.take(SCW) for _ in range(2)]
        vt0 = ar.take(2, P)
        og0 = ar.take(N)
        lastp, lastv = ar.take(1), ar.take(1)
        U = 2 * B
        E0 = -EMIN

        def R(e):
            return EMAX - e

        def a0_load(sp, m, s):
            return sp.dma_start(w0[s], m).then_inc(sem(f"a0_w{s}"), 16)

        def a0_sp(sp):
            for s in range(2):
                a0_load(sp, dram["w_a0"][s], s)
            with sp.Fori(1, HP // 2) as mm:
                for s in range(2):
                    sp.wait_ge(sem("a0_y"), mm * U + (s - 1) * B)
                    a0_load(sp, dram["w_a0"][bass.ds(2 * mm + s, 1), :, :].rearrange("a p w -> p (a w)"), s)

        def a0_pe(pe):
            n0a.pe(pe)
            n0b.pe(pe)
            pe.wait_ge(*n0b.done())
            with pe.Fori(0, HP // 2) as mm:
                base = mm * U

                def project(j):
                    s, b = j // B, j % B
                    if b == 0:
                        pe.wait_ge(sem(f"a0_w{s}"), 16 * mm + 16)
                    for i in range(4):
                        for k in range(C):
                            mmul = pe.matmul(ps[:, i, 0:N], w0[s][:, (i * C + k) * P:(i * C + k + 1) * P],
                                             XN2[:, k, b * N:(b + 1) * N], start=(k == 0), stop=(k == C - 1))
                        if i % 2:
                            mmul.then_inc(sem("a0_proj"), 1)

                def values(j):
                    pe.wait_ge(sem("a0_vg"), base + j + 1)
                    for i in range(2):
                        pe.transpose(ps[:, 7, i * P:(i + 1) * P], v0[j % 2][:, i * P:(i + 1) * P], ident)
                    pe.wait_ge(sem("a0_qk256"), base + j + 1)
                    pe.matmul(ps[:, 7, 2 * P:2 * P + 1], const("headones"), lastp, start=True, stop=True).then_inc(sem("a0_vt"), 1)

                def scores(j):
                    pe.wait_ge(sem("a0_prep"), base + j + 1)
                    pe.wait_ge(sem("a0_prepg"), base + j + 1)
                    pe.wait_ge(sem("a0_added"), base + j + 1)
                    pe.nop(nofuse=True)
                    for h in range(2):
                        rows = slice(64 * h, 64 * h + 64)

                        def block(r0, r1, c0, lhs, rhs):
                            return pe.matmul(ps[r0:r1, 4 + h, c0:c0 + rhs.shape[1]], lhs, rhs, start=True, stop=True)

                        for i in range(2):
                            cb = i * SC0
                            for n in range(4):
                                g = 4 * i + n
                                block(32 * n, 32 * n + 16, cb + 32 * n, kA[rows, g, :], q16[rows, 2 * g, :])
                                block(32 * n, 32 * n + 32, cb + 32 * n + 16, kB[rows, g, :], q16[rows, 2 * g + 1, :])
                            for n in range(2):
                                g = 2 * i + n
                                block(64 * n, 64 * n + 32, cb + 64 * n + 32, k32[rows, g, :], q32[rows, g, :])
                            block(0, 64, cb + 64, k64[rows, i, :], q64[rows, i, :])
                        block(0, P, P, k128[rows, 0, :], q128[rows, :])
                        block(0, P, SC0 + P, k128[rows, 1, :], q0[j % 2][rows, 2 * P:N]).then_inc(sem("a0_s"), 1)

                def mix(j):
                    pe.wait_ge(sem("a0_vsb"), base + j + 1)
                    for h in range(2):
                        pe.wait_ge(sem("a0_at"), 2 * base + 2 * j + h + 1)
                        o = ps[64 * h:64 * h + 64, 6, :]
                        pe.matmul(o[:, 0:N], vt0[:, 0, 64 * h:64 * h + 64], at0[h][:, 0:SC0], start=True, stop=False)
                        mmul = pe.matmul(o[:, P:N], vt0[:, 1, 64 * h:64 * h + 64], at0[h][:, SC0:SCW], start=False, stop=True)
                    mmul.then_inc(sem("a0_o"), 1)

                def output(j):
                    pe.wait_ge(sem("a0_og"), base + j + 1)
                    for d in range(C):
                        mmul = pe.matmul(ps[:, 4 + d, 0:N], w0[j // B][:, 1024 + d * P:1024 + (d + 1) * P], og0, start=True, stop=True)
                    mmul.then_inc(sem("a0_y"), 1)

                project(0)
                values(0)
                for j in range(U):
                    scores(j)
                    if j + 1 < U:
                        project(j + 1)
                    mix(j)
                    if j + 1 < U:
                        values(j + 1)
                    output(j)

        def a0_act(act):
            n0a.act(act)
            n0b.act(act)
            act.wait_ge(sem("a0_lg"), 2)
            act.activation(lga[:, 1, :], lga[:, 0, :], ACT.Exp).then_inc(sem("a0_lga"), 1)
            act.wait_ge(sem("a0_lga"), 1)
            act.activation(lga[:, 2, :], lga[:, 1, :], ACT.Ln, bias=1.0).then_inc(sem("a0_lga"), 1)
            act.wait_ge(sem("a0_lg"), 4)
            for m in range(HP):
                act.activation(powt[:, m, :], const("expo")[:, 0:NEXP], ACT.Exp, scale=lga[:, 3, m:m + 1])
                last = act.activation(powr[:, m, :], const("expo_r"), ACT.Exp, scale=lga[:, 3, m:m + 1])
                last.then_inc(sem("a0_pow"), 1)
            with act.Fori(0, HP // 2) as mm:
                base = mm * U
                for j in range(U):
                    w = w0[j // B]
                    act.wait_ge(sem("a0_proj"), 2 * base + 2 * j + 1)
                    act.activation(q0[j % 2], ps[:, 0, 0:N], ACT.Identity, bias=w[:, 1280:1281])
                    act.activation(k0[j % 2], ps[:, 1, 0:N], ACT.Identity, bias=w[:, 1281:1282]).then_inc(sem("a0_qk"), 1)
                    act.wait_ge(sem("a0_proj"), 2 * base + 2 * j + 2)
                    act.activation(v0[j % 2], ps[:, 2, 0:N], ACT.Identity, bias=w[:, 1282:1283])
                    act.activation(g0[j % 2], ps[:, 3, 0:N], ACT.Silu, bias=w[:, 1283:1284]).then_inc(sem("a0_vg"), 1)

        def a0_dve(dve):
            n0a.dve(dve)
            n0b.dve(dve)
            for i, op in enumerate((ALU.mult, ALU.min)):
                if i == 0:
                    dve.tensor_scalar(lga[:, 0, :], vec("alpha"), -1.0, None, op).then_inc(sem("a0_lg"), 1)
                else:
                    dve.wait_ge(sem("a0_lg"), 1)
                    dve.tensor_tensor(lga[:, 0, :], lga[:, 0, :], vec("alpha"), op).then_inc(sem("a0_lg"), 1)
            dve.tensor_scalar(lga[:, 3, :], vec("alpha"), 0.0, None, ALU.min).then_inc(sem("a0_lg"), 1)
            dve.wait_ge(sem("a0_lga"), 2)
            dve.wait_ge(sem("a0_lg"), 3)
            dve.tensor_tensor(lga[:, 3, :], lga[:, 3, :], lga[:, 2, :], ALU.subtract).then_inc(sem("a0_lg"), 1)
            dve.wait_ge(*n0b.done())
            for c in range(C):
                dve.scalar_tensor_tensor(HT[:, c, :], XN[:, c, :], vec("bO0")[:, c:c + 1], HT[:, c, :], ALU.add, ALU.add).then_inc(sem("a0_res"), 1)
            for h in range(2):
                dve.memset(at0[h], 0.0).then_inc(sem("a0_zero"), 1)
            dve.memset(ps[:, 4:6, 0:SCW], 0.0).then_inc(sem("a0_added"), 1)
            dve.wait_ge(sem("a0_zero"), 2)
            dve.wait_ge(sem("a0_res"), C)
            dve.wait_ge(sem("a0_pow"), HP)
            with dve.Fori(0, HP // 2) as mm:
                base = mm * U

                def prep(j):
                    s, b = j // B, j % B
                    up, down = tab[:, 0, :], tab[:, 1, :]
                    if b == 0:
                        m = 2 * mm + s
                        dve.tensor_copy(up, powt[:, bass.ds(m, 1), :].rearrange("p a e -> p (a e)")).then_inc(sem("a0_tab"), 1)
                        dve.tensor_copy(down, powr[:, bass.ds(m, 1), :].rearrange("p a e -> p (a e)")).then_inc(sem("a0_tab"), 1)
                        dve.wait_ge(sem("a0_tab"), 4 * mm + 2 * s + 2)
                    q, k = q0[j % 2], k0[j % 2]
                    dve.wait_ge(sem("a0_qk"), base + j + 1)
                    dve.tensor_tensor(lastp, q[:, N - 1:N], k[:, N - 1:N], ALU.mult).then_inc(sem("a0_qk256"), 1)

                    def view(x, n):
                        return x[:, 0:2 * P].rearrange("p (a b) -> p a b", b=n)

                    dve.tensor_tensor(q16, view(q, 16), over(up[:, E0 - 8:E0 + 8], 16), ALU.mult)
                    dve.tensor_tensor(kA, view(k, 32)[:, :, 0:16], over(down[:, R(8):R(8) + 16], 8), ALU.mult)
                    dve.tensor_tensor(kB, view(k, 32), over(down[:, R(24):R(24) + 32], 8), ALU.mult)
                    dve.tensor_tensor(q32, view(q, 64)[:, :, 32:64], over(up[:, E0:E0 + 32], 4), ALU.mult)
                    dve.tensor_tensor(k32, view(k, 64)[:, :, 0:32], over(down[:, R(32):R(32) + 32], 4), ALU.mult).then_inc(sem("a0_prep"), 1)

                def tokens(j):
                    dve.wait_ge(sem("a0_vt"), base + j + 1)
                    dve.tensor_copy(vt0, ps[:, 7, 0:2 * P].rearrange("p (a b) -> p a b", b=P))
                    dve.tensor_tensor(lastv, ps[:, 7, 2 * P:2 * P + 1], v0[j % 2][:, N - 1:N], ALU.mult).then_inc(sem("a0_vsb"), 1)

                def mask(j):
                    for h in range(2):
                        dve.wait_ge(sem("a0_s"), 2 * base + 2 * j + h + 1)
                        dve.nop(nofuse=True)
                        dve.copy_predicated(at0[h], const("causal").bitcast(u32), ps[:, 4 + h, 0:SCW]).then_inc(sem("a0_at"), 1)

                def gate(j):
                    dve.wait_ge(sem("a0_o"), base + j + 1)
                    dve.wait_ge(sem("a0_vg"), base + j + 1)
                    dve.wait_ge(sem("a0_vsb"), base + j + 1)
                    g = g0[j % 2]
                    dve.tensor_copy(og0, ps[:, 6, 0:N]).then_inc(sem("a0_oc"), 1)
                    dve.wait_ge(sem("a0_oc"), 2 * base + 2 * j + 1)
                    dve.tensor_tensor(og0[:, N - 1:N], og0[:, N - 1:N], lastv, ALU.add).then_inc(sem("a0_oc"), 1)
                    dve.wait_ge(sem("a0_oc"), 2 * base + 2 * j + 2)
                    dve.tensor_tensor(og0, og0, g, ALU.mult).then_inc(sem("a0_og"), 1)

                def add(j):
                    b = j % B
                    h = HT[:, :, b * N:(b + 1) * N]
                    dve.wait_ge(sem("a0_y"), base + j + 1)
                    dve.tensor_tensor(h, h, ps[:, 4:6, 0:N], ALU.add).then_inc(sem("a0_added"), 1)

                prep(0)
                tokens(0)
                for j in range(U):
                    mask(j)
                    if j + 1 < U:
                        prep(j + 1)
                    gate(j)
                    if j + 1 < U:
                        tokens(j + 1)
                    add(j)

        def a0_pool(pool):
            with pool.Fori(0, HP // 2) as mm:
                base = mm * U
                for j in range(U):
                    if j:
                        pool.wait_ge(sem("a0_s"), 2 * base + 2 * j)
                    pool.wait_ge(sem("a0_tab"), 4 * mm + 2 * (j // B) + 2)
                    pool.wait_ge(sem("a0_qk"), base + j + 1)
                    q, k = q0[j % 2], k0[j % 2]
                    up, down = tab[:, 0, :], tab[:, 1, :]
                    pool.tensor_tensor(q64, q[:, 0:2 * P].rearrange("p (a b) -> p a b", b=P)[:, :, 64:P], over(up[:, E0:E0 + 64], 2), ALU.mult)
                    pool.tensor_tensor(k64, k[:, 0:2 * P].rearrange("p (a b) -> p a b", b=P)[:, :, 0:64], over(down[:, R(64):R(64) + 64], 2), ALU.mult)
                    pool.tensor_tensor(q128, q[:, P:N], up[:, E0:E0 + P + 1], ALU.mult)
                    pool.tensor_tensor(k128, k[:, 0:2 * P].rearrange("p (a b) -> p a b", b=P), over(down[:, R(P):R(P) + P], 2), ALU.mult)\
                        .then_inc(sem("a0_prepg"), 1)

        h_a0 = [(sem("a0_added"), HP * B + 1)]

        FA = Arena()
        FA.at = 3 * D * B + 3 * D
        hid = [FA.take(8, CW) for _ in range(2)]
        sig = FA.take(2, CW)
        cwb = [FA.take(T) for _ in range(2)]
        scaled = [FA.take(C, CW) for _ in range(2)]
        cwt = FA.take(T)
        wr = FA.take(C, 40)
        lg = FA.take(NT, 40)
        prob = FA.take(NT, 40)
        vals = FA.take(NT, 48)
        repl = FA.take(NT, 48)
        cw = FA.take(NT, 40)
        top8 = FA.take(NT, 8)
        red = FA.take(4, NT)
        grp = FA.take(NT, 10)
        grpr = FA.take(NT, 10)

        class Units:
            def __init__(self, f, i, s, c):
                self.f, self.i, self.s, self.c = f, i, s, c
                self.n = 6 * i + 3 * s + c
                self.par = (3 * s + c) % 2

            def next(self):
                if self.c + 1 < NC:
                    return Units(self.f, self.i, self.s, self.c + 1)
                return Units(self.f, self.i + self.s, 1 - self.s, 0)

            def tile(self, m):
                return self.n * self.f.mt + m, ((3 * self.s + self.c) * self.f.mt + m) % self.f.depth

        def sweep(eng, f, hidden, outputs):
            loops = (f.units - 1) // 2
            hidden(Units(f, 0, 0, 0))
            with eng.Fori(0, loops) as i:
                for s in range(2):
                    for c in range(NC):
                        u = Units(f, i, s, c)
                        hidden(u.next())
                        outputs(u)
            rest = f.units - 2 * loops
            for s in range(rest):
                for c in range(NC):
                    u = Units(f, loops, s, c)
                    if s < rest - 1 or c < NC - 1:
                        hidden(u.next())
                    outputs(u)

        class Layer:
            def __init__(self, f, ready, src=None):
                self.f, self.p = f, f.name
                self.norm = Norm(HT, XN, ready)
                self.rows = {"f0": 9, "f1": 16, "f2": 33, "f3": 8}[f.name]
                self.experts = {"f0": 8, "f1": 16, "f2": 40, "f3": 8}[f.name]
                self.cwd = nc.dram_tensor(f"cw_{f.name}", (self.rows, T), f32, kind="Internal").ap()
                self.extra = 1 if f.name == "f2" else 0
                self.index = FFNS.index(f)

            steps = 0

            def sem(self, n):
                return sem(f"{self.p}_{n}")

            def once(self, n, v):
                each = {"wr": 16, "logits": 1, "shifted": 1, "prob": 1, "cw": 1, "cwps": 1, "cwt": 3, "cwd": 16}[n]
                before = self.index
                if n == "shifted":
                    before = self.index // 2
                return sem(f"route_{n}"), each * before + v

            def done(self):
                return [(self.sem("added"), 2 + NC * (self.f.units + self.extra))]

            def load_up(self, sp, src, s):
                sp.dma_start(wup[s][:, 0:self.f.up_words], src).then_inc(self.sem(f"up{s}"), 16)

            def load_dn(self, sp, src, s):
                sp.dma_start(wdn[s][:, 0:self.f.dn_words], src).then_inc(self.sem(f"dn{s}"), 16)

            def load_cw(self, sp, src, s):
                sp.dma_start(cwb[s], src.broadcast_to([P, T])).then_inc(self.sem(f"cw{s}"), 16)

            def sp_first(self, sp, prev):
                if prev is not None:
                    sp.wait_ge(prev.sem("hid"), prev.f.depth + prev.f.mt * NC * prev.f.units)
                    sp.wait_ge(prev.sem("taken"), 2 + NC * prev.f.units)
                for s in range(2):
                    self.load_up(sp, dram["up_" + self.p][s], s)
                    self.load_dn(sp, dram["dn_" + self.p][s], s)

            def sp(self, sp):
                sp.wait_ge(self.norm_gate[0], self.norm_gate[1])
                sp.dma_start(wr[:, :, 0:self.experts], dram["wr_" + self.p]).then_inc(sem("route_wr"), 16)
                sp.wait_ge(*self.once("cwt", 3))
                sp.dma_start(self.cwd, cwt[0:self.rows, :]).then_inc(sem("route_cwd"), 16)
                sp.wait_ge(*self.once("cwd", 16))
                for s in range(2):
                    self.load_cw(sp, self.cwd[s:s + 1, :], s)

                def more(g, i, s):
                    sp.wait_ge(self.sem("hid"), self.f.depth + self.f.mt * (6 * i + 3 * s - 3))
                    self.load_up(sp, dram["up_" + self.p][bass.ds(g, 1), :, :].rearrange("a p w -> p (a w)"), s)
                    sp.wait_ge(self.sem("taken"), 2 + 6 * i + 3 * s - 3)
                    self.load_dn(sp, dram["dn_" + self.p][bass.ds(g, 1), :, :].rearrange("a p w -> p (a w)"), s)
                    self.load_cw(sp, self.cwd[bass.ds(g, 1), :], s)

                pairs = self.f.units // 2
                if pairs > 1:
                    with sp.Fori(1, pairs) as i:
                        for s in range(2):
                            more(2 * i + s, i, s)
                if self.f.units % 2:
                    more(2 * pairs, pairs, 0)
                if self.extra:
                    sp.wait_ge(self.sem("taken"), 2 + NC * (self.f.units - 1))
                    self.load_cw(sp, self.cwd[self.f.units:self.f.units + 1, :], 0)

            def pe(self, pe):
                f = self.f
                self.norm.pe(pe)
                pe.wait_ge(*self.norm.done())
                pe.wait_ge(*self.once("wr", 16))
                for j, t0 in enumerate(TILES):
                    for k in range(C):
                        mm = pe.matmul(ps[:, 0, j * 40:j * 40 + self.experts], XN[:, k, t0:t0 + P], wr[:, k, 0:self.experts],
                                       start=(k == 0), stop=(k == C - 1))
                mm.then_inc(sem("route_logits"), 1)
                pe.wait_ge(*self.once("cw", 1))
                for j in range(NT):
                    mm = pe.transpose(ps[0:self.rows, 1 + j // 4, (j % 4) * P:(j % 4 + 1) * P], cw[:, j, 0:self.rows], ident)
                mm.then_inc(sem("route_cwps"), 1)
                pe.wait_ge(*self.once("cwt", 3))

                def hidden(u):
                    if u.c == 0:
                        pe.wait_ge(self.sem(f"up{u.s}"), 16 * u.i + 16)
                    t0, w = CHUNKS[u.c]
                    for m in range(f.mt):
                        t, slot = u.tile(m)
                        pe.wait_ge(self.sem("hid"), t + 1)
                        for a in range(f.up_mats):
                            for k in range(C):
                                col = ((a * C + k) * f.mt + m) * P
                                mm = pe.matmul(ps[:, slot * f.psums + a, 0:w], wup[u.s][:, col:col + P], XN[:, k, t0:t0 + w],
                                               start=(k == 0), stop=(k == C - 1))
                        mm.then_inc(self.sem("hps"), 1)

                def outputs(u):
                    if u.c == 0:
                        pe.wait_ge(self.sem(f"dn{u.s}"), 16 * u.i + 16)
                    w = CHUNKS[u.c][1]
                    pe.wait_ge(self.sem("taken"), u.n + 1)
                    pe.wait_ge(self.sem("hid"), f.depth + (u.n + 1) * f.mt)
                    for d in range(C):
                        for m in range(f.mt):
                            mm = pe.matmul(ps[:, 4 + 2 * u.par + d, 0:w], wdn[u.s][:, m * D + d * P:m * D + (d + 1) * P],
                                           hid[u.par][:, m, 0:w], start=(m == 0), stop=(m == f.mt - 1))
                    mm.then_inc(self.sem("out"), 1)

                sweep(pe, f, hidden, outputs)

            def act(self, act):
                f = self.f
                self.norm.act(act)
                self.route_act(act)
                if not f.gated:
                    act.sem_inc(self.sem("hid"), f.depth)
                func = ACT.Silu if f.act == "Silu" else ACT.Relu

                def hidden(u):
                    w = CHUNKS[u.c][1]
                    for m in range(f.mt):
                        t, slot = u.tile(m)
                        act.wait_ge(self.sem("hps"), t + 1)
                        bias = wup[u.s][:, f.up_w + m:f.up_w + m + 1] if f.has_bias else 0.0
                        if f.gated:
                            act.activation(sig[:, slot, 0:w], ps[:, slot * 2, 0:w], func, bias=bias).then_inc(self.sem("sig"), 1)
                        else:
                            act.activation(hid[u.par][:, m, 0:w], ps[:, slot, 0:w], func, bias=bias).then_inc(self.sem("hid"), 1)

                sweep(act, f, hidden, lambda u: None)

            def dve(self, dve):
                f = self.f
                self.norm.dve(dve)
                self.route_dve(dve)
                dve.wait_ge(*self.once("cwps", 1))
                for n in range(2):
                    dve.tensor_copy(cwt[0:self.rows, 4 * P * n:4 * P * (n + 1)], ps[0:self.rows, 1 + n, 0:4 * P]).then_inc(sem("route_cwt"), 1)
                dve.tensor_copy(cwt[0:self.rows, 8 * P:T], ps[0:self.rows, 3, P - (T - 8 * P):P]).then_inc(sem("route_cwt"), 1)
                dve.sem_inc(self.sem("taken"), 2)
                if f.gated:
                    dve.sem_inc(self.sem("hid"), f.depth)

                def hidden(u):
                    if not f.gated:
                        return
                    w = CHUNKS[u.c][1]
                    for m in range(f.mt):
                        t, slot = u.tile(m)
                        dve.wait_ge(self.sem("sig"), t + 1)
                        x = ps[:, slot * 2 + 1, 0:w]
                        if f.has_bias:
                            b = wup[u.s][:, f.up_w + f.mt + m:f.up_w + f.mt + m + 1]
                            ins = dve.scalar_tensor_tensor(hid[u.par][:, m, 0:w], x, b, sig[:, slot, 0:w], ALU.add, ALU.mult)
                        else:
                            ins = dve.tensor_tensor(hid[u.par][:, m, 0:w], x, sig[:, slot, 0:w], ALU.mult)
                        ins.then_inc(self.sem("hid"), 1)

                def outputs(u):
                    t0, w = CHUNKS[u.c]
                    if u.c == 0:
                        dve.wait_ge(self.sem(f"cw{u.s}"), 16 * u.i + 16)
                    dve.wait_ge(self.sem("added"), u.n + 1)
                    dve.wait_ge(self.sem("out"), u.n + 1)
                    o, src, k = scaled[u.par], ps[:, 4 + 2 * u.par:6 + 2 * u.par, 0:w], cwb[u.s][:, t0:t0 + w]
                    if f.has_bias:
                        for d in range(C):
                            ins = dve.scalar_tensor_tensor(o[:, d, 0:w], src[:, d, :], wdn[u.s][:, f.dn_w + d:f.dn_w + d + 1], k, ALU.add, ALU.mult)
                    else:
                        ins = dve.tensor_tensor(o[:, :, 0:w], src, over(k, C), ALU.mult)
                    ins.then_inc(self.sem("taken"), 1)

                sweep(dve, f, hidden, outputs)
                if self.extra:
                    dve.wait_ge(self.sem("cw0"), 16 * (f.units // 2) + 16)
                    for c, (t0, w) in enumerate(CHUNKS):
                        u = NC * f.units + c
                        dve.wait_ge(self.sem("added"), u + 1)
                        dve.tensor_tensor(scaled[u % 2][:, :, 0:w], XN[:, :, t0:t0 + w], over(cwb[0][:, t0:t0 + w], C), ALU.mult)\
                            .then_inc(self.sem("taken"), 1)

            def pool(self, pool):
                pool.sem_inc(self.sem("added"), 2)

                def outputs(u):
                    t0, w = CHUNKS[u.c]
                    pool.wait_ge(self.sem("added"), u.n + 2)
                    pool.wait_ge(self.sem("taken"), u.n + 3)
                    h = HT[:, :, t0:t0 + w]
                    pool.tensor_tensor(h, h, scaled[u.par][:, :, 0:w], ALU.add).then_inc(self.sem("added"), 1)

                sweep(pool, self.f, lambda u: None, outputs)
                for c in range(NC * self.extra):
                    outputs(Units(self.f, self.f.units // 2, 0, c))

            def step(self, dve, ins):
                Layer.steps += 1
                ins.then_inc(sem("route_step"), 1)
                dve.wait_ge(sem("route_step"), Layer.steps)

            def top(self, dve, k, e, v, r):
                s = 8 - k
                for n in range(s):
                    self.step(dve, dve.memset(v[:, :, e + n:e + n + 1], -2e38 - n * 1e37))
                for j in range(NT):
                    ins = dve.max(top8[:, j, :], v[:, j, 0:e + s])
                self.step(dve, ins)
                self.step(dve, dve.tensor_copy(top8[:, :, k:8], v[:, :, e:e + s]))
                for j in range(NT):
                    ins = dve.match_replace(r[:, j, 0:e + s], top8[:, j, :], v[:, j, 0:e + s], 3e38)
                self.step(dve, ins)
                self.step(dve, dve.tensor_tensor(r[:, :, 0:e], r[:, :, 0:e], v[:, :, 0:e], ALU.not_equal))

            def normalise(self, dve, x, e):
                self.step(dve, dve.tensor_reduce(red[:, 1, :], x, AX.X, ALU.add))
                self.step(dve, dve.reciprocal(red[:, 2, :], red[:, 1, :]))
                self.step(dve, dve.tensor_tensor(x, x, spread(red[:, 2, :], e), ALU.mult))

            def route_act(self, act):
                e = self.experts
                if self.p in ("f0", "f2"):
                    act.wait_ge(*self.once("shifted", 1))
                    act.activation(prob[:, :, 0:e], lg[:, :, 0:e], ACT.Exp).then_inc(sem("route_prob"), 1)
                if self.p == "f1":
                    act.wait_ge(*self.once("logits", 1))
                    act.activation(prob[:, :, 0:e], ps[:, 0, 0:NT * 40].rearrange("p (a b) -> p a b", b=40)[:, :, 0:e], ACT.Sigmoid)\
                        .then_inc(sem("route_prob"), 1)

            def route_dve(self, dve):
                e, st = self.experts, self.step
                logits = ps[:, 0, 0:NT * 40].rearrange("p (a b) -> p a b", b=40)[:, :, 0:e]
                pr, v, r, x = prob[:, :, 0:e], vals, repl, cw
                dve.wait_ge(*self.once("logits", 1))
                if self.p in ("f0", "f2"):
                    st(dve, dve.tensor_reduce(red[:, 0, :], logits, AX.X, ALU.max))
                    dve.tensor_tensor(lg[:, :, 0:e], logits, spread(red[:, 0, :], e), ALU.subtract).then_inc(sem("route_shifted"), 1)
                if self.p != "f3":
                    dve.wait_ge(*self.once("prob", 1))
                if self.p == "f0":
                    self.normalise(dve, pr, e)
                    st(dve, dve.tensor_copy(v[:, :, 0:e], pr))
                    self.top(dve, 2, e, v, r)
                    st(dve, dve.memset(x[:, :, 0:1], 1.0))
                    st(dve, dve.tensor_tensor(x[:, :, 1:e + 1], pr, r[:, :, 0:e], ALU.mult))
                    self.normalise(dve, x[:, :, 1:e + 1], e)
                    last = dve.tensor_copy(red[:, 3, :], red[:, 2, :])
                if self.p == "f1":
                    st(dve, dve.tensor_reduce(grp[:, :, 0:4], pr.rearrange("p a (g b) -> p a g b", b=4), AX.X, ALU.max))
                    for n in range(4):
                        st(dve, dve.memset(grp[:, :, 4 + n:5 + n], -1e38 - n * 1e37))
                    self.top_groups(dve)
                    g4 = grpr[:, :, 0:4].unsqueeze(3).broadcast_to([P, NT, 4, 4])
                    v4 = v[:, :, 0:e].rearrange("p a (g b) -> p a g b", b=4)
                    st(dve, dve.tensor_tensor(v4, pr.rearrange("p a (g b) -> p a g b", b=4), g4, ALU.mult))
                    st(dve, dve.tensor_scalar(grpr[:, :, 0:4], grpr[:, :, 0:4], -1.0, BIG, ALU.add, ALU.mult))
                    st(dve, dve.tensor_tensor(v4, v4, g4, ALU.add))
                    self.top(dve, 4, e, v, r)
                    st(dve, dve.tensor_tensor(x[:, :, 0:e], pr, r[:, :, 0:e], ALU.mult))
                    self.normalise(dve, x[:, :, 0:e], e)
                    last = dve.tensor_scalar(x[:, :, 0:e], x[:, :, 0:e], 2.5, None, ALU.mult)
                if self.p == "f2":
                    self.normalise(dve, pr, e)
                    st(dve, dve.tensor_tensor(v[:, :, 0:e], pr, over(vec("score_b"), NT), ALU.add))
                    self.top(dve, 6, e, v, r)
                    st(dve, dve.scalar_tensor_tensor(x[:, :, 0:e], pr, 2.5, r[:, :, 0:e], ALU.mult, ALU.mult))
                    st(dve, dve.tensor_reduce(red[:, 0, :], x[:, :, 32:40], AX.X, ALU.add))
                    last = dve.tensor_copy(x[:, :, 32:33], red[:, 0, :].unsqueeze(2))
                if self.p == "f3":
                    st(dve, dve.tensor_tensor(v[:, :, 0:e], logits, over(vec("gate_b"), NT), ALU.add))
                    self.top(dve, 1, e, v, r)
                    last = dve.tensor_copy(x[:, :, 0:e], r[:, :, 0:e])
                last.then_inc(sem("route_cw"), 1)

            def top_groups(self, dve):
                for n in range(2):
                    self.step(dve, dve.memset(grp[:, :, 8 + n:9 + n], -2e38 - n * 1e37))
                for j in range(NT):
                    ins = dve.max(top8[:, j, :], grp[:, j, :])
                self.step(dve, ins)
                self.step(dve, dve.tensor_copy(top8[:, :, 2:8], grp[:, :, 4:10]))
                for j in range(NT):
                    ins = dve.match_replace(grpr[:, j, :], top8[:, j, :], grp[:, j, :], 3e38)
                self.step(dve, ins)
                self.step(dve, dve.tensor_tensor(grpr[:, :, 0:4], grpr[:, :, 0:4], grp[:, :, 0:4], ALU.not_equal))

        f0 = Layer(FFNS[0], lambda c: h_a0)
        f0.norm_gate = (sem("a0_added"), HP * B + 1)
        h_f0 = f0.done()

        def f0_sp(sp):
            f0.sp_first(sp, None)
            f0.sp(sp)

        def f0_pe(pe):
            f0.pe(pe)

        def f0_act(act):
            f0.act(act)

        def f0_dve(dve):
            f0.dve(dve)

        def f0_pool(pool):
            f0.pool(pool)

        n1a = Norm(HT, XN, lambda c: h_f0)
        n1b = Norm(XN, XN2, lambda c: [n1a.done(c)], centred=False, eps=RMS_EPS)
        ar = Arena()
        w1 = [w[:, 0:A1_W] for w in watt]
        q1, k1, v1 = ([ar.take(N) for _ in range(2)] for _ in range(3))
        sm1 = [ar.take(SCW) for _ in range(2)]
        nmax1 = ar.take(2, 2)
        sum1, rs1 = ar.take(2, 2), ar.take(2, 2)
        at1 = [ar.take(SCW) for _ in range(2)]
        vs1 = ar.take(2, P)
        og1 = ar.take(N)

        def a1_sp(sp):
            sp.wait_ge(sem("a0_y"), HP * B)
            for s in range(2):
                sp.dma_start(w1[s], dram["w_a1"][s]).then_inc(sem(f"a1_w{s}"), 16)
            with sp.Fori(1, HP // 2) as mm:
                for s in range(2):
                    sp.wait_ge(sem("a1_y"), mm * U + (s - 1) * B)
                    sp.dma_start(w1[s], dram["w_a1"][bass.ds(2 * mm + s, 1), :, :].rearrange("a p w -> p (a w)")).then_inc(sem(f"a1_w{s}"), 16)

        def a1_pe(pe):
            n1a.pe(pe)
            n1b.pe(pe)
            pe.wait_ge(*n1b.done())
            with pe.Fori(0, HP // 2) as mm:
                base = mm * U

                def project(j):
                    s, b = j // B, j % B
                    if b == 0:
                        pe.wait_ge(sem(f"a1_w{s}"), 16 * mm + 16)
                    for i in range(3):
                        for k in range(C):
                            mmul = pe.matmul(ps[:, i, 0:N], w1[s][:, (i * C + k) * P:(i * C + k + 1) * P],
                                             XN2[:, k, b * N:(b + 1) * N], start=(k == 0), stop=(k == C - 1))
                        if i:
                            mmul.then_inc(sem("a1_proj"), 1)

                def values(j):
                    pe.wait_ge(sem("a1_v"), base + j + 1)
                    for i in range(2):
                        mmul = pe.transpose(ps[:, 7, i * P:(i + 1) * P], v1[j % 2][:, i * P:(i + 1) * P], ident)
                    mmul.then_inc(sem("a1_vt"), 1)

                def scores(j):
                    pe.wait_ge(sem("a1_qk"), base + j + 1)
                    pe.wait_ge(sem("a1_added"), base + j + 1)
                    for h in range(2):
                        rows = slice(64 * h, 64 * h + 64)
                        q, k = q1[j % 2][rows, :], k1[j % 2][rows, :]
                        pe.matmul(ps[:, 4 + h, 0:SC0], k[:, 0:P], q, start=True, stop=True)
                        pe.matmul(ps[:, 4 + h, SC0:SCW], k[:, P:2 * P], q[:, P:N], start=True, stop=True).then_inc(sem("a1_s"), 1)

                def mix(j):
                    pe.wait_ge(sem("a1_vs"), base + j + 1)
                    for h in range(2):
                        o = ps[64 * h:64 * h + 64, 6, :]
                        pe.matmul(o[:, 0:N], vs1[:, 0, 64 * h:64 * h + 64], at1[h][:, 0:SC0], start=True, stop=False)
                        mmul = pe.matmul(o[:, P:N], vs1[:, 1, 64 * h:64 * h + 64], at1[h][:, SC0:SCW], start=False, stop=True)
                    mmul.then_inc(sem("a1_o"), 1)

                def output(j):
                    pe.wait_ge(sem("a1_og"), base + j + 1)
                    for d in range(C):
                        mmul = pe.matmul(ps[:, 4 + d, 0:N], w1[j // B][:, 768 + d * P:768 + (d + 1) * P], og1, start=True, stop=True)
                    mmul.then_inc(sem("a1_y"), 1)

                project(0)
                values(0)
                for j in range(U):
                    scores(j)
                    if j + 1 < U:
                        project(j + 1)
                    mix(j)
                    if j + 1 < U:
                        values(j + 1)
                    output(j)

        def a1_act(act):
            n1a.act(act)
            n1b.act(act)
            with act.Fori(0, HP // 2) as mm:
                base = mm * U

                def take(j):
                    w = w1[j // B]
                    act.wait_ge(sem("a1_proj"), 2 * base + 2 * j + 1)
                    act.activation(q1[j % 2], ps[:, 0, 0:N], ACT.Identity, bias=w[:, 1024:1025])
                    act.activation(k1[j % 2], ps[:, 1, 0:N], ACT.Identity, bias=w[:, 1025:1026]).then_inc(sem("a1_qk"), 1)
                    act.wait_ge(sem("a1_proj"), 2 * base + 2 * j + 2)
                    act.activation(v1[j % 2], ps[:, 2, 0:N], ACT.Identity, bias=w[:, 1026:1027]).then_inc(sem("a1_v"), 1)

                def exps(j):
                    for h in range(2):
                        act.wait_ge(sem("a1_max"), 2 * base + 2 * j + h + 1)
                        for i, (a, b) in enumerate(((0, SC0), (SC0, SCW))):
                            e = act.activation(at1[h][:, a:b], sm1[h][:, a:b], ACT.Exp, bias=nmax1[:, h, i:i + 1],
                                               accum_out=sum1[:, h, i:i + 1])
                        e.then_inc(sem("a1_exp"), 1)

                take(0)
                for j in range(U):
                    exps(j)
                    if j + 1 < U:
                        take(j + 1)

        def a1_dve(dve):
            n1a.dve(dve)
            n1b.dve(dve)
            dve.wait_ge(*n1b.done())
            for c in range(C):
                h = HT[:, c, :]
                dve.tensor_scalar(h, h, vec("bO1")[:, c:c + 1], None, ALU.add).then_inc(sem("a1_bias"), 1)
            dve.wait_ge(sem("a1_bias"), C)
            dve.sem_inc(sem("a1_added"), 1)
            with dve.Fori(0, HP // 2) as mm:
                base = mm * U

                def hide(j):
                    for h in range(2):
                        n = 2 * base + 2 * j + h
                        dve.wait_ge(sem("a1_s"), n + 1)
                        dve.tensor_tensor(sm1[h], ps[:, 4 + h, 0:SCW], const("hide"), ALU.add).then_inc(sem("a1_hid"), 1)
                        dve.wait_ge(sem("a1_hid"), n + 1)
                        dve.tensor_reduce(nmax1[:, h, 0:1], sm1[h][:, 0:SC0], AX.X, ALU.max, negate=True)
                        dve.tensor_reduce(nmax1[:, h, 1:2], sm1[h][:, SC0:SCW], AX.X, ALU.max, negate=True).then_inc(sem("a1_max"), 1)

                def values(j):
                    n = base + j + 1
                    dve.wait_ge(sem("a1_exp"), 2 * n)
                    dve.reciprocal(rs1, sum1).then_inc(sem("a1_rs"), 1)
                    dve.wait_ge(sem("a1_rs"), n)
                    dve.wait_ge(sem("a1_vt"), n)
                    for h in range(2):
                        v = ps[:, 7, 0:2 * P].rearrange("p (a b) -> p a b", b=P)[:, :, 64 * h:64 * h + 64]
                        ins = dve.tensor_tensor(vs1[:, :, 64 * h:64 * h + 64], v, spread(rs1[:, h, :], 64), ALU.mult)
                    ins.then_inc(sem("a1_vs"), 1)

                def take(j):
                    n = base + j + 1
                    dve.wait_ge(sem("a1_o"), n)
                    dve.tensor_copy(og1, ps[:, 6, 0:N]).then_inc(sem("a1_oc"), 1)
                    dve.wait_ge(sem("a1_oc"), n)
                    dve.tensor_tensor(og1[:, N - 1:N], og1[:, N - 1:N], v1[j % 2][:, N - 1:N], ALU.add).then_inc(sem("a1_og"), 1)

                def add(j):
                    h = HT[:, :, (j % B) * N:(j % B + 1) * N]
                    dve.wait_ge(sem("a1_y"), base + j + 1)
                    dve.tensor_tensor(h, h, ps[:, 4:6, 0:N], ALU.add).then_inc(sem("a1_added"), 1)

                for j in range(U):
                    hide(j)
                    values(j)
                    take(j)
                    add(j)

        h_a1 = [(sem("a1_added"), HP * B + 1)]

        f1 = Layer(FFNS[1], lambda c: h_a1)
        f1.norm_gate = h_a1[0]
        h_f1 = f1.done()

        def f1_sp(sp):
            f1.sp_first(sp, f0)
            f1.sp(sp)

        def f1_pe(pe):
            f1.pe(pe)

        def f1_act(act):
            f1.act(act)

        def f1_dve(dve):
            f1.dve(dve)

        def f1_pool(pool):
            f1.pool(pool)

        n2 = Norm(HT, XN, lambda c: h_f1)
        ar = Arena()
        H4 = 4
        w2 = [w[:, 0:A2_W] for w in watt]
        q2, k2, v2 = ([ar.take(N) for _ in range(2)] for _ in range(3))
        pr2 = [ar.take(H4, N) for _ in range(2)]
        mx2, nm2 = ar.take(2, H4), ar.take(2, H4)
        sm2, rs2 = ar.take(2, H4), ar.take(2, H4)
        pt2 = ar.take(2, H4 * N)
        vt2 = ar.take(2, P)
        ql2 = ar.take(H4)
        vl2 = ar.take(H4)
        pl2 = ar.take(N, rows=H4)
        ml2 = ar.take(4, rows=H4)
        pk2 = ar.take(N, rows=H4)
        vr2 = ar.take(P, rows=H4)
        os2 = ar.take(N)
        QS = 1.0 / 16
        pt2v = pt2.rearrange("p t (h q) -> p t h q", q=N)
        UA2 = 2 * B

        def a2_sp(sp):
            sp.wait_ge(sem("a1_y"), HP * B)
            for s in range(2):
                sp.dma_start(w2[s], dram["w_a2"][s]).then_inc(sem(f"a2_w{s}"), 16)
            for s in range(2):
                sp.wait_ge(sem("a2_qk"), B * (s + 1))
                sp.wait_ge(sem("a2_v"), B * (s + 1))
                sp.dma_start(w2[s], dram["w_a2"][2 + s]).then_inc(sem(f"a2_w{s}"), 16)

        def a2_pe(pe):
            n2.pe(pe)
            pe.wait_ge(*n2.done())
            with pe.Fori(0, 2) as mm:
                base = mm * UA2

                def project(j):
                    s, b = j // B, j % B
                    if b == 0:
                        pe.wait_ge(sem(f"a2_w{s}"), 16 * mm + 16)
                    pe.wait_ge(sem("a2_taken"), base + j + 1)
                    for i in range(3):
                        for k in range(C):
                            mmul = pe.matmul(ps[:, i, 0:N], w2[s][:, (i * C + k) * P:(i * C + k + 1) * P],
                                             XN[:, k, b * N:(b + 1) * N], start=(k == 0), stop=(k == C - 1))
                        if i:
                            mmul.then_inc(sem("a2_proj"), 1)

                def unit(j):
                    n = base + j
                    q, k, v = q2[j % 2], k2[j % 2], v2[j % 2]
                    pe.wait_ge(sem("a2_qk"), n + 1)
                    for i in range(2):
                        if i:
                            pe.wait_ge(sem("a2_exp"), 3 * n + 1)
                            pe.nop(nofuse=True)
                        for h in range(H4):
                            r = slice(32 * h, 32 * h + 32)
                            mmul = pe.matmul(ps[:, 4 + h, 0:N], q[r, i * P:(i + 1) * P], k[r, :], start=True, stop=True)
                        mmul.then_inc(sem("a2_s"), 1)
                        if i == 0:
                            pe.wait_ge(sem("a2_v"), n + 1)
                            pe.wait_ge(sem("a2_last"), n + 1)
                            for t in range(2):
                                pe.transpose(ps[:, 3, t * P:(t + 1) * P], v[:, t * P:(t + 1) * P], ident)
                            pe.transpose(ps[0:H4, 3, 2 * P:3 * P], vl2, ident).then_inc(sem("a2_vt"), 1)
                            pe.matmul(ps[0:H4, 2, 0:N], ql2, k, start=True, stop=True).then_inc(sem("a2_s"), 1)
                    for i in range(2):
                        pe.wait_ge(sem("a2_p"), 2 * n + i + 1)
                        if i:
                            pe.wait_ge(sem("a2_pt"), 2 * n + 1)
                        for h in range(H4):
                            for t in range(2):
                                pe.transpose(ps[:, t, h * P:(h + 1) * P], pr2[i][:, h, t * P:(t + 1) * P], ident)
                        if i == 0:
                            pe.wait_ge(sem("a2_pl"), n + 1)
                            pe.nop(nofuse=True)
                            for t in range(2):
                                pe.transpose(ps[:, 2, 300 + H4 * t:300 + H4 * (t + 1)], pl2[:, t * P:(t + 1) * P], ident[0:H4, 0:H4])
                        pe.transpose(ps[0:H4, 2, i * P:(i + 1) * P], pr2[i][:, :, N - 1], ident).then_inc(sem("a2_tp"), 1)
                    pe.wait_ge(sem("a2_pt"), 2 * n + 2)
                    pe.wait_ge(sem("a2_vsb"), n + 1)
                    for h in range(H4):
                        for t in range(2):
                            pe.matmul(ps[32 * h:32 * h + 32, 3, 0:N], vt2[:, t, 32 * h:32 * h + 32], pt2v[:, t, h, :],
                                      start=(t == 0), stop=(t == 1))
                    pe.matmul(ps[:, 3, 0:N], vr2, pk2, start=False, stop=True, skip_group_check=True).then_inc(sem("a2_o"), 1)

                def output(j):
                    c = j // B
                    pe.wait_ge(sem("a2_os"), base + j + 1)
                    pe.matmul(ps[64 * c:64 * c + 64, 2, 0:N], const("unpad")[:, 0:64], os2, start=True, stop=True).then_inc(sem("a2_y"), 1)

                for j in range(UA2):
                    project(j)
                    unit(j)
                    output(j)

        def a2_act(act):
            n2.act(act)
            with act.Fori(0, 2) as mm:
                base = mm * UA2
                for j in range(UA2):
                    n = base + j
                    act.wait_ge(sem("a2_proj"), 2 * n + 1)
                    act.copy(q2[j % 2], ps[:, 0, 0:N])
                    act.copy(k2[j % 2], ps[:, 1, 0:N]).then_inc(sem("a2_qk"), 1)
                    act.wait_ge(sem("a2_proj"), 2 * n + 2)
                    act.copy(v2[j % 2], ps[:, 2, 0:N]).then_inc(sem("a2_v"), 1)
                    for i in range(3):
                        act.wait_ge(sem("a2_max"), 3 * n + i + 1)
                        if i == 1:
                            act.activation(pl2, ps[0:H4, 2, 0:N], ACT.Exp, bias=ml2[:, 1:2], scale=QS, accum_out=ml2[:, 2:3])\
                                .then_inc(sem("a2_exp"), 1)
                            continue
                        i //= 2
                        for h in range(H4):
                            e = act.activation(pr2[i][:, h, :], ps[:, 4 + h, 0:N], ACT.Exp, bias=nm2[:, i, h:h + 1], scale=QS,
                                               accum_out=sm2[:, i, h:h + 1])
                        e.then_inc(sem("a2_exp"), 1)

        def a2_dve(dve):
            n2.dve(dve)
            dve.wait_ge(*n2.done())
            dve.sem_inc(sem("a2_taken"), 1)
            with dve.Fori(0, 2) as mm:
                base = mm * UA2
                for j in range(UA2):
                    n = base + j
                    q, k, v = q2[j % 2], k2[j % 2], v2[j % 2]
                    dve.wait_ge(sem("a2_qk"), n + 1)
                    dve.tensor_scalar(ql2, const("block4"), q[:, N - 1:N], None, ALU.mult)
                    dve.wait_ge(sem("a2_v"), n + 1)
                    dve.tensor_scalar(vl2, const("block4"), v[:, N - 1:N], None, ALU.mult).then_inc(sem("a2_last"), 1)
                    for i in range(3):
                        dve.wait_ge(sem("a2_s"), 3 * n + i + 1)
                        if i == 1:
                            dve.tensor_reduce(ml2[:, 0:1], ps[0:H4, 2, 0:N], AX.X, ALU.max, negate=True).then_inc(sem("a2_mx"), 1)
                            dve.wait_ge(sem("a2_mx"), 3 * n + i + 1)
                            dve.tensor_scalar(ml2[:, 1:2], ml2[:, 0:1], QS, None, ALU.mult).then_inc(sem("a2_max"), 1)
                        else:
                            dve.tensor_reduce(mx2[:, i // 2, :], ps[:, 4:8, 0:N], AX.X, ALU.max, negate=True).then_inc(sem("a2_mx"), 1)
                            dve.wait_ge(sem("a2_mx"), 3 * n + i + 1)
                            dve.tensor_scalar(nm2[:, i // 2, :], mx2[:, i // 2, :], QS, None, ALU.mult).then_inc(sem("a2_max"), 1)
                    dve.wait_ge(sem("a2_exp"), 3 * n + 2)
                    dve.reciprocal(ml2[:, 3:4], ml2[:, 2:3]).then_inc(sem("a2_rs"), 1)
                    dve.wait_ge(sem("a2_rs"), 3 * n + 1)
                    dve.tensor_scalar(pl2, pl2, ml2[:, 3:4], None, ALU.mult).then_inc(sem("a2_pl"), 1)
                    dve.wait_ge(sem("a2_pl"), n + 1)
                    dve.tensor_copy(pk2[:, N - 1:N], pl2[:, N - 1:N])
                    dve.wait_ge(sem("a2_vt"), n + 1)
                    dve.tensor_copy(vt2, ps[:, 3, 0:2 * P].rearrange("p (a b) -> p a b", b=P))
                    dve.tensor_copy(vr2, ps[0:H4, 3, 2 * P:3 * P]).then_inc(sem("a2_vsb"), 1)
                    for i in range(2):
                        dve.wait_ge(sem("a2_exp"), 3 * n + 1 + 2 * i)
                        dve.reciprocal(rs2[:, i, :], sm2[:, i, :]).then_inc(sem("a2_rs"), 1)
                        dve.wait_ge(sem("a2_rs"), 3 * n + 2 + i)
                        dve.tensor_tensor(pr2[i], pr2[i], spread(rs2[:, i, :], N), ALU.mult).then_inc(sem("a2_p"), 1)
                    for i in range(2):
                        dve.wait_ge(sem("a2_tp"), 2 * n + i + 1)
                        for t in range(2):
                            dve.tensor_copy(pt2v[:, t, :, i * P:(i + 1) * P], ps[:, t, :].rearrange("p (h q) -> p h q", q=P))
                        if i == 0:
                            dve.tensor_copy(pt2v[:, :, :, N - 1], ps[:, 2, 300:300 + 2 * H4].rearrange("p (t h) -> p t h", h=H4))
                        dve.tensor_copy(pk2[:, i * P:(i + 1) * P], ps[0:H4, 2, i * P:(i + 1) * P]).then_inc(sem("a2_pt"), 1)
                    dve.wait_ge(sem("a2_o"), n + 1)
                    dve.tensor_copy(os2, ps[:, 3, 0:N]).then_inc(sem("a2_os"), 1)
                    dve.wait_ge(sem("a2_y"), n + 1)
                    c, b = j // B, j % B
                    r = slice(64 * c, 64 * c + 64)
                    h = HT[r, bass.ds(mm, 1), b * N:(b + 1) * N].rearrange("p a n -> p (a n)")
                    dve.tensor_tensor(h, h, ps[r, 2, 0:N], ALU.add).then_inc(sem("a2_taken"), 1)

        h_a2 = [(sem("a2_taken"), 4 * B + 1)]

        f2 = Layer(FFNS[2], lambda c: h_a2)
        f2.norm_gate = h_a2[0]
        h_f2 = f2.done()

        def f2_sp(sp):
            f2.sp_first(sp, f1)
            f2.sp(sp)

        def f2_pe(pe):
            f2.pe(pe)

        def f2_act(act):
            f2.act(act)

        def f2_dve(dve):
            f2.dve(dve)

        def f2_pool(pool):
            f2.pool(pool)

        n3 = Norm(HT, XN, lambda c: h_f2)
        DI, NS, KT = 512, 16, 4
        NH = NS // 2
        ar = Arena()
        u3, r3, d3 = ar.take(KT, T), ar.take(KT, T), ar.take(KT, T)
        at_bufs = ar.at
        hb3 = [ar.take(NH * N) for _ in range(4)]
        bc3 = [[ar.take(NH * N) for _ in range(4)],
               [x[:, :, :].rearrange("p c t -> p (c t)") for x in (XN, XN2, XC, SQ)]]
        al = Arena()
        al.at = at_bufs
        win3, wde3, wbc3 = al.take(C, 2 * DI), al.take(KT, DI), al.take(KT, 2 * NS)
        ab3 = al.take(KT, T)
        bct3 = al.take(T, rows=2 * NS)
        dA3 = [w[:, 0:NH * N] for w in wup]
        wo3 = watt[0][:, 0:KT * D].rearrange("p (k d) -> p k d", d=D)
        a3c = watt[0][:, KT * D:KT * D + 64]
        a3e = watt[0][:, KT * D + 64:KT * D + 128]
        du3 = [watt[1][:, N * i:N * (i + 1)] for i in range(2)]
        y3 = [watt[1][:, N * (2 + i):N * (3 + i)] for i in range(2)]
        bcd = nc.dram_tensor("state_rows", (2 * NS, T), f32, kind="Internal").ap()
        UB = 4 * KT

        def bc_load(sp, b, s):
            for i in range(4):
                src = bcd[NH * i:NH * (i + 1), b * N:(b + 1) * N] if isinstance(b, int) else bcd[NH * i:NH * (i + 1), bass.ds(b * N, N)]
                dst = bc3[s][i].rearrange("p (n t) -> p n t", t=N)
                sp.dma_start(dst, src.unsqueeze(0).broadcast_to([P, NH, N])).then_inc(sem(f"a3_bc{s}"), 16)

        def a3_sp(sp):
            sp.wait_ge(*h_f2[0])
            sp.dma_start(win3, dram["w3_in"]).then_inc(sem("a3_w"), 16)
            sp.dma_start(wde3, dram["w3_delta"]).then_inc(sem("a3_w"), 16)
            sp.dma_start(wbc3, dram["w3_bc"]).then_inc(sem("a3_w"), 16)
            sp.dma_start(wo3, dram["w3_out"]).then_inc(sem("a3_w"), 16)
            sp.wait_ge(sem("a3_bct"), NC)
            sp.dma_start(bcd, bct3).then_inc(sem("a3_bcd"), 16)
            sp.wait_ge(sem("a3_bcd"), 16)
            sp.wait_ge(sem("a3_delta"), KT)
            for b in range(2):
                bc_load(sp, b, b)
            for s in range(2):
                sp.wait_ge(sem("a3_hc"), 2 * KT * (s + 1))
                bc_load(sp, 2 + s, s)

        def a3_pe(pe):
            n3.pe(pe)
            pe.wait_ge(*n3.done())
            pe.wait_ge(sem("a3_w"), 64)
            n = 0
            for m in range(2 * KT):
                for t0, w in CHUNKS:
                    if n >= 4:
                        pe.wait_ge(sem("a3_in"), n - 3)
                    for k in range(C):
                        mmul = pe.matmul(ps[:, n % 4, 0:w], win3[:, k, m * P:(m + 1) * P], XN[:, k, t0:t0 + w], start=(k == 0), stop=(k == C - 1))
                    mmul.then_inc(sem("a3_inps"), 1)
                    n += 1
            for c, (t0, w) in enumerate(CHUNKS):
                for k in range(KT):
                    mmul = pe.matmul(ps[0:2 * NS, 4 + c, 0:w], wbc3[:, k, :], u3[:, k, t0:t0 + w], start=(k == 0), stop=(k == KT - 1))
                mmul.then_inc(sem("a3_bcps"), 1)
            n = 0
            pe.wait_ge(sem("a3_in"), 2 * KT * NC)
            for m in range(KT):
                for t0, w in CHUNKS:
                    if n >= 4:
                        pe.wait_ge(sem("a3_pre"), n - 3)
                    for k in range(KT):
                        mmul = pe.matmul(ps[:, n % 4, 0:w], wde3[:, k, m * P:(m + 1) * P], u3[:, k, t0:t0 + w], start=(k == 0), stop=(k == KT - 1))
                    mmul.then_inc(sem("a3_deps"), 1)
                    n += 1
            pe.wait_ge(sem("a3_pre"), KT * NC)
            pe.wait_ge(sem("a3_bct"), NC)
            pe.sem_inc(sem("a3_sum"), 4)
            with pe.Fori(0, 2) as bb:
                base = UB * bb

                def total(s, ct, hf):
                    n = 8 * s + 2 * ct + hf
                    pe.wait_ge(sem("a3_hc"), base + n + 1)
                    if hf == 0:
                        pe.wait_ge(sem("a3_yfree"), 2 * KT * bb + KT * s + ct + 1)
                    for i in range(NH):
                        mmul = pe.matmul(ps[:, ct % 2, 0:N], ident, hb3[n % 4][:, i * N:(i + 1) * N],
                                         start=(hf == 0 and i == 0), stop=(hf == 1 and i == NH - 1))
                    mmul.then_inc(sem("a3_sum"), 1)

                def output(s, ct):
                    pe.wait_ge(sem("a3_y"), 2 * KT * bb + KT * s + ct + 1)
                    if ct == 0:
                        pe.wait_ge(sem("a3_added"), 2 * bb + s + 1)
                    for d in range(C):
                        mmul = pe.matmul(ps[:, 4 + 2 * s + d, 0:N], wo3[:, ct, d * P:(d + 1) * P], y3[ct % 2], start=(ct == 0), stop=(ct == KT - 1))
                    mmul.then_inc(sem("a3_o"), 1)

                last = None
                for s in range(2):
                    for ct in range(KT):
                        total(s, ct, 0)
                        if last:
                            output(*last)
                        total(s, ct, 1)
                        last = (s, ct)
                output(*last)

        def a3_act(act):
            n3.act(act)
            act.activation(a3e, vec("A_log"), ACT.Exp).then_inc(sem("a3_ae"), 1)
            n = 0
            for m in range(2 * KT):
                dst = u3[:, m, :] if m < KT else r3[:, m - KT, :]
                for t0, w in CHUNKS:
                    act.wait_ge(sem("a3_inps"), n + 1)
                    act.activation(dst[:, t0:t0 + w], ps[:, n % 4, 0:w], ACT.Silu).then_inc(sem("a3_in"), 1)
                    n += 1
            for c, (t0, w) in enumerate(CHUNKS):
                act.wait_ge(sem("a3_bcps"), c + 1)
                act.copy(bct3[:, t0:t0 + w], ps[0:2 * NS, 4 + c, 0:w]).then_inc(sem("a3_bct"), 1)
            n = 0
            for m in range(KT):
                for t0, w in CHUNKS:
                    act.wait_ge(sem("a3_deps"), n + 1)
                    act.activation(d3[:, m, t0:t0 + w], ps[:, n % 4, 0:w], ACT.Identity, bias=vec("b_delta")[:, m:m + 1])
                    act.activation(ab3[:, m, t0:t0 + w], ps[:, n % 4, 0:w], ACT.Abs, bias=vec("b_delta")[:, m:m + 1]).then_inc(sem("a3_pre"), 1)
                    n += 1
                act.wait_ge(sem("a3_pre"), n)
                act.activation(ab3[:, m, :], ab3[:, m, :], ACT.Exp, scale=-1.0).then_inc(sem("a3_sp"), 1)
                act.wait_ge(sem("a3_sp"), 2 * m + 1)
                act.activation(ab3[:, m, :], ab3[:, m, :], ACT.Ln, bias=1.0).then_inc(sem("a3_sp"), 1)
            act.wait_ge(sem("a3_delta"), KT)
            act.wait_ge(sem("a3_a"), 3)
            with act.Fori(0, 2) as bb:
                base = UB * bb
                for s in range(2):
                    for ct in range(KT):
                        for hf in range(2):
                            n = 8 * s + 2 * ct + hf
                            act.wait_ge(sem("a3_dafree"), base + n + 1)
                            act.nop(nofuse=True)
                            d = d3[:, ct, bass.ds((2 * bb + s) * N + 1, N - 1)]
                            for i in range(NH):
                                col = ct * NS + hf * NH + i
                                e = act.activation(dA3[n % 2][:, i * N + 1:(i + 1) * N], d, ACT.Exp, scale=a3c[:, col:col + 1])
                            e.then_inc(sem("a3_da"), 1)

        def a3_dve(dve):
            n3.dve(dve)
            dve.wait_ge(sem("a3_ae"), 1)
            dve.tensor_scalar(a3c, a3e, -1.0, None, ALU.mult).then_inc(sem("a3_a"), 1)
            for i in range(2):
                dve.memset(dA3[i].rearrange("p (n t) -> p n t", t=N)[:, :, 0:1], 0.0).then_inc(sem("a3_a"), 1)
            for m in range(KT):
                dve.wait_ge(sem("a3_sp"), 2 * m + 2)
                dve.scalar_tensor_tensor(d3[:, m, :], d3[:, m, :], 0.0, ab3[:, m, :], ALU.max, ALU.add).then_inc(sem("a3_delta"), 1)
            dve.sem_inc(sem("a3_dafree"), 2)
            dve.sem_inc(sem("a3_yfree"), 2)
            dve.sem_inc(sem("a3_added"), 2)
            with dve.Fori(0, 2) as bb:
                base = UB * bb

                def scan(s, ct, hf):
                    n = 8 * s + 2 * ct + hf
                    h = hb3[n % 4]
                    dve.wait_ge(sem("a3_da"), base + n + 1)
                    dve.wait_ge(sem("a3_dbu"), base + n + 1)
                    dve.tensor_tensor_scan(h, dA3[n % 2], h, 0.0, ALU.mult, ALU.add).then_inc(sem("a3_dafree"), 1)
                    dve.wait_ge(sem("a3_dafree"), base + n + 3)
                    dve.tensor_tensor(h, h, bc3[s][2 + hf], ALU.mult).then_inc(sem("a3_hc"), 1)

                def finish(s, ct):
                    n = 2 * KT * bb + KT * s + ct
                    cols = bass.ds((2 * bb + s) * N, N)
                    dve.wait_ge(sem("a3_sum"), 2 * n + 6)
                    dve.scalar_tensor_tensor(y3[ct % 2], u3[:, ct, cols], vec("D_param")[:, ct:ct + 1], ps[:, ct % 2, 0:N], ALU.mult, ALU.add)\
                        .then_inc(sem("a3_yfree"), 1)
                    dve.wait_ge(sem("a3_yfree"), n + 3)
                    dve.tensor_tensor(y3[ct % 2], y3[ct % 2], r3[:, ct, cols], ALU.mult).then_inc(sem("a3_y"), 1)

                def add(s):
                    h = HT[:, :, bass.ds((2 * bb + s) * N, N)]
                    dve.wait_ge(sem("a3_o"), 2 * KT * bb + KT * (s + 1))
                    dve.tensor_tensor(h, h, ps[:, 4 + 2 * s:6 + 2 * s, 0:N], ALU.add).then_inc(sem("a3_added"), 1)

                last = None
                for s in range(2):
                    for ct in range(KT):
                        scan(s, ct, 0)
                        if last:
                            finish(*last)
                        scan(s, ct, 1)
                        if last and last[1] == KT - 1:
                            add(last[0])
                        last = (s, ct)
                finish(*last)
                add(last[0])

        def a3_pool(pool):
            pool.wait_ge(sem("a3_delta"), KT)
            pool.sem_inc(sem("a3_du"), 1)
            with pool.Fori(0, 2) as bb:
                base = UB * bb
                for s in range(2):
                    cols = bass.ds((2 * bb + s) * N, N)
                    for ct in range(KT):
                        for hf in range(2):
                            n = 8 * s + 2 * ct + hf
                            d = du3[ct % 2]
                            if hf == 0:
                                if ct == 0:
                                    pool.wait_ge(sem(f"a3_bc{s}"), 64 * bb + 64)
                                pool.nop(nofuse=True)
                                pool.tensor_tensor(d, d3[:, ct, cols], u3[:, ct, cols], ALU.mult).then_inc(sem("a3_du"), 1)
                                pool.wait_ge(sem("a3_du"), 2 * KT * bb + KT * s + ct + 2)
                            pool.wait_ge(sem("a3_sum"), base + n + 1)
                            pool.tensor_tensor(hb3[n % 4].rearrange("p (n t) -> p n t", t=N), bc3[s][hf].rearrange("p (n t) -> p n t", t=N),
                                               over(d, NH), ALU.mult).then_inc(sem("a3_dbu"), 1)

        h_a3 = [(sem("a3_added"), B + 2)]

        f3 = Layer(FFNS[3], lambda c: h_a3)
        f3.norm_gate = h_a3[0]
        h_f3 = f3.done()

        def f3_sp(sp):
            sp.wait_ge(*h_a3[0])
            f3.sp_first(sp, f2)
            f3.sp(sp)

        def f3_pe(pe):
            f3.pe(pe)

        def f3_act(act):
            f3.act(act)

        def f3_dve(dve):
            f3.dve(dve)

        def f3_pool(pool):
            f3.pool(pool)

        def store_sp(sp):
            for s, v in h_f3:
                sp.wait_ge(s, v)
            sp.dma_start(out.rearrange("(c p) t -> p c t", p=P), HT[:, :, :]).then_inc(sem("stored"), 16)
            sp.wait_ge(sem("stored"), 16)

        block = ctx.enter_context(nc.Block())

        @block.sync
        def _(sp):
            tok_sp(sp)
            a0_sp(sp)
            f0_sp(sp)
            a1_sp(sp)
            f1_sp(sp)
            a2_sp(sp)
            f2_sp(sp)
            a3_sp(sp)
            f3_sp(sp)
            store_sp(sp)

        @block.tensor
        def _(pe):
            tok_pe(pe)
            tok_norm.pe(pe)
            a0_pe(pe)
            f0_pe(pe)
            a1_pe(pe)
            f1_pe(pe)
            a2_pe(pe)
            f2_pe(pe)
            a3_pe(pe)
            f3_pe(pe)

        @block.scalar
        def _(act):
            tok_norm.act(act)
            a0_act(act)
            f0_act(act)
            a1_act(act)
            f1_act(act)
            a2_act(act)
            f2_act(act)
            a3_act(act)
            f3_act(act)

        @block.vector
        def _(dve):
            tok_dve(dve)
            tok_norm.dve(dve)
            tok_cls(dve)
            a0_dve(dve)
            f0_dve(dve)
            a1_dve(dve)
            f1_dve(dve)
            a2_dve(dve)
            f2_dve(dve)
            a3_dve(dve)
            f3_dve(dve)

        @block.gpsimd
        def _(pool):
            a0_pool(pool)
            f0_pool(pool)
            f1_pool(pool)
            f2_pool(pool)
            a3_pool(pool)
            f3_pool(pool)


def constants():
    out = np.zeros((P, CONST_W), np.float32)
    r = np.arange(P)

    def put(name, v):
        a, b = CONSTS[name]
        out[:, a:b] = v
    put("ident", np.eye(P))
    put("mean", 1.0 / D)
    put("headones", r[:, None] // 64 == r[None, :] // 64)
    put("expo", np.arange(EMIN, EMAX + 1)[None])
    put("expo_r", np.arange(EMAX, EMIN - 1, -1)[None])
    seen = np.concatenate([np.arange(N)[None] >= r[:, None], np.arange(P, N)[None] >= r[:, None] + P], 1)
    put("causal", seen)
    put("hide", np.where(seen, 0.0, -BIG))
    un = np.zeros((P, 2, 64))
    for p in range(P):
        if p % 32 < 16:
            un[p, 0, 16 * (p // 32) + p % 32] = 1
    un[:, 1] = un[:, 0]
    put("unpad", un.reshape(P, -1))
    put("block4", r[:, None] // 32 == np.arange(4)[None])
    return out


def by_part(a):
    a = np.asarray(a)
    return np.ascontiguousarray(a.reshape((-1, P) + a.shape[1:]).swapaxes(0, 1))


def pack(*parts):
    return np.concatenate([np.asarray(p, np.float32).reshape(P, -1) for p in parts], 1)


def layouts(i):
    i = {k: np.asarray(v) for k, v in i.items()}
    a = {"consts": constants()}
    x = i["x"].reshape(B, 5, 16, 8, 16, 8).transpose(0, 2, 4, 1, 3, 5).reshape(B * D, PF)
    a["xt"] = by_part(np.concatenate([x.T, np.zeros((3 * P - PF, B * D), np.float32)]))
    a["wtok"] = by_part(np.concatenate([i["L0_tok_W"], np.zeros((3 * P - PF, D), np.float32)]))

    def col(v):
        return by_part(v.reshape(-1))

    a["vecs"] = pack(col(i["cls_tok"]), col(i["L0_tok_gamma"]), col(i["L0_attn_ln_gamma"]), col(i["L0_attn_ln_beta"]),
                     col(i["L0_attn_bO"]), col(i["L1_attn_b_o"]), col(i["L0_attn_alpha_logit"]), col(i["L3_attn_b_delta"]),
                     by_part(i["L3_attn_A_log"]), col(i["L3_attn_D_param"]),
                     np.repeat(i["L3_ffn_gate_b"][None], P, 0), np.repeat(i["L2_ffn_e_score_correction_bias"][None], P, 0))
    pairs = []
    for m in range(HP):
        rows = slice(m * P, (m + 1) * P)
        pairs.append(pack(*[by_part(i["L0_attn_W" + n][rows].T) for n in ("Q", "K", "V", "g")],
                          i["L0_attn_WO"][:, rows].T, *[col(i["L0_attn_b" + n][rows]) for n in ("Q", "K", "V", "g")]))
    a["w_a0"] = np.stack(pairs)
    w, bq = i["L1_attn_W_qkv"].reshape(1024, 3, D), i["L1_attn_b_qkv"].reshape(1024, 3)
    pairs = []
    for m in range(HP):
        rows = slice(m * P, (m + 1) * P)
        pairs.append(pack(*[by_part(w[rows, n].T) for n in range(3)], i["L1_attn_W_o"][:, rows].T,
                          *[col(bq[rows, n]) for n in range(3)]))
    a["w_a1"] = np.stack(pairs)
    quads = []
    for m in range(4):
        parts = []
        for n in "qkv":
            wt = np.zeros((D, 4, 32), np.float32)
            wt[:, :, 0:16] = i["L2_attn_W" + n][64 * m:64 * m + 64].T.reshape(D, 4, 16)
            parts.append(by_part(wt.reshape(D, P)))
        quads.append(pack(*parts))
    a["w_a2"] = np.stack(quads)
    def ups(mats, biases=()):
        return pack(*[by_part(m) for m in mats], *[col(b) for b in biases])
    f0 = [(i["L0_ffn_w1_shared"], i["L0_ffn_w2_shared"])] + list(zip(i["L0_ffn_w1_routed"], i["L0_ffn_w2_routed"]))
    a["up_f0"] = np.stack([ups([w1]) for w1, _ in f0])
    a["dn_f0"] = np.stack([pack(by_part(w2)) for _, w2 in f0])
    a["up_f1"] = np.stack([ups([i["L1_ffn_W1"][e].T, i["L1_ffn_W3"][e].T], [i["L1_ffn_b1"][e], i["L1_ffn_b3"][e]]) for e in range(16)])
    a["dn_f1"] = np.stack([pack(by_part(i["L1_ffn_W2"][e].T), col(i["L1_ffn_b2"][e])) for e in range(16)])
    gu = i["L2_ffn_gate_up_proj"]
    a["up_f2"] = np.stack([ups([gu[e, 0:P].T, gu[e, P:].T]) for e in range(32)])
    a["dn_f2"] = np.stack([pack(by_part(i["L2_ffn_down_proj"][e].T)) for e in range(32)])
    a["up_f3"] = np.stack([ups([i["L3_ffn_w1"][e].T], [i["L3_ffn_b1"][e]]) for e in range(8)])
    a["dn_f3"] = np.stack([pack(by_part(i["L3_ffn_w2"][e].T), col(i["L3_ffn_b2"][e])) for e in range(8)])
    a["wr_f0"] = by_part(i["L0_ffn_w_router"])
    a["wr_f1"] = by_part(i["L1_ffn_Wg"].T)
    a["wr_f2"] = by_part(i["L2_ffn_classifier_weight"].T)
    a["wr_f3"] = by_part(i["L3_ffn_gate_w"].T)
    a["w3_in"] = by_part(i["L3_attn_W_in"])
    a["w3_delta"] = by_part(i["L3_attn_W_delta"])
    a["w3_bc"] = by_part(np.concatenate([i["L3_attn_W_B"], i["L3_attn_W_C"]], 1))
    a["w3_out"] = by_part(i["L3_attn_W_out"])
    return a


def kernel(**inputs):
    import concourse.bacc as bacc
    from concourse.bass_utils import run_bass_kernel_spmd

    nc = bacc.Bacc("TRN2", target_bir_lowering=False, num_devices=1)
    arrays = {f"in_{n}": a for n, a in layouts(inputs).items()}
    dram = {n[3:]: nc.dram_tensor(n, a.shape, mybir.dt.float32, kind="ExternalInput").ap() for n, a in arrays.items()}
    out = nc.dram_tensor("out_0", (D, T), mybir.dt.float32, kind="ExternalOutput").ap()
    build(nc, dram, out)
    r = run_bass_kernel_spmd(nc, [arrays], core_ids=[0])
    return np.ascontiguousarray(np.asarray(r.results[0]["out_0"]).T).reshape(B, N, D)
```

```python
from contextlib import ExitStack

import numpy as np
import concourse.bass as bass
from concourse import mybir

P = 128
D = 256
C = D // P
B = 4
N = 257
T = B * N
PF = 320
EPS = 1e-5
RMS_EPS = 1.1920929e-07
BANK = 512
CHUNKS = [(0, 344), (344, 342), (686, 342)]
CW = 344
NC = len(CHUNKS)
TILES = [128 * j for j in range(8)] + [T - 128]
NT = len(TILES)
SC0, SC1 = N, N - P
SCW = SC0 + SC1
EMIN, EMAX = -8, 128
NEXP = EMAX - EMIN + 1
BIG = 1e30


class Ffn:
    def __init__(self, name, units, mt, gated, act, has_bias):
        self.name, self.units, self.mt, self.gated, self.act, self.has_bias = name, units, mt, gated, act, has_bias
        self.up_mats = 2 if gated else 1
        self.up_w = self.up_mats * C * mt * P
        self.biases = self.up_mats * mt + C if has_bias else 0
        self.up_words = self.up_w + self.biases
        self.dn_w = mt * D
        self.psums = self.up_mats
        self.depth = 4 // self.psums


FFNS = [Ffn("f0", 9, 8, False, "Silu", False), Ffn("f1", 16, 2, True, "Silu", True),
        Ffn("f2", 32, 1, True, "Silu", False), Ffn("f3", 8, 8, False, "Relu", True)]

CONSTS = {}
_at = 0
for _n, _w in (("ident", P), ("mean", P), ("headones", P), ("expo", NEXP), ("expo_r", NEXP), ("causal", SCW), ("hide", SCW),
               ("unpad", 2 * 64), ("block4", 4)):
    CONSTS[_n] = (_at, _at + _w)
    _at += _w
CONST_W = _at


VECS = {}
_at = 0
for _n, _w in (("cls", C), ("tok_gamma", C), ("ln_gamma", C), ("ln_beta", C), ("bO0", C), ("bO1", C), ("alpha", 8),
               ("b_delta", 4), ("A_log", 64), ("D_param", 4), ("gate_b", 8), ("score_b", 40)):
    VECS[_n] = (_at, _at + _w)
    _at += _w
VEC_W = _at
HP = 8
A0_W = 4 * C * P + D + 4
A1_W = 3 * C * P + D + 3
A2_W = 3 * C * P
ARENA_W = 34000


def build(nc, dram, out):
    f32 = mybir.dt.float32
    u32 = mybir.dt.uint32
    ALU = mybir.AluOpType
    ACT = mybir.ActivationFunctionType
    AX = mybir.AxisListType
    ctx = ExitStack()
    with ctx:
        def sb(name, shape):
            return ctx.enter_context(nc.sbuf_tensor(name, shape, f32))

        sems = {}

        def sem(name):
            if name not in sems:
                sems[name] = ctx.enter_context(nc.semaphore(name))
            return sems[name]

        HT = sb("HT", [P, C, T])
        XN = sb("XN", [P, C, T])
        XN2 = sb("XN2", [P, C, T + 2])
        XC = sb("XC", [P, C, T])
        SQ = sb("SQ", [P, C, T])
        consts = sb("consts", [P, CONST_W])
        vecs = sb("vecs", [P, VEC_W])
        watt = [sb(f"watt{s}", [P, A0_W]) for s in range(2)]
        epsc = sb("epsc", [P, 2])
        region = (nc.sbuf_base + 31) // 32 * 32

        def at(name, shape, offset, dtype=f32):
            t = nc.alloc_sbuf_tensor_at(name, [P] + shape, dtype, offset=region + 4 * offset)
            return t, offset + (int(np.prod(shape)) + 7) // 8 * 8

        arena, _ = at("arena", [ARENA_W], 0)
        ps = ctx.enter_context(nc.psum_tensor("ps", [P, 8, BANK], f32))

        class Arena:
            def __init__(self):
                self.at = 0

            def take(self, *shape, rows=P):
                w = int(np.prod(shape))
                v = arena[0:rows, self.at:self.at + w]
                self.at += w
                assert self.at <= ARENA_W, self.at
                if len(shape) == 2:
                    v = v.rearrange("p (a b) -> p a b", b=shape[1])
                elif len(shape) == 3:
                    v = v.rearrange("p (a b c) -> p a b c", b=shape[1], c=shape[2])
                return v

        def const(name):
            a, b = CONSTS[name]
            return consts[:, a:b]

        def vec(name):
            a, b = VECS[name]
            return vecs[:, a:b]

        ident, mean_mat = const("ident"), const("mean")

        def spread(col, w):
            return col.unsqueeze(2).broadcast_to([col.shape[0], col.shape[1], w])

        def over(row, n):
            return row.unsqueeze(1).broadcast_to([row.shape[0], n, row.shape[1]])

        class Norm:
            count = 0

            def __init__(self, src, dst, ready, centred=True, eps=EPS, gamma=None, beta=None):
                self.src, self.dst, self.ready = src, dst, ready
                self.centred, self.eps, self.gamma, self.beta = centred, eps, gamma, beta
                self.base = NC * Norm.count
                self.cbase = NC * Norm.centred_before if centred else None
                Norm.count += 1
                Norm.centred_before += centred
                self.gbase = 2 * NC * Norm.gamma_before
                Norm.gamma_before += gamma is not None

            centred_before = 0
            gamma_before = 0

            def done(self, c=NC - 1):
                return sem("ln_out"), self.base + c + 1

            def pe(self, pe):
                if self.centred:
                    for c, (t0, w) in enumerate(CHUNKS):
                        for s, v in self.ready(c):
                            pe.wait_ge(s, v)
                        for k in range(C):
                            mm = pe.matmul(ps[:, c, 0:w], mean_mat, self.src[:, k, t0:t0 + w], start=(k == 0), stop=(k == C - 1))
                        mm.then_inc(sem("ln_mean"), 1)
                for c, (t0, w) in enumerate(CHUNKS):
                    pe.wait_ge(sem("ln_sq"), self.base + c + 1)
                    for k in range(C):
                        mm = pe.matmul(ps[:, NC + c, 0:w], mean_mat, SQ[:, k, t0:t0 + w], start=(k == 0), stop=(k == C - 1))
                    mm.then_inc(sem("ln_var"), 1)

            def act(self, act):
                for c, (t0, w) in enumerate(CHUNKS):
                    if self.centred:
                        act.wait_ge(sem("ln_cent"), self.cbase + c + 1)
                        x = XC
                    else:
                        for s, v in self.ready(c):
                            act.wait_ge(s, v)
                        x = self.src
                    act.activation(SQ[:, :, t0:t0 + w], x[:, :, t0:t0 + w], ACT.Square).then_inc(sem("ln_sq"), 1)
                for c, (t0, w) in enumerate(CHUNKS):
                    act.wait_ge(sem("ln_var"), self.base + c + 1)
                    act.wait_ge(sem("ln_eps"), 2)
                    eps = epsc[:, 0:1] if self.eps == EPS else epsc[:, 1:2]
                    act.activation(SQ[:, 0, t0:t0 + w], ps[:, NC + c, 0:w], ACT.Sqrt, bias=eps).then_inc(sem("ln_std"), 1)

            def dve(self, dve):
                if self.centred:
                    for c, (t0, w) in enumerate(CHUNKS):
                        dve.wait_ge(sem("ln_mean"), self.cbase + c + 1)
                        dve.tensor_tensor(XC[:, :, t0:t0 + w], self.src[:, :, t0:t0 + w], over(ps[:, c, 0:w], C),
                                          ALU.subtract).then_inc(sem("ln_cent"), 1)
                x = XC if self.centred else self.src
                for c, (t0, w) in enumerate(CHUNKS):
                    n = self.base + c + 1
                    dve.wait_ge(sem("ln_std"), n)
                    dve.reciprocal(SQ[:, 1, t0:t0 + w], SQ[:, 0, t0:t0 + w]).then_inc(sem("ln_rstd"), 1)
                    dve.wait_ge(sem("ln_rstd"), n)
                    last = dve.tensor_tensor(self.dst[:, :, t0:t0 + w], x[:, :, t0:t0 + w], over(SQ[:, 1, t0:t0 + w], C), ALU.mult)
                    if self.gamma is not None:
                        for k in range(C):
                            last.then_inc(sem("ln_scaled"), 1)
                            dve.wait_ge(sem("ln_scaled"), self.gbase + C * c + k + 1)
                            v = self.dst[:, k, t0:t0 + w]
                            if self.beta is None:
                                last = dve.tensor_scalar(v, v, self.gamma[:, k:k + 1], None, ALU.mult)
                            else:
                                last = dve.tensor_scalar(v, v, self.gamma[:, k:k + 1], self.beta[:, k:k + 1], ALU.mult, ALU.add)
                    last.then_inc(sem("ln_out"), 1)

        ar = Arena()
        xt = ar.take(3, B * D)
        wtok = ar.take(3, D)

        def tok_sp(sp):
            sp.dma_start(xt, dram["xt"]).then_inc(sem("tok_in"), 16)
            sp.dma_start(wtok, dram["wtok"]).then_inc(sem("tok_in"), 16)
            sp.dma_start(consts[:, :], dram["consts"]).then_inc(sem("const_in"), 16)
            sp.dma_start(vecs[:, :], dram["vecs"]).then_inc(sem("const_in"), 16)

        def tok_pe(pe):
            pe.wait_ge(sem("tok_in"), 32)
            for b in range(B):
                for d in range(C):
                    for k in range(3):
                        r = min(P, PF - k * P)
                        mm = pe.matmul(ps[:, 2 * b + d, 0:D], wtok[0:r, k, d * P:(d + 1) * P], xt[0:r, k, b * D:(b + 1) * D],
                                       start=(k == 0), stop=(k == 2))
                mm.then_inc(sem("tok_ps"), 1)
            pe.wait_ge(sem("const_in"), 32)

        def cls_columns(dve):
            return dve.tensor_copy(HT[:, :, :].rearrange("p c (b n) -> p c b n", n=N)[:, :, :, 0], spread(vec("cls"), B))

        def tok_dve(dve):
            dve.memset(epsc[:, 0:1], EPS).then_inc(sem("ln_eps"), 1)
            dve.memset(epsc[:, 1:2], RMS_EPS).then_inc(sem("ln_eps"), 1)
            dve.wait_ge(sem("const_in"), 32)
            cls_columns(dve).then_inc(sem("tok_h"), 1)
            for b in range(B):
                dve.wait_ge(sem("tok_ps"), b + 1)
                dve.tensor_copy(HT[:, :, b * N + 1:(b + 1) * N], ps[:, 2 * b:2 * b + 2, 0:D]).then_inc(sem("tok_h"), 1)

        tok_norm = Norm(HT, HT, lambda c: [(sem("tok_h"), B + 1)], gamma=vec("tok_gamma"))

        def tok_cls(dve):
            dve.wait_ge(*tok_norm.done())
            cls_columns(dve).then_inc(sem("h0"), 1)

        n0a = Norm(HT, XN, lambda c: [(sem("h0"), 1)])
        n0b = Norm(XN, XN2, lambda c: [n0a.done(c)], gamma=vec("ln_gamma"), beta=vec("ln_beta"))
        ar = Arena()
        w0 = [w[:, 0:A0_W] for w in watt]
        powt = ar.take(HP, NEXP)
        powr = ar.take(HP, NEXP)
        tab = ar.take(2, NEXP)
        lga = ar.take(4, HP)
        q0, k0, v0, g0 = ([ar.take(N) for _ in range(2)] for _ in range(4))
        q16, kA, kB = ar.take(16, 16), ar.take(8, 16), ar.take(8, 32)
        q32, k32 = ar.take(4, 32), ar.take(4, 32)
        q64, k64 = ar.take(2, 64), ar.take(2, 64)
        q128, k128 = ar.take(P + 1), ar.take(2, P)
        at0 = [ar.take(SCW) for _ in range(2)]
        vt0 = ar.take(2, P)
        og0 = ar.take(N)
        lastp, lastv = ar.take(1), ar.take(1)
        U = 2 * B
        E0 = -EMIN

        def R(e):
            return EMAX - e

        def a0_load(sp, m, s):
            return sp.dma_start(w0[s], m).then_inc(sem(f"a0_w{s}"), 16)

        def a0_sp(sp):
            for s in range(2):
                a0_load(sp, dram["w_a0"][s], s)
            with sp.Fori(1, HP // 2) as mm:
                for s in range(2):
                    sp.wait_ge(sem("a0_y"), mm * U + (s - 1) * B)
                    a0_load(sp, dram["w_a0"][bass.ds(2 * mm + s, 1), :, :].rearrange("a p w -> p (a w)"), s)

        def a0_pe(pe):
            n0a.pe(pe)
            n0b.pe(pe)
            pe.wait_ge(*n0b.done())
            with pe.Fori(0, HP // 2) as mm:
                base = mm * U

                def project(j):
                    s, b = j // B, j % B
                    if b == 0:
                        pe.wait_ge(sem(f"a0_w{s}"), 16 * mm + 16)
                    for i in range(4):
                        for k in range(C):
                            mmul = pe.matmul(ps[:, i, 0:N], w0[s][:, (i * C + k) * P:(i * C + k + 1) * P],
                                             XN2[:, k, b * N:(b + 1) * N], start=(k == 0), stop=(k == C - 1))
                        if i % 2:
                            mmul.then_inc(sem("a0_proj"), 1)

                def values(j):
                    pe.wait_ge(sem("a0_vg"), base + j + 1)
                    for i in range(2):
                        pe.transpose(ps[:, 7, i * P:(i + 1) * P], v0[j % 2][:, i * P:(i + 1) * P], ident)
                    pe.wait_ge(sem("a0_qk256"), base + j + 1)
                    pe.matmul(ps[:, 7, 2 * P:2 * P + 1], const("headones"), lastp, start=True, stop=True).then_inc(sem("a0_vt"), 1)

                def scores(j):
                    pe.wait_ge(sem("a0_prep"), base + j + 1)
                    pe.wait_ge(sem("a0_prepg"), base + j + 1)
                    pe.wait_ge(sem("a0_added"), base + j + 1)
                    pe.nop(nofuse=True)
                    for h in range(2):
                        rows = slice(64 * h, 64 * h + 64)

                        def block(r0, r1, c0, lhs, rhs):
                            return pe.matmul(ps[r0:r1, 4 + h, c0:c0 + rhs.shape[1]], lhs, rhs, start=True, stop=True)

                        for i in range(2):
                            cb = i * SC0
                            for n in range(4):
                                g = 4 * i + n
                                block(32 * n, 32 * n + 16, cb + 32 * n, kA[rows, g, :], q16[rows, 2 * g, :])
                                block(32 * n, 32 * n + 32, cb + 32 * n + 16, kB[rows, g, :], q16[rows, 2 * g + 1, :])
                            for n in range(2):
                                g = 2 * i + n
                                block(64 * n, 64 * n + 32, cb + 64 * n + 32, k32[rows, g, :], q32[rows, g, :])
                            block(0, 64, cb + 64, k64[rows, i, :], q64[rows, i, :])
                        block(0, P, P, k128[rows, 0, :], q128[rows, :])
                        block(0, P, SC0 + P, k128[rows, 1, :], q0[j % 2][rows, 2 * P:N]).then_inc(sem("a0_s"), 1)

                def mix(j):
                    pe.wait_ge(sem("a0_vsb"), base + j + 1)
                    for h in range(2):
                        pe.wait_ge(sem("a0_at"), 2 * base + 2 * j + h + 1)
                        o = ps[64 * h:64 * h + 64, 6, :]
                        pe.matmul(o[:, 0:N], vt0[:, 0, 64 * h:64 * h + 64], at0[h][:, 0:SC0], start=True, stop=False)
                        mmul = pe.matmul(o[:, P:N], vt0[:, 1, 64 * h:64 * h + 64], at0[h][:, SC0:SCW], start=False, stop=True)
                    mmul.then_inc(sem("a0_o"), 1)

                def output(j):
                    pe.wait_ge(sem("a0_og"), base + j + 1)
                    for d in range(C):
                        mmul = pe.matmul(ps[:, 4 + d, 0:N], w0[j // B][:, 1024 + d * P:1024 + (d + 1) * P], og0, start=True, stop=True)
                    mmul.then_inc(sem("a0_y"), 1)

                project(0)
                values(0)
                for j in range(U):
                    scores(j)
                    if j + 1 < U:
                        project(j + 1)
                    mix(j)
                    if j + 1 < U:
                        values(j + 1)
                    output(j)

        def a0_act(act):
            n0a.act(act)
            n0b.act(act)
            act.wait_ge(sem("a0_lg"), 2)
            act.activation(lga[:, 1, :], lga[:, 0, :], ACT.Exp).then_inc(sem("a0_lga"), 1)
            act.wait_ge(sem("a0_lga"), 1)
            act.activation(lga[:, 2, :], lga[:, 1, :], ACT.Ln, bias=1.0).then_inc(sem("a0_lga"), 1)
            act.wait_ge(sem("a0_lg"), 4)
            for m in range(HP):
                act.activation(powt[:, m, :], const("expo")[:, 0:NEXP], ACT.Exp, scale=lga[:, 3, m:m + 1])
                last = act.activation(powr[:, m, :], const("expo_r"), ACT.Exp, scale=lga[:, 3, m:m + 1])
                last.then_inc(sem("a0_pow"), 1)
            with act.Fori(0, HP // 2) as mm:
                base = mm * U
                for j in range(U):
                    w = w0[j // B]
                    act.wait_ge(sem("a0_proj"), 2 * base + 2 * j + 1)
                    act.activation(q0[j % 2], ps[:, 0, 0:N], ACT.Identity, bias=w[:, 1280:1281])
                    act.activation(k0[j % 2], ps[:, 1, 0:N], ACT.Identity, bias=w[:, 1281:1282]).then_inc(sem("a0_qk"), 1)
                    act.wait_ge(sem("a0_proj"), 2 * base + 2 * j + 2)
                    act.activation(v0[j % 2], ps[:, 2, 0:N], ACT.Identity, bias=w[:, 1282:1283])
                    act.activation(g0[j % 2], ps[:, 3, 0:N], ACT.Silu, bias=w[:, 1283:1284]).then_inc(sem("a0_vg"), 1)

        def a0_dve(dve):
            n0a.dve(dve)
            n0b.dve(dve)
            for i, op in enumerate((ALU.mult, ALU.min)):
                if i == 0:
                    dve.tensor_scalar(lga[:, 0, :], vec("alpha"), -1.0, None, op).then_inc(sem("a0_lg"), 1)
                else:
                    dve.wait_ge(sem("a0_lg"), 1)
                    dve.tensor_tensor(lga[:, 0, :], lga[:, 0, :], vec("alpha"), op).then_inc(sem("a0_lg"), 1)
            dve.tensor_scalar(lga[:, 3, :], vec("alpha"), 0.0, None, ALU.min).then_inc(sem("a0_lg"), 1)
            dve.wait_ge(sem("a0_lga"), 2)
            dve.wait_ge(sem("a0_lg"), 3)
            dve.tensor_tensor(lga[:, 3, :], lga[:, 3, :], lga[:, 2, :], ALU.subtract).then_inc(sem("a0_lg"), 1)
            dve.wait_ge(*n0b.done())
            for c in range(C):
                dve.scalar_tensor_tensor(HT[:, c, :], XN[:, c, :], vec("bO0")[:, c:c + 1], HT[:, c, :], ALU.add, ALU.add).then_inc(sem("a0_res"), 1)
            for h in range(2):
                dve.memset(at0[h], 0.0).then_inc(sem("a0_zero"), 1)
            dve.memset(ps[:, 4:6, 0:SCW], 0.0).then_inc(sem("a0_added"), 1)
            dve.wait_ge(sem("a0_zero"), 2)
            dve.wait_ge(sem("a0_res"), C)
            dve.wait_ge(sem("a0_pow"), HP)
            with dve.Fori(0, HP // 2) as mm:
                base = mm * U

                def prep(j):
                    s, b = j // B, j % B
                    up, down = tab[:, 0, :], tab[:, 1, :]
                    if b == 0:
                        m = 2 * mm + s
                        dve.tensor_copy(up, powt[:, bass.ds(m, 1), :].rearrange("p a e -> p (a e)")).then_inc(sem("a0_tab"), 1)
                        dve.tensor_copy(down, powr[:, bass.ds(m, 1), :].rearrange("p a e -> p (a e)")).then_inc(sem("a0_tab"), 1)
                        dve.wait_ge(sem("a0_tab"), 4 * mm + 2 * s + 2)
                    q, k = q0[j % 2], k0[j % 2]
                    dve.wait_ge(sem("a0_qk"), base + j + 1)
                    dve.tensor_tensor(lastp, q[:, N - 1:N], k[:, N - 1:N], ALU.mult).then_inc(sem("a0_qk256"), 1)

                    def view(x, n):
                        return x[:, 0:2 * P].rearrange("p (a b) -> p a b", b=n)

                    dve.tensor_tensor(q16, view(q, 16), over(up[:, E0 - 8:E0 + 8], 16), ALU.mult)
                    dve.tensor_tensor(kA, view(k, 32)[:, :, 0:16], over(down[:, R(8):R(8) + 16], 8), ALU.mult)
                    dve.tensor_tensor(kB, view(k, 32), over(down[:, R(24):R(24) + 32], 8), ALU.mult)
                    dve.tensor_tensor(q32, view(q, 64)[:, :, 32:64], over(up[:, E0:E0 + 32], 4), ALU.mult)
                    dve.tensor_tensor(k32, view(k, 64)[:, :, 0:32], over(down[:, R(32):R(32) + 32], 4), ALU.mult).then_inc(sem("a0_prep"), 1)

                def tokens(j):
                    dve.wait_ge(sem("a0_vt"), base + j + 1)
                    dve.tensor_copy(vt0, ps[:, 7, 0:2 * P].rearrange("p (a b) -> p a b", b=P))
                    dve.tensor_tensor(lastv, ps[:, 7, 2 * P:2 * P + 1], v0[j % 2][:, N - 1:N], ALU.mult).then_inc(sem("a0_vsb"), 1)

                def mask(j):
                    for h in range(2):
                        dve.wait_ge(sem("a0_s"), 2 * base + 2 * j + h + 1)
                        dve.nop(nofuse=True)
                        dve.copy_predicated(at0[h], const("causal").bitcast(u32), ps[:, 4 + h, 0:SCW]).then_inc(sem("a0_at"), 1)

                def gate(j):
                    dve.wait_ge(sem("a0_o"), base + j + 1)
                    dve.wait_ge(sem("a0_vg"), base + j + 1)
                    dve.wait_ge(sem("a0_vsb"), base + j + 1)
                    g = g0[j % 2]
                    dve.tensor_copy(og0, ps[:, 6, 0:N]).then_inc(sem("a0_oc"), 1)
                    dve.wait_ge(sem("a0_oc"), 2 * base + 2 * j + 1)
                    dve.tensor_tensor(og0[:, N - 1:N], og0[:, N - 1:N], lastv, ALU.add).then_inc(sem("a0_oc"), 1)
                    dve.wait_ge(sem("a0_oc"), 2 * base + 2 * j + 2)
                    dve.tensor_tensor(og0, og0, g, ALU.mult).then_inc(sem("a0_og"), 1)

                def add(j):
                    b = j % B
                    h = HT[:, :, b * N:(b + 1) * N]
                    dve.wait_ge(sem("a0_y"), base + j + 1)
                    dve.tensor_tensor(h, h, ps[:, 4:6, 0:N], ALU.add).then_inc(sem("a0_added"), 1)

                prep(0)
                tokens(0)
                for j in range(U):
                    mask(j)
                    if j + 1 < U:
                        prep(j + 1)
                    gate(j)
                    if j + 1 < U:
                        tokens(j + 1)
                    add(j)

        def a0_pool(pool):
            with pool.Fori(0, HP // 2) as mm:
                base = mm * U
                for j in range(U):
                    if j:
                        pool.wait_ge(sem("a0_s"), 2 * base + 2 * j)
                    pool.wait_ge(sem("a0_tab"), 4 * mm + 2 * (j // B) + 2)
                    pool.wait_ge(sem("a0_qk"), base + j + 1)
                    q, k = q0[j % 2], k0[j % 2]
                    up, down = tab[:, 0, :], tab[:, 1, :]
                    pool.tensor_tensor(q64, q[:, 0:2 * P].rearrange("p (a b) -> p a b", b=P)[:, :, 64:P], over(up[:, E0:E0 + 64], 2), ALU.mult)
                    pool.tensor_tensor(k64, k[:, 0:2 * P].rearrange("p (a b) -> p a b", b=P)[:, :, 0:64], over(down[:, R(64):R(64) + 64], 2), ALU.mult)
                    pool.tensor_tensor(q128, q[:, P:N], up[:, E0:E0 + P + 1], ALU.mult)
                    pool.tensor_tensor(k128, k[:, 0:2 * P].rearrange("p (a b) -> p a b", b=P), over(down[:, R(P):R(P) + P], 2), ALU.mult)\
                        .then_inc(sem("a0_prepg"), 1)

        h_a0 = [(sem("a0_added"), HP * B + 1)]

        fr = mybir.dt.float32r
        at_ = 0

        def take(name, shape, dtype=f32):
            nonlocal at_
            t, at_ = at(name, shape, at_, dtype)
            return t

        wu = [[take(f"wu{s}{x}", [2 * 8 * P], fr) for x in ("hi", "lo")] for s in range(2)]
        wd = [[take(f"wd{s}{x}", [8 * D], fr) for x in ("hi", "lo")] for s in range(2)]
        xs = [take(f"xs{x}", [C, T], fr) for x in ("hi", "lo")]
        hid = [[take(f"hid{u}{x}", [8, CW], fr) for x in ("hi", "lo")] for u in range(2)]
        raw_h = take("raw_h", [4, CW])
        sig = take("sig", [2, CW])
        scaled = [take(f"scaled{u}", [C, CW]) for u in range(2)]
        bias = [take(f"bias{s}", [16]) for s in range(2)]
        cwt = take("cwt", [T])
        wr = take("wr", [C, 40])
        lg, prob, cw = take("lg", [NT, 40]), take("prob", [NT, 40]), take("cw", [NT, 40])
        vals, repl = take("vals", [NT, 48]), take("repl", [NT, 48])
        top8, red = take("top8", [NT, 8]), take("red", [4, NT])
        grp, grpr = take("grp", [NT, 10]), take("grpr", [NT, 10])
        assert region + 4 * at_ <= nc.sbuf_usable_end
        raw_up = XN2[:, :, :].rearrange("p c t -> p (c t)")
        raw_dn = XC[:, :, :].rearrange("p c t -> p (c t)")
        cwb = [w[:, 0:T] for w in watt]

        def mm3(pe, out, w, x, first, last):
            for n, (i, j) in enumerate(((0, 0), (0, 1), (1, 0))):
                mm = pe.matmul(out, w[i], x[j], start=(first and n == 0), stop=(last and n == 2))
            return mm

        class Units:
            def __init__(self, f, i, s, c):
                self.f, self.i, self.s, self.c = f, i, s, c
                self.n = 6 * i + 3 * s + c
                self.par = (3 * s + c) % 2

            def expert(self):
                return 2 * self.i + self.s

            def last(self):
                return isinstance(self.i, int) and 2 * self.i + self.s == self.f.units - 1

            def next(self):
                if self.c + 1 < NC:
                    return Units(self.f, self.i, self.s, self.c + 1)
                return Units(self.f, self.i + self.s, 1 - self.s, 0)

            def tile(self, m):
                return self.n * self.f.mt + m, ((3 * self.s + self.c) * self.f.mt + m) % self.f.depth

        def sweep(eng, f, hidden, outputs):
            loops = (f.units - 1) // 2
            hidden(Units(f, 0, 0, 0))
            with eng.Fori(0, loops) as i:
                for s in range(2):
                    for c in range(NC):
                        u = Units(f, i, s, c)
                        hidden(u.next())
                        outputs(u)
            rest = f.units - 2 * loops
            for s in range(rest):
                for c in range(NC):
                    u = Units(f, loops, s, c)
                    if s < rest - 1 or c < NC - 1:
                        hidden(u.next())
                    outputs(u)

        class Layer:
            def __init__(self, f, ready, src=None):
                self.f, self.p = f, f.name
                self.norm = Norm(HT, XN, ready)
                self.rows = {"f0": 9, "f1": 16, "f2": 33, "f3": 8}[f.name]
                self.experts = {"f0": 8, "f1": 16, "f2": 40, "f3": 8}[f.name]
                self.cwd = nc.dram_tensor(f"cw_{f.name}", (self.rows, T), f32, kind="Internal").ap()
                self.extra = 1 if f.name == "f2" else 0
                self.index = FFNS.index(f)
                Layer.all.append(self)

            all = []
            steps = 0

            def sem(self, n):
                return sem(f"ff_{n}")

            def counts(self, n):
                u = self.f.units
                tiles, units = NC * u * self.f.mt, NC * (u + self.extra)
                return {"upraw": 16 * u, "dnraw": 16 * u, "cw0": 16 * ((u + 1) // 2 + self.extra), "cw1": 16 * (u // 2),
                        "wuhi": u, "wdhi": u, "wu": u, "wd": u, "hps": tiles, "sig": tiles * self.f.gated,
                        "got": tiles, "hhi": tiles, "hid": tiles, "out": NC * u,
                        "taken": units, "added": units, "xs": 2}[n]

            def at(self, n, v):
                return self.sem(n), sum(x.counts(n) for x in Layer.all[:self.index]) + v

            def once(self, n, v):
                each = {"wr": 16, "logits": 1, "shifted": 1, "prob": 1, "cw": 1, "cwps": 1, "cwt": 3, "cwd": 16}[n]
                before = self.index
                if n == "shifted":
                    before = self.index // 2
                return sem(f"route_{n}"), each * before + v

            def done(self):
                return [self.at("added", 2 + NC * (self.f.units + self.extra))]

            def load_up(self, sp, src):
                sp.dma_start(raw_up[:, 0:self.f.up_words], src).then_inc(self.sem("upraw"), 16)

            def load_dn(self, sp, src):
                sp.dma_start(raw_dn[:, 0:self.f.dn_w], src).then_inc(self.sem("dnraw"), 16)

            def load_cw(self, sp, src, s):
                sp.dma_start(cwb[s], src.broadcast_to([P, T])).then_inc(self.sem(f"cw{s}"), 16)

            def sp(self, sp):
                for sm, v in self.norm.ready(0):
                    sp.wait_ge(sm, v)
                sp.dma_start(wr[:, :, 0:self.experts], dram["wr_" + self.p]).then_inc(sem("route_wr"), 16)
                self.load_up(sp, dram["up_" + self.p][0])
                sp.wait_ge(*self.norm.done())
                self.load_dn(sp, dram["dn_" + self.p][0])
                sp.wait_ge(*self.once("cwt", 3))
                sp.dma_start(self.cwd, cwt[0:self.rows, :]).then_inc(sem("route_cwd"), 16)
                sp.wait_ge(*self.once("cwd", 16))
                self.load_cw(sp, self.cwd[0:1, :], 0)

                def more(g, i, s):
                    sp.wait_ge(*self.at("wu", g))
                    self.load_up(sp, dram["up_" + self.p][bass.ds(g, 1), :, :].rearrange("a p w -> p (a w)"))
                    sp.wait_ge(*self.at("wd", g))
                    self.load_dn(sp, dram["dn_" + self.p][bass.ds(g, 1), :, :].rearrange("a p w -> p (a w)"))
                    if not (isinstance(g, int) and g == 1):
                        sp.wait_ge(*self.at("taken", 2 + 6 * i + 3 * s - 3))
                    self.load_cw(sp, self.cwd[bass.ds(g, 1), :], s)

                more(1, 0, 1)
                pairs = self.f.units // 2
                with sp.Fori(1, pairs) as i:
                    for s in range(2):
                        more(2 * i + s, i, s)
                if self.f.units % 2:
                    more(2 * pairs, pairs, 0)
                if self.extra:
                    sp.wait_ge(*self.at("taken", 2 + NC * (self.f.units - 1)))
                    self.load_cw(sp, self.cwd[self.f.units:self.f.units + 1, :], 0)

            def pe(self, pe):
                f = self.f
                self.norm.pe(pe)
                pe.wait_ge(*self.norm.done())
                pe.wait_ge(*self.once("wr", 16))
                for j, t0 in enumerate(TILES):
                    for k in range(C):
                        mm = pe.matmul(ps[:, 0, j * 40:j * 40 + self.experts], XN[:, k, t0:t0 + P], wr[:, k, 0:self.experts],
                                       start=(k == 0), stop=(k == C - 1))
                mm.then_inc(sem("route_logits"), 1)
                pe.wait_ge(*self.once("cw", 1))
                for j in range(NT):
                    mm = pe.transpose(ps[0:self.rows, 1 + j // 4, (j % 4) * P:(j % 4 + 1) * P], cw[:, j, 0:self.rows], ident)
                mm.then_inc(sem("route_cwps"), 1)
                pe.wait_ge(*self.once("cwt", 3))

                pe.wait_ge(*self.at("xs", 2))

                def hidden(u):
                    if u.c == 0:
                        pe.wait_ge(*self.at("wu", u.expert() + 1))
                    t0, w = CHUNKS[u.c]
                    for m in range(f.mt):
                        t, slot = u.tile(m)
                        pe.wait_ge(*self.at("got", 4 - f.depth + t + 1))
                        for a in range(f.up_mats):
                            for k in range(C):
                                col = ((a * C + k) * f.mt + m) * P
                                mm = mm3(pe, ps[:, slot * f.psums + a, 0:w], [x[:, col:col + P] for x in wu[u.s]],
                                         [x[:, k, t0:t0 + w] for x in xs], k == 0, k == C - 1)
                        mm.then_inc(self.sem("hps"), 1)

                def outputs(u):
                    if u.c == 0:
                        pe.wait_ge(*self.at("wd", u.expert() + 1))
                    w = CHUNKS[u.c][1]
                    pe.wait_ge(*self.at("taken", u.n + 1))
                    pe.wait_ge(*self.at("hid", 4 + (u.n + 1) * f.mt))
                    for d in range(C):
                        for m in range(f.mt):
                            col = m * D + d * P
                            mm = mm3(pe, ps[:, 4 + 2 * u.par + d, 0:w], [x[:, col:col + P] for x in wd[u.s]],
                                     [x[:, m, 0:w] for x in hid[u.par]], m == 0, m == f.mt - 1)
                    mm.then_inc(self.sem("out"), 1)

                sweep(pe, f, hidden, outputs)

            def split_act(self, act, g, c, spare=None):
                s, raw, words, name = (g[1], raw_up, self.f.up_w, "wu") if c == 0 else (g[1], raw_dn, self.f.dn_w, "wd")
                g = g[0]
                act.wait_ge(*self.at("upraw" if c == 0 else "dnraw", 16 * g + 16))
                if spare is not None:
                    act.wait_ge(*spare)
                act.copy((wu if c == 0 else wd)[s][0][:, 0:words], raw[:, 0:words]).then_inc(self.sem(name + "hi"), 1)

            def split_dve(self, dve, g, c):
                s, raw, words, name = (g[1], raw_up, self.f.up_w, "wu") if c == 0 else (g[1], raw_dn, self.f.dn_w, "wd")
                g = g[0]
                dve.wait_ge(*self.at(name + "hi", g + 1))
                hi, lo = (wu if c == 0 else wd)[s]
                if c == 0 and self.f.biases:
                    dve.tensor_copy(bias[s][:, 0:self.f.biases], raw[:, words:words + self.f.biases])
                dve.tensor_tensor(lo[:, 0:words], raw[:, 0:words], hi[:, 0:words].bitcast(f32), ALU.subtract).then_inc(self.sem(name), 1)

            def act(self, act):
                f = self.f
                self.norm.act(act)
                self.route_act(act)
                act.wait_ge(*self.norm.done())
                act.copy(xs[0][:, :, :], XN[:, :, :]).then_inc(self.sem("xs"), 1)
                self.split_act(act, (0, 0), 0)
                self.split_act(act, (0, 0), 1)
                if self.index == 0:
                    act.sem_inc(self.sem("got"), 4)
                func = ACT.Silu if f.act == "Silu" else ACT.Relu

                def hidden(u):
                    w = CHUNKS[u.c][1]
                    if u.c == 0 and f.biases:
                        act.wait_ge(*self.at("wu", u.expert() + 1))
                    for m in range(f.mt):
                        t, slot = u.tile(m)
                        act.wait_ge(*self.at("hps", t + 1))
                        b = bias[u.s][:, m:m + 1] if f.has_bias else 0.0
                        if f.gated:
                            act.activation(sig[:, slot, 0:w], ps[:, slot * 2, 0:w], func, bias=b).then_inc(self.sem("sig"), 1)
                        else:
                            act.wait_ge(*self.at("hid", t + 1))
                            act.activation(raw_h[:, slot, 0:w], ps[:, slot, 0:w], func, bias=b).then_inc(self.sem("got"), 1)

                def ahead(u):
                    if u.c < 2 and not u.last():
                        self.split_act(act, (u.expert() + 1, 1 - u.s), u.c, self.at("taken", 2 + NC * u.expert()))

                sweep(act, f, hidden, ahead)

            def dve(self, dve):
                f = self.f
                self.norm.dve(dve)
                self.route_dve(dve)
                dve.wait_ge(*self.once("cwps", 1))
                for n in range(2):
                    dve.tensor_copy(cwt[0:self.rows, 4 * P * n:4 * P * (n + 1)], ps[0:self.rows, 1 + n, 0:4 * P]).then_inc(sem("route_cwt"), 1)
                dve.tensor_copy(cwt[0:self.rows, 8 * P:T], ps[0:self.rows, 3, P - (T - 8 * P):P]).then_inc(sem("route_cwt"), 1)
                dve.wait_ge(*self.at("xs", 1))
                dve.tensor_tensor(xs[1][:, :, :], XN[:, :, :], xs[0][:, :, :].bitcast(f32), ALU.subtract).then_inc(self.sem("xs"), 1)
                self.split_dve(dve, (0, 0), 0)
                self.split_dve(dve, (0, 0), 1)
                if self.index == 0:
                    dve.sem_inc(self.sem("taken"), 2)
                    dve.sem_inc(self.sem("hid"), 4)

                def hidden(u):
                    w = CHUNKS[u.c][1]
                    for m in range(f.mt):
                        t, slot = u.tile(m)
                        if f.gated:
                            dve.wait_ge(*self.at("sig", t + 1))
                            x = ps[:, slot * 2 + 1, 0:w]
                            raw = raw_h[:, slot, 0:w]
                            if f.has_bias:
                                ins = dve.scalar_tensor_tensor(raw, x, bias[u.s][:, f.mt + m:f.mt + m + 1], sig[:, slot, 0:w], ALU.add, ALU.mult)
                            else:
                                ins = dve.tensor_tensor(raw, x, sig[:, slot, 0:w], ALU.mult)
                            ins.then_inc(self.sem("got"), 1)
                        raw = raw_h[:, slot, 0:w]
                        hi, lo = (x[:, m, 0:w] for x in hid[u.par])
                        dve.wait_ge(*self.at("got", 4 + t + 1))
                        dve.tensor_copy(hi, raw).then_inc(self.sem("hhi"), 1)
                        dve.wait_ge(*self.at("hhi", t + 1))
                        dve.tensor_tensor(lo, raw, hi.bitcast(f32), ALU.subtract).then_inc(self.sem("hid"), 1)

                def outputs(u):
                    t0, w = CHUNKS[u.c]
                    if u.c == 0:
                        dve.wait_ge(*self.at(f"cw{u.s}", 16 * u.i + 16))
                    dve.wait_ge(*self.at("added", u.n + 1))
                    dve.wait_ge(*self.at("out", u.n + 1))
                    o, src, k = scaled[u.par], ps[:, 4 + 2 * u.par:6 + 2 * u.par, 0:w], cwb[u.s][:, t0:t0 + w]
                    if f.has_bias:
                        for d in range(C):
                            b = bias[u.s][:, f.up_mats * f.mt + d:f.up_mats * f.mt + d + 1]
                            ins = dve.scalar_tensor_tensor(o[:, d, 0:w], src[:, d, :], b, k, ALU.add, ALU.mult)
                    else:
                        ins = dve.tensor_tensor(o[:, :, 0:w], src, over(k, C), ALU.mult)
                    ins.then_inc(self.sem("taken"), 1)
                    if u.c < 2 and not u.last():
                        self.split_dve(dve, (u.expert() + 1, 1 - u.s), u.c)

                sweep(dve, f, hidden, outputs)
                if self.extra:
                    dve.wait_ge(*self.at("cw0", 16 * (f.units // 2) + 16))
                    for c, (t0, w) in enumerate(CHUNKS):
                        u = NC * f.units + c
                        dve.wait_ge(*self.at("added", u + 1))
                        dve.tensor_tensor(scaled[u % 2][:, :, 0:w], XN[:, :, t0:t0 + w], over(cwb[0][:, t0:t0 + w], C), ALU.mult)\
                            .then_inc(self.sem("taken"), 1)

            def pool(self, pool):
                if self.index == 0:
                    pool.sem_inc(self.sem("added"), 2)

                def outputs(u):
                    t0, w = CHUNKS[u.c]
                    pool.wait_ge(*self.at("added", u.n + 2))
                    pool.wait_ge(*self.at("taken", u.n + 3))
                    h = HT[:, :, t0:t0 + w]
                    pool.tensor_tensor(h, h, scaled[u.par][:, :, 0:w], ALU.add).then_inc(self.sem("added"), 1)

                sweep(pool, self.f, lambda u: None, outputs)
                for c in range(NC * self.extra):
                    outputs(Units(self.f, self.f.units // 2, 0, c))

            def step(self, dve, ins):
                Layer.steps += 1
                ins.then_inc(sem("route_step"), 1)
                dve.wait_ge(sem("route_step"), Layer.steps)

            def top(self, dve, k, e, v, r):
                s = 8 - k
                for n in range(s):
                    self.step(dve, dve.memset(v[:, :, e + n:e + n + 1], -2e38 - n * 1e37))
                for j in range(NT):
                    ins = dve.max(top8[:, j, :], v[:, j, 0:e + s])
                self.step(dve, ins)
                self.step(dve, dve.tensor_copy(top8[:, :, k:8], v[:, :, e:e + s]))
                for j in range(NT):
                    ins = dve.match_replace(r[:, j, 0:e + s], top8[:, j, :], v[:, j, 0:e + s], 3e38)
                self.step(dve, ins)
                self.step(dve, dve.tensor_tensor(r[:, :, 0:e], r[:, :, 0:e], v[:, :, 0:e], ALU.not_equal))

            def normalise(self, dve, x, e):
                self.step(dve, dve.tensor_reduce(red[:, 1, :], x, AX.X, ALU.add))
                self.step(dve, dve.reciprocal(red[:, 2, :], red[:, 1, :]))
                self.step(dve, dve.tensor_tensor(x, x, spread(red[:, 2, :], e), ALU.mult))

            def route_act(self, act):
                e = self.experts
                if self.p in ("f0", "f2"):
                    act.wait_ge(*self.once("shifted", 1))
                    act.activation(prob[:, :, 0:e], lg[:, :, 0:e], ACT.Exp).then_inc(sem("route_prob"), 1)
                if self.p == "f1":
                    act.wait_ge(*self.once("logits", 1))
                    act.activation(prob[:, :, 0:e], ps[:, 0, 0:NT * 40].rearrange("p (a b) -> p a b", b=40)[:, :, 0:e], ACT.Sigmoid)\
                        .then_inc(sem("route_prob"), 1)

            def route_dve(self, dve):
                e, st = self.experts, self.step
                logits = ps[:, 0, 0:NT * 40].rearrange("p (a b) -> p a b", b=40)[:, :, 0:e]
                pr, v, r, x = prob[:, :, 0:e], vals, repl, cw
                dve.wait_ge(*self.once("logits", 1))
                if self.p in ("f0", "f2"):
                    st(dve, dve.tensor_reduce(red[:, 0, :], logits, AX.X, ALU.max))
                    dve.tensor_tensor(lg[:, :, 0:e], logits, spread(red[:, 0, :], e), ALU.subtract).then_inc(sem("route_shifted"), 1)
                if self.p != "f3":
                    dve.wait_ge(*self.once("prob", 1))
                if self.p == "f0":
                    self.normalise(dve, pr, e)
                    st(dve, dve.tensor_copy(v[:, :, 0:e], pr))
                    self.top(dve, 2, e, v, r)
                    st(dve, dve.memset(x[:, :, 0:1], 1.0))
                    st(dve, dve.tensor_tensor(x[:, :, 1:e + 1], pr, r[:, :, 0:e], ALU.mult))
                    self.normalise(dve, x[:, :, 1:e + 1], e)
                    last = dve.tensor_copy(red[:, 3, :], red[:, 2, :])
                if self.p == "f1":
                    st(dve, dve.tensor_reduce(grp[:, :, 0:4], pr.rearrange("p a (g b) -> p a g b", b=4), AX.X, ALU.max))
                    for n in range(4):
                        st(dve, dve.memset(grp[:, :, 4 + n:5 + n], -1e38 - n * 1e37))
                    self.top_groups(dve)
                    g4 = grpr[:, :, 0:4].unsqueeze(3).broadcast_to([P, NT, 4, 4])
                    v4 = v[:, :, 0:e].rearrange("p a (g b) -> p a g b", b=4)
                    st(dve, dve.tensor_tensor(v4, pr.rearrange("p a (g b) -> p a g b", b=4), g4, ALU.mult))
                    st(dve, dve.tensor_scalar(grpr[:, :, 0:4], grpr[:, :, 0:4], -1.0, BIG, ALU.add, ALU.mult))
                    st(dve, dve.tensor_tensor(v4, v4, g4, ALU.add))
                    self.top(dve, 4, e, v, r)
                    st(dve, dve.tensor_tensor(x[:, :, 0:e], pr, r[:, :, 0:e], ALU.mult))
                    self.normalise(dve, x[:, :, 0:e], e)
                    last = dve.tensor_scalar(x[:, :, 0:e], x[:, :, 0:e], 2.5, None, ALU.mult)
                if self.p == "f2":
                    self.normalise(dve, pr, e)
                    st(dve, dve.tensor_tensor(v[:, :, 0:e], pr, over(vec("score_b"), NT), ALU.add))
                    self.top(dve, 6, e, v, r)
                    st(dve, dve.scalar_tensor_tensor(x[:, :, 0:e], pr, 2.5, r[:, :, 0:e], ALU.mult, ALU.mult))
                    st(dve, dve.tensor_reduce(red[:, 0, :], x[:, :, 32:40], AX.X, ALU.add))
                    last = dve.tensor_copy(x[:, :, 32:33], red[:, 0, :].unsqueeze(2))
                if self.p == "f3":
                    st(dve, dve.tensor_tensor(v[:, :, 0:e], logits, over(vec("gate_b"), NT), ALU.add))
                    self.top(dve, 1, e, v, r)
                    last = dve.tensor_copy(x[:, :, 0:e], r[:, :, 0:e])
                last.then_inc(sem("route_cw"), 1)

            def top_groups(self, dve):
                for n in range(2):
                    self.step(dve, dve.memset(grp[:, :, 8 + n:9 + n], -2e38 - n * 1e37))
                for j in range(NT):
                    ins = dve.max(top8[:, j, :], grp[:, j, :])
                self.step(dve, ins)
                self.step(dve, dve.tensor_copy(top8[:, :, 2:8], grp[:, :, 4:10]))
                for j in range(NT):
                    ins = dve.match_replace(grpr[:, j, :], top8[:, j, :], grp[:, j, :], 3e38)
                self.step(dve, ins)
                self.step(dve, dve.tensor_tensor(grpr[:, :, 0:4], grpr[:, :, 0:4], grp[:, :, 0:4], ALU.not_equal))

        f0 = Layer(FFNS[0], lambda c: h_a0)
        h_f0 = f0.done()

        def f0_sp(sp):
            f0.sp(sp)

        def f0_pe(pe):
            f0.pe(pe)

        def f0_act(act):
            f0.act(act)

        def f0_dve(dve):
            f0.dve(dve)

        def f0_pool(pool):
            f0.pool(pool)

        n1a = Norm(HT, XN, lambda c: h_f0)
        n1b = Norm(XN, XN2, lambda c: [n1a.done(c)], centred=False, eps=RMS_EPS)
        ar = Arena()
        w1 = [w[:, 0:A1_W] for w in watt]
        q1, k1, v1 = ([ar.take(N) for _ in range(2)] for _ in range(3))
        sm1 = [ar.take(SCW) for _ in range(2)]
        nmax1 = ar.take(2, 2)
        sum1, rs1 = ar.take(2, 2), ar.take(2, 2)
        at1 = [ar.take(SCW) for _ in range(2)]
        vs1 = ar.take(2, P)
        og1 = ar.take(N)

        def a1_sp(sp):
            sp.wait_ge(*h_f0[0])
            for s in range(2):
                sp.dma_start(w1[s], dram["w_a1"][s]).then_inc(sem(f"a1_w{s}"), 16)
            with sp.Fori(1, HP // 2) as mm:
                for s in range(2):
                    sp.wait_ge(sem("a1_y"), mm * U + (s - 1) * B)
                    sp.dma_start(w1[s], dram["w_a1"][bass.ds(2 * mm + s, 1), :, :].rearrange("a p w -> p (a w)")).then_inc(sem(f"a1_w{s}"), 16)

        def a1_pe(pe):
            n1a.pe(pe)
            n1b.pe(pe)
            pe.wait_ge(*n1b.done())
            with pe.Fori(0, HP // 2) as mm:
                base = mm * U

                def project(j):
                    s, b = j // B, j % B
                    if b == 0:
                        pe.wait_ge(sem(f"a1_w{s}"), 16 * mm + 16)
                    for i in range(3):
                        for k in range(C):
                            mmul = pe.matmul(ps[:, i, 0:N], w1[s][:, (i * C + k) * P:(i * C + k + 1) * P],
                                             XN2[:, k, b * N:(b + 1) * N], start=(k == 0), stop=(k == C - 1))
                        if i:
                            mmul.then_inc(sem("a1_proj"), 1)

                def values(j):
                    pe.wait_ge(sem("a1_v"), base + j + 1)
                    for i in range(2):
                        mmul = pe.transpose(ps[:, 7, i * P:(i + 1) * P], v1[j % 2][:, i * P:(i + 1) * P], ident)
                    mmul.then_inc(sem("a1_vt"), 1)

                def scores(j):
                    pe.wait_ge(sem("a1_qk"), base + j + 1)
                    pe.wait_ge(sem("a1_added"), base + j + 1)
                    for h in range(2):
                        rows = slice(64 * h, 64 * h + 64)
                        q, k = q1[j % 2][rows, :], k1[j % 2][rows, :]
                        pe.matmul(ps[:, 4 + h, 0:SC0], k[:, 0:P], q, start=True, stop=True)
                        pe.matmul(ps[:, 4 + h, SC0:SCW], k[:, P:2 * P], q[:, P:N], start=True, stop=True).then_inc(sem("a1_s"), 1)

                def mix(j):
                    pe.wait_ge(sem("a1_vs"), base + j + 1)
                    for h in range(2):
                        o = ps[64 * h:64 * h + 64, 6, :]
                        pe.matmul(o[:, 0:N], vs1[:, 0, 64 * h:64 * h + 64], at1[h][:, 0:SC0], start=True, stop=False)
                        mmul = pe.matmul(o[:, P:N], vs1[:, 1, 64 * h:64 * h + 64], at1[h][:, SC0:SCW], start=False, stop=True)
                    mmul.then_inc(sem("a1_o"), 1)

                def output(j):
                    pe.wait_ge(sem("a1_og"), base + j + 1)
                    for d in range(C):
                        mmul = pe.matmul(ps[:, 4 + d, 0:N], w1[j // B][:, 768 + d * P:768 + (d + 1) * P], og1, start=True, stop=True)
                    mmul.then_inc(sem("a1_y"), 1)

                project(0)
                values(0)
                for j in range(U):
                    scores(j)
                    if j + 1 < U:
                        project(j + 1)
                    mix(j)
                    if j + 1 < U:
                        values(j + 1)
                    output(j)

        def a1_act(act):
            n1a.act(act)
            n1b.act(act)
            with act.Fori(0, HP // 2) as mm:
                base = mm * U

                def take(j):
                    w = w1[j // B]
                    act.wait_ge(sem("a1_proj"), 2 * base + 2 * j + 1)
                    act.activation(q1[j % 2], ps[:, 0, 0:N], ACT.Identity, bias=w[:, 1024:1025])
                    act.activation(k1[j % 2], ps[:, 1, 0:N], ACT.Identity, bias=w[:, 1025:1026]).then_inc(sem("a1_qk"), 1)
                    act.wait_ge(sem("a1_proj"), 2 * base + 2 * j + 2)
                    act.activation(v1[j % 2], ps[:, 2, 0:N], ACT.Identity, bias=w[:, 1026:1027]).then_inc(sem("a1_v"), 1)

                def exps(j):
                    for h in range(2):
                        act.wait_ge(sem("a1_max"), 2 * base + 2 * j + h + 1)
                        for i, (a, b) in enumerate(((0, SC0), (SC0, SCW))):
                            e = act.activation(at1[h][:, a:b], sm1[h][:, a:b], ACT.Exp, bias=nmax1[:, h, i:i + 1],
                                               accum_out=sum1[:, h, i:i + 1])
                        e.then_inc(sem("a1_exp"), 1)

                take(0)
                for j in range(U):
                    exps(j)
                    if j + 1 < U:
                        take(j + 1)

        def a1_dve(dve):
            n1a.dve(dve)
            n1b.dve(dve)
            dve.wait_ge(*n1b.done())
            for c in range(C):
                h = HT[:, c, :]
                dve.tensor_scalar(h, h, vec("bO1")[:, c:c + 1], None, ALU.add).then_inc(sem("a1_bias"), 1)
            dve.wait_ge(sem("a1_bias"), C)
            dve.sem_inc(sem("a1_added"), 1)
            with dve.Fori(0, HP // 2) as mm:
                base = mm * U

                def hide(j):
                    for h in range(2):
                        n = 2 * base + 2 * j + h
                        dve.wait_ge(sem("a1_s"), n + 1)
                        dve.tensor_tensor(sm1[h], ps[:, 4 + h, 0:SCW], const("hide"), ALU.add).then_inc(sem("a1_hid"), 1)
                        dve.wait_ge(sem("a1_hid"), n + 1)
                        dve.tensor_reduce(nmax1[:, h, 0:1], sm1[h][:, 0:SC0], AX.X, ALU.max, negate=True)
                        dve.tensor_reduce(nmax1[:, h, 1:2], sm1[h][:, SC0:SCW], AX.X, ALU.max, negate=True).then_inc(sem("a1_max"), 1)

                def values(j):
                    n = base + j + 1
                    dve.wait_ge(sem("a1_exp"), 2 * n)
                    dve.reciprocal(rs1, sum1).then_inc(sem("a1_rs"), 1)
                    dve.wait_ge(sem("a1_rs"), n)
                    dve.wait_ge(sem("a1_vt"), n)
                    for h in range(2):
                        v = ps[:, 7, 0:2 * P].rearrange("p (a b) -> p a b", b=P)[:, :, 64 * h:64 * h + 64]
                        ins = dve.tensor_tensor(vs1[:, :, 64 * h:64 * h + 64], v, spread(rs1[:, h, :], 64), ALU.mult)
                    ins.then_inc(sem("a1_vs"), 1)

                def take(j):
                    n = base + j + 1
                    dve.wait_ge(sem("a1_o"), n)
                    dve.tensor_copy(og1, ps[:, 6, 0:N]).then_inc(sem("a1_oc"), 1)
                    dve.wait_ge(sem("a1_oc"), n)
                    dve.tensor_tensor(og1[:, N - 1:N], og1[:, N - 1:N], v1[j % 2][:, N - 1:N], ALU.add).then_inc(sem("a1_og"), 1)

                def add(j):
                    h = HT[:, :, (j % B) * N:(j % B + 1) * N]
                    dve.wait_ge(sem("a1_y"), base + j + 1)
                    dve.tensor_tensor(h, h, ps[:, 4:6, 0:N], ALU.add).then_inc(sem("a1_added"), 1)

                for j in range(U):
                    hide(j)
                    values(j)
                    take(j)
                    add(j)

        h_a1 = [(sem("a1_added"), HP * B + 1)]

        f1 = Layer(FFNS[1], lambda c: h_a1)
        h_f1 = f1.done()

        def f1_sp(sp):
            f1.sp(sp)

        def f1_pe(pe):
            f1.pe(pe)

        def f1_act(act):
            f1.act(act)

        def f1_dve(dve):
            f1.dve(dve)

        def f1_pool(pool):
            f1.pool(pool)

        n2 = Norm(HT, XN, lambda c: h_f1)
        ar = Arena()
        H4 = 4
        w2 = [w[:, 0:A2_W] for w in watt]
        q2, k2, v2 = ([ar.take(N) for _ in range(2)] for _ in range(3))
        pr2 = [ar.take(H4, N) for _ in range(2)]
        mx2, nm2 = ar.take(2, H4), ar.take(2, H4)
        sm2, rs2 = ar.take(2, H4), ar.take(2, H4)
        pt2 = ar.take(2, H4 * N)
        vt2 = [ar.take(2, P) for _ in range(2)]
        ql2 = ar.take(H4)
        vl2 = ar.take(H4)
        pl2 = ar.take(N, rows=H4)
        ml2 = ar.take(4, rows=H4)
        pk2 = [ar.take(N, rows=H4) for _ in range(2)]
        vr2 = [ar.take(P, rows=H4) for _ in range(2)]
        os2 = ar.take(N)
        QS = 1.0 / 16
        pt2v = pt2.rearrange("p t (h q) -> p t h q", q=N)
        UA2 = 2 * B

        def a2_sp(sp):
            sp.wait_ge(*h_f1[0])
            for s in range(2):
                sp.dma_start(w2[s], dram["w_a2"][s]).then_inc(sem(f"a2_w{s}"), 16)
            for s in range(2):
                sp.wait_ge(sem("a2_qk"), B * (s + 1))
                sp.wait_ge(sem("a2_v"), B * (s + 1))
                sp.dma_start(w2[s], dram["w_a2"][2 + s]).then_inc(sem(f"a2_w{s}"), 16)

        def a2_pe(pe):
            n2.pe(pe)
            pe.wait_ge(*n2.done())
            with pe.Fori(0, 2) as mm:
                base = mm * UA2

                def project(j):
                    s, b = j // B, j % B
                    if b == 0:
                        pe.wait_ge(sem(f"a2_w{s}"), 16 * mm + 16)
                    if j >= 2:
                        pe.wait_ge(sem("a2_g1"), base + j - 1)
                    for i in range(3):
                        for k in range(C):
                            mmul = pe.matmul(ps[:, i, 0:N], w2[s][:, (i * C + k) * P:(i * C + k + 1) * P],
                                             XN[:, k, b * N:(b + 1) * N], start=(k == 0), stop=(k == C - 1))
                        if i:
                            mmul.then_inc(sem("a2_proj"), 1)

                def score(j, i):
                    if i:
                        pe.wait_ge(sem("a2_e0"), base + j + 1)
                    else:
                        pe.wait_ge(sem("a2_qk"), base + j + 1)
                        if j:
                            pe.wait_ge(sem("a2_e1"), base + j)
                    pe.nop(nofuse=True)
                    for h in range(H4):
                        r = slice(32 * h, 32 * h + 32)
                        mmul = pe.matmul(ps[:, 4 + h, 0:N], q2[j % 2][r, i * P:(i + 1) * P], k2[j % 2][r, :], start=True, stop=True)
                    mmul.then_inc(sem(f"a2_s{i}"), 1)

                def values(j):
                    pe.wait_ge(sem("a2_v"), base + j + 1)
                    pe.wait_ge(sem("a2_last"), base + j + 1)
                    if j >= 2:
                        pe.wait_ge(sem("a2_taken"), base + j - 1)
                    for t in range(2):
                        pe.transpose(ps[:, 3, t * P:(t + 1) * P], v2[j % 2][:, t * P:(t + 1) * P], ident)
                    pe.transpose(ps[0:H4, 3, 2 * P:3 * P], vl2, ident).then_inc(sem("a2_vt"), 1)

                def last(j):
                    pe.wait_ge(sem("a2_vsb"), base + j + 1)
                    pe.matmul(ps[0:H4, 3, 0:N], ql2, k2[j % 2], start=True, stop=True).then_inc(sem("a2_sl"), 1)

                def turn(j, i):
                    pe.wait_ge(sem(f"a2_p{i}"), base + j + 1)
                    if i:
                        pe.wait_ge(sem("a2_g0"), base + j + 1)
                    elif j + 1 < UA2:
                        pe.wait_ge(sem("a2_v"), base + j + 2)
                    for h in range(H4):
                        for t in range(2):
                            pe.transpose(ps[:, t, h * P:(h + 1) * P], pr2[i][:, h, t * P:(t + 1) * P], ident)
                    if i == 0:
                        pe.wait_ge(sem("a2_pl"), base + j + 1)
                        pe.nop(nofuse=True)
                        for t in range(2):
                            pe.transpose(ps[:, 2, 300 + H4 * t:300 + H4 * (t + 1)], pl2[:, t * P:(t + 1) * P], ident[0:H4, 0:H4])
                    pe.transpose(ps[0:H4, 2, i * P:(i + 1) * P], pr2[i][:, :, N - 1], ident).then_inc(sem(f"a2_t{i}"), 1)

                def mix(j):
                    pe.wait_ge(sem("a2_g1"), base + j + 1)
                    if j + 1 < UA2:
                        pe.wait_ge(sem("a2_el"), base + j + 2)
                    for h in range(H4):
                        for t in range(2):
                            pe.matmul(ps[32 * h:32 * h + 32, 3, 0:N], vt2[j % 2][:, t, 32 * h:32 * h + 32], pt2v[:, t, h, :],
                                      start=(t == 0), stop=(t == 1))
                    pe.matmul(ps[:, 3, 0:N], vr2[j % 2], pk2[j % 2], start=False, stop=True, skip_group_check=True).then_inc(sem("a2_o"), 1)

                def output(j):
                    c = j // B
                    pe.wait_ge(sem("a2_os"), base + j + 1)
                    pe.matmul(ps[64 * c:64 * c + 64, 3, 0:N], const("unpad")[:, 0:64], os2, start=True, stop=True).then_inc(sem("a2_y"), 1)

                project(0)
                values(0)
                score(0, 0)
                last(0)
                for j in range(UA2):
                    if j + 1 < UA2:
                        project(j + 1)
                    score(j, 1)
                    if j:
                        mix(j - 1)
                    turn(j, 0)
                    if j:
                        output(j - 1)
                    if j + 1 < UA2:
                        values(j + 1)
                    turn(j, 1)
                    if j + 1 < UA2:
                        score(j + 1, 0)
                        last(j + 1)
                mix(UA2 - 1)
                output(UA2 - 1)
                pe.wait_ge(sem("a2_taken"), base + UA2)

        def a2_act(act):
            n2.act(act)
            with act.Fori(0, 2) as mm:
                base = mm * UA2

                def take(j):
                    act.wait_ge(sem("a2_proj"), 2 * base + 2 * j + 1)
                    act.copy(q2[j % 2], ps[:, 0, 0:N])
                    act.copy(k2[j % 2], ps[:, 1, 0:N]).then_inc(sem("a2_qk"), 1)
                    act.wait_ge(sem("a2_proj"), 2 * base + 2 * j + 2)
                    act.copy(v2[j % 2], ps[:, 2, 0:N]).then_inc(sem("a2_v"), 1)

                def exps(j, i):
                    act.wait_ge(sem(f"a2_m{i}"), base + j + 1)
                    for h in range(H4):
                        e = act.activation(pr2[i][:, h, :], ps[:, 4 + h, 0:N], ACT.Exp, bias=nm2[:, i, h:h + 1], scale=QS,
                                           accum_out=sm2[:, i, h:h + 1])
                    e.then_inc(sem(f"a2_e{i}"), 1)

                def exp_last(j):
                    act.wait_ge(sem("a2_ml"), base + j + 1)
                    act.activation(pl2, ps[0:H4, 3, 0:N], ACT.Exp, bias=ml2[:, 1:2], scale=QS, accum_out=ml2[:, 2:3])\
                        .then_inc(sem("a2_el"), 1)

                take(0)
                exps(0, 0)
                exp_last(0)
                for j in range(UA2):
                    if j + 1 < UA2:
                        take(j + 1)
                    exps(j, 1)
                    if j + 1 < UA2:
                        exps(j + 1, 0)
                        exp_last(j + 1)

        def a2_dve(dve):
            n2.dve(dve)
            dve.wait_ge(*n2.done())
            with dve.Fori(0, 2) as mm:
                base = mm * UA2

                def by_head(j):
                    dve.wait_ge(sem("a2_v"), base + j + 1)
                    dve.tensor_scalar(ql2, const("block4"), q2[j % 2][:, N - 1:N], None, ALU.mult)
                    dve.tensor_scalar(vl2, const("block4"), v2[j % 2][:, N - 1:N], None, ALU.mult).then_inc(sem("a2_last"), 1)

                def values(j):
                    dve.wait_ge(sem("a2_vt"), base + j + 1)
                    dve.tensor_copy(vt2[j % 2], ps[:, 3, 0:2 * P].rearrange("p (a b) -> p a b", b=P))
                    dve.tensor_copy(vr2[j % 2], ps[0:H4, 3, 2 * P:3 * P]).then_inc(sem("a2_vsb"), 1)

                def maxima(j, i):
                    dve.wait_ge(sem(f"a2_s{i}"), base + j + 1)
                    dve.tensor_reduce(mx2[:, i, :], ps[:, 4:8, 0:N], AX.X, ALU.max, negate=True).then_inc(sem(f"a2_x{i}"), 1)
                    dve.wait_ge(sem(f"a2_x{i}"), base + j + 1)
                    dve.tensor_scalar(nm2[:, i, :], mx2[:, i, :], QS, None, ALU.mult).then_inc(sem(f"a2_m{i}"), 1)

                def max_last(j):
                    dve.wait_ge(sem("a2_sl"), base + j + 1)
                    dve.tensor_reduce(ml2[:, 0:1], ps[0:H4, 3, 0:N], AX.X, ALU.max, negate=True).then_inc(sem("a2_xl"), 1)
                    dve.wait_ge(sem("a2_xl"), base + j + 1)
                    dve.tensor_scalar(ml2[:, 1:2], ml2[:, 0:1], QS, None, ALU.mult).then_inc(sem("a2_ml"), 1)

                def normalise(j, i):
                    dve.wait_ge(sem(f"a2_e{i}"), base + j + 1)
                    dve.reciprocal(rs2[:, i, :], sm2[:, i, :]).then_inc(sem(f"a2_r{i}"), 1)
                    dve.wait_ge(sem(f"a2_r{i}"), base + j + 1)
                    dve.tensor_tensor(pr2[i], pr2[i], spread(rs2[:, i, :], N), ALU.mult).then_inc(sem(f"a2_p{i}"), 1)

                def normalise_last(j):
                    dve.wait_ge(sem("a2_el"), base + j + 1)
                    dve.reciprocal(ml2[:, 3:4], ml2[:, 2:3]).then_inc(sem("a2_rl"), 1)
                    dve.wait_ge(sem("a2_rl"), base + j + 1)
                    dve.tensor_scalar(pl2, pl2, ml2[:, 3:4], None, ALU.mult).then_inc(sem("a2_pl"), 1)
                    dve.wait_ge(sem("a2_pl"), base + j + 1)
                    dve.tensor_copy(pk2[j % 2][:, N - 1:N], pl2[:, N - 1:N])

                def take(j, i):
                    dve.wait_ge(sem(f"a2_t{i}"), base + j + 1)
                    for t in range(2):
                        dve.tensor_copy(pt2v[:, t, :, i * P:(i + 1) * P], ps[:, t, :].rearrange("p (h q) -> p h q", q=P))
                    if i == 0:
                        dve.tensor_copy(pt2v[:, :, :, N - 1], ps[:, 2, 300:300 + 2 * H4].rearrange("p (t h) -> p t h", h=H4))
                    dve.tensor_copy(pk2[j % 2][:, i * P:(i + 1) * P], ps[0:H4, 2, i * P:(i + 1) * P]).then_inc(sem(f"a2_g{i}"), 1)

                def heads_out(j):
                    dve.wait_ge(sem("a2_o"), base + j + 1)
                    dve.tensor_copy(os2, ps[:, 3, 0:N]).then_inc(sem("a2_os"), 1)

                def add(j):
                    c, b = j // B, j % B
                    r = slice(64 * c, 64 * c + 64)
                    dve.wait_ge(sem("a2_y"), base + j + 1)
                    h = HT[r, bass.ds(mm, 1), b * N:(b + 1) * N].rearrange("p a n -> p (a n)")
                    dve.tensor_tensor(h, h, ps[r, 3, 0:N], ALU.add).then_inc(sem("a2_taken"), 1)

                by_head(0)
                values(0)
                maxima(0, 0)
                max_last(0)
                normalise(0, 0)
                normalise_last(0)
                for j in range(UA2):
                    maxima(j, 1)
                    if j + 1 < UA2:
                        by_head(j + 1)
                    if j:
                        heads_out(j - 1)
                    take(j, 0)
                    if j:
                        add(j - 1)
                    if j + 1 < UA2:
                        values(j + 1)
                    normalise(j, 1)
                    take(j, 1)
                    if j + 1 < UA2:
                        maxima(j + 1, 0)
                        max_last(j + 1)
                        normalise(j + 1, 0)
                        normalise_last(j + 1)
                heads_out(UA2 - 1)
                add(UA2 - 1)

        h_a2 = [(sem("a2_taken"), 4 * B)]

        f2 = Layer(FFNS[2], lambda c: h_a2)
        h_f2 = f2.done()

        def f2_sp(sp):
            f2.sp(sp)

        def f2_pe(pe):
            f2.pe(pe)

        def f2_act(act):
            f2.act(act)

        def f2_dve(dve):
            f2.dve(dve)

        def f2_pool(pool):
            f2.pool(pool)

        n3 = Norm(HT, XN, lambda c: h_f2)
        DI, NS, KT = 512, 16, 4
        NH = NS // 2
        ar = Arena()
        u3, r3, d3 = ar.take(KT, T), ar.take(KT, T), ar.take(KT, T)
        at_bufs = ar.at
        hb3 = [ar.take(NH * N) for _ in range(4)]
        bc3 = [[ar.take(NH * N) for _ in range(4)],
               [x[:, :, :].rearrange("p c t -> p (c t)")[:, 0:NH * N] for x in (XN, XN2, XC, SQ)]]
        al = Arena()
        al.at = at_bufs
        win3, wde3, wbc3 = al.take(C, 2 * DI), al.take(KT, DI), al.take(KT, 2 * NS)
        ab3 = al.take(KT, T)
        bct3 = al.take(T, rows=2 * NS)
        dA3 = [ar.take(NH * N) for _ in range(2)]
        wo3 = watt[0][:, 0:KT * D].rearrange("p (k d) -> p k d", d=D)
        a3c = watt[0][:, KT * D:KT * D + 64]
        a3e = watt[0][:, KT * D + 64:KT * D + 128]
        du3 = [watt[1][:, N * i:N * (i + 1)] for i in range(2)]
        y3 = [watt[1][:, N * (2 + i):N * (3 + i)] for i in range(2)]
        bcd = nc.dram_tensor("state_rows", (2 * NS, T), f32, kind="Internal").ap()
        UB = 4 * KT

        def bc_load(sp, b, s):
            for i in range(4):
                src = bcd[NH * i:NH * (i + 1), b * N:(b + 1) * N] if isinstance(b, int) else bcd[NH * i:NH * (i + 1), bass.ds(b * N, N)]
                dst = bc3[s][i].rearrange("p (n t) -> p n t", t=N)
                sp.dma_start(dst, src.unsqueeze(0).broadcast_to([P, NH, N])).then_inc(sem(f"a3_bc{s}"), 16)

        def a3_sp(sp):
            sp.wait_ge(*h_f2[0])
            sp.dma_start(win3, dram["w3_in"]).then_inc(sem("a3_w"), 16)
            sp.dma_start(wde3, dram["w3_delta"]).then_inc(sem("a3_w"), 16)
            sp.dma_start(wbc3, dram["w3_bc"]).then_inc(sem("a3_w"), 16)
            sp.dma_start(wo3, dram["w3_out"]).then_inc(sem("a3_w"), 16)
            sp.wait_ge(sem("a3_bct"), NC)
            sp.dma_start(bcd, bct3).then_inc(sem("a3_bcd"), 16)
            sp.wait_ge(sem("a3_bcd"), 16)
            sp.wait_ge(sem("a3_delta"), KT)
            for b in range(2):
                bc_load(sp, b, b)
            for s in range(2):
                sp.wait_ge(sem("a3_hc"), 2 * KT * (s + 1))
                bc_load(sp, 2 + s, s)

        def a3_pe(pe):
            n3.pe(pe)
            pe.wait_ge(*n3.done())
            pe.wait_ge(sem("a3_w"), 64)
            n = 0
            for m in range(2 * KT):
                for t0, w in CHUNKS:
                    if n >= 4:
                        pe.wait_ge(sem("a3_in"), n - 3)
                    for k in range(C):
                        mmul = pe.matmul(ps[:, n % 4, 0:w], win3[:, k, m * P:(m + 1) * P], XN[:, k, t0:t0 + w], start=(k == 0), stop=(k == C - 1))
                    mmul.then_inc(sem("a3_inps"), 1)
                    n += 1
            for c, (t0, w) in enumerate(CHUNKS):
                for k in range(KT):
                    mmul = pe.matmul(ps[0:2 * NS, 4 + c, 0:w], wbc3[:, k, :], u3[:, k, t0:t0 + w], start=(k == 0), stop=(k == KT - 1))
                mmul.then_inc(sem("a3_bcps"), 1)
            n = 0
            pe.wait_ge(sem("a3_in"), 2 * KT * NC)
            for m in range(KT):
                for t0, w in CHUNKS:
                    if n >= 4:
                        pe.wait_ge(sem("a3_pre"), n - 3)
                    for k in range(KT):
                        mmul = pe.matmul(ps[:, n % 4, 0:w], wde3[:, k, m * P:(m + 1) * P], u3[:, k, t0:t0 + w], start=(k == 0), stop=(k == KT - 1))
                    mmul.then_inc(sem("a3_deps"), 1)
                    n += 1
            pe.wait_ge(sem("a3_pre"), KT * NC)
            pe.wait_ge(sem("a3_bct"), NC)
            pe.sem_inc(sem("a3_sum"), 4)
            with pe.Fori(0, 2) as bb:
                base = UB * bb

                def total(s, ct, hf):
                    n = 8 * s + 2 * ct + hf
                    pe.wait_ge(sem("a3_hc"), base + n + 1)
                    if hf == 0:
                        pe.wait_ge(sem("a3_yfree"), 2 * KT * bb + KT * s + ct + 1)
                    for i in range(NH):
                        mmul = pe.matmul(ps[:, ct % 2, 0:N], ident, hb3[n % 4][:, i * N:(i + 1) * N],
                                         start=(hf == 0 and i == 0), stop=(hf == 1 and i == NH - 1))
                    mmul.then_inc(sem("a3_sum"), 1)

                def output(s, ct):
                    pe.wait_ge(sem("a3_y"), 2 * KT * bb + KT * s + ct + 1)
                    if ct == 0:
                        pe.wait_ge(sem("a3_added"), 2 * bb + s + 1)
                    for d in range(C):
                        mmul = pe.matmul(ps[:, 4 + 2 * s + d, 0:N], wo3[:, ct, d * P:(d + 1) * P], y3[ct % 2], start=(ct == 0), stop=(ct == KT - 1))
                    mmul.then_inc(sem("a3_o"), 1)

                last = None
                for s in range(2):
                    for ct in range(KT):
                        total(s, ct, 0)
                        if last:
                            output(*last)
                        total(s, ct, 1)
                        last = (s, ct)
                output(*last)

        def a3_act(act):
            n3.act(act)
            act.activation(a3e, vec("A_log"), ACT.Exp).then_inc(sem("a3_ae"), 1)
            n = 0
            for m in range(2 * KT):
                dst = u3[:, m, :] if m < KT else r3[:, m - KT, :]
                for t0, w in CHUNKS:
                    act.wait_ge(sem("a3_inps"), n + 1)
                    act.activation(dst[:, t0:t0 + w], ps[:, n % 4, 0:w], ACT.Silu).then_inc(sem("a3_in"), 1)
                    n += 1
            for c, (t0, w) in enumerate(CHUNKS):
                act.wait_ge(sem("a3_bcps"), c + 1)
                act.copy(bct3[:, t0:t0 + w], ps[0:2 * NS, 4 + c, 0:w]).then_inc(sem("a3_bct"), 1)
            n = 0
            for m in range(KT):
                for t0, w in CHUNKS:
                    act.wait_ge(sem("a3_deps"), n + 1)
                    act.activation(d3[:, m, t0:t0 + w], ps[:, n % 4, 0:w], ACT.Identity, bias=vec("b_delta")[:, m:m + 1])
                    act.activation(ab3[:, m, t0:t0 + w], ps[:, n % 4, 0:w], ACT.Abs, bias=vec("b_delta")[:, m:m + 1]).then_inc(sem("a3_pre"), 1)
                    n += 1
                act.wait_ge(sem("a3_pre"), n)
                act.activation(ab3[:, m, :], ab3[:, m, :], ACT.Exp, scale=-1.0).then_inc(sem("a3_sp"), 1)
                act.wait_ge(sem("a3_sp"), 2 * m + 1)
                act.activation(ab3[:, m, :], ab3[:, m, :], ACT.Ln, bias=1.0).then_inc(sem("a3_sp"), 1)
            act.wait_ge(sem("a3_delta"), KT)
            act.wait_ge(sem("a3_a"), 3)
            with act.Fori(0, 2) as bb:
                base = UB * bb
                for s in range(2):
                    for ct in range(KT):
                        for hf in range(2):
                            n = 8 * s + 2 * ct + hf
                            act.wait_ge(sem("a3_dafree"), base + n + 1)
                            act.nop(nofuse=True)
                            d = d3[:, ct, bass.ds((2 * bb + s) * N + 1, N - 1)]
                            for i in range(NH):
                                col = ct * NS + hf * NH + i
                                e = act.activation(dA3[n % 2][:, i * N + 1:(i + 1) * N], d, ACT.Exp, scale=a3c[:, col:col + 1])
                            e.then_inc(sem("a3_da"), 1)

        def a3_dve(dve):
            n3.dve(dve)
            dve.wait_ge(sem("a3_ae"), 1)
            dve.tensor_scalar(a3c, a3e, -1.0, None, ALU.mult).then_inc(sem("a3_a"), 1)
            for i in range(2):
                dve.memset(dA3[i].rearrange("p (n t) -> p n t", t=N)[:, :, 0:1], 0.0).then_inc(sem("a3_a"), 1)
            for m in range(KT):
                dve.wait_ge(sem("a3_sp"), 2 * m + 2)
                dve.scalar_tensor_tensor(d3[:, m, :], d3[:, m, :], 0.0, ab3[:, m, :], ALU.max, ALU.add).then_inc(sem("a3_delta"), 1)
            dve.sem_inc(sem("a3_dafree"), 2)
            dve.sem_inc(sem("a3_yfree"), 2)
            dve.sem_inc(sem("a3_added"), 2)
            with dve.Fori(0, 2) as bb:
                base = UB * bb

                def scan(s, ct, hf):
                    n = 8 * s + 2 * ct + hf
                    h = hb3[n % 4]
                    dve.wait_ge(sem("a3_da"), base + n + 1)
                    dve.wait_ge(sem("a3_dbu"), base + n + 1)
                    dve.tensor_tensor_scan(h, dA3[n % 2], h, 0.0, ALU.mult, ALU.add).then_inc(sem("a3_dafree"), 1)
                    dve.wait_ge(sem("a3_dafree"), base + n + 3)
                    dve.tensor_tensor(h, h, bc3[s][2 + hf], ALU.mult).then_inc(sem("a3_hc"), 1)

                def finish(s, ct):
                    n = 2 * KT * bb + KT * s + ct
                    cols = bass.ds((2 * bb + s) * N, N)
                    dve.wait_ge(sem("a3_sum"), 2 * n + 6)
                    dve.scalar_tensor_tensor(y3[ct % 2], u3[:, ct, cols], vec("D_param")[:, ct:ct + 1], ps[:, ct % 2, 0:N], ALU.mult, ALU.add)\
                        .then_inc(sem("a3_yfree"), 1)
                    dve.wait_ge(sem("a3_yfree"), n + 3)
                    dve.tensor_tensor(y3[ct % 2], y3[ct % 2], r3[:, ct, cols], ALU.mult).then_inc(sem("a3_y"), 1)

                def add(s):
                    h = HT[:, :, bass.ds((2 * bb + s) * N, N)]
                    dve.wait_ge(sem("a3_o"), 2 * KT * bb + KT * (s + 1))
                    dve.tensor_tensor(h, h, ps[:, 4 + 2 * s:6 + 2 * s, 0:N], ALU.add).then_inc(sem("a3_added"), 1)

                last = None
                for s in range(2):
                    for ct in range(KT):
                        scan(s, ct, 0)
                        if last:
                            finish(*last)
                        scan(s, ct, 1)
                        if last and last[1] == KT - 1:
                            add(last[0])
                        last = (s, ct)
                finish(*last)
                add(last[0])

        def a3_pool(pool):
            pool.wait_ge(sem("a3_delta"), KT)
            pool.sem_inc(sem("a3_du"), 1)
            with pool.Fori(0, 2) as bb:
                base = UB * bb
                for s in range(2):
                    cols = bass.ds((2 * bb + s) * N, N)
                    for ct in range(KT):
                        for hf in range(2):
                            n = 8 * s + 2 * ct + hf
                            d = du3[ct % 2]
                            if hf == 0:
                                if ct == 0:
                                    pool.wait_ge(sem(f"a3_bc{s}"), 64 * bb + 64)
                                pool.nop(nofuse=True)
                                pool.tensor_tensor(d, d3[:, ct, cols], u3[:, ct, cols], ALU.mult).then_inc(sem("a3_du"), 1)
                                pool.wait_ge(sem("a3_du"), 2 * KT * bb + KT * s + ct + 2)
                            pool.wait_ge(sem("a3_sum"), base + n + 1)
                            pool.tensor_tensor(hb3[n % 4].rearrange("p (n t) -> p n t", t=N), bc3[s][hf].rearrange("p (n t) -> p n t", t=N),
                                               over(d, NH), ALU.mult).then_inc(sem("a3_dbu"), 1)

        h_a3 = [(sem("a3_added"), B + 2)]

        f3 = Layer(FFNS[3], lambda c: h_a3)
        h_f3 = f3.done()

        def f3_sp(sp):
            f3.sp(sp)

        def f3_pe(pe):
            f3.pe(pe)

        def f3_act(act):
            f3.act(act)

        def f3_dve(dve):
            f3.dve(dve)

        def f3_pool(pool):
            f3.pool(pool)

        def store_sp(sp):
            for s, v in h_f3:
                sp.wait_ge(s, v)
            sp.dma_start(out.rearrange("(c p) t -> p c t", p=P), HT[:, :, :]).then_inc(sem("stored"), 16)
            sp.wait_ge(sem("stored"), 16)

        block = ctx.enter_context(nc.Block())

        @block.sync
        def _(sp):
            tok_sp(sp)
            a0_sp(sp)
            f0_sp(sp)
            a1_sp(sp)
            f1_sp(sp)
            a2_sp(sp)
            f2_sp(sp)
            a3_sp(sp)
            f3_sp(sp)
            store_sp(sp)

        @block.tensor
        def _(pe):
            tok_pe(pe)
            tok_norm.pe(pe)
            a0_pe(pe)
            f0_pe(pe)
            a1_pe(pe)
            f1_pe(pe)
            a2_pe(pe)
            f2_pe(pe)
            a3_pe(pe)
            f3_pe(pe)

        @block.scalar
        def _(act):
            tok_norm.act(act)
            a0_act(act)
            f0_act(act)
            a1_act(act)
            f1_act(act)
            a2_act(act)
            f2_act(act)
            a3_act(act)
            f3_act(act)

        @block.vector
        def _(dve):
            tok_dve(dve)
            tok_norm.dve(dve)
            tok_cls(dve)
            a0_dve(dve)
            f0_dve(dve)
            a1_dve(dve)
            f1_dve(dve)
            a2_dve(dve)
            f2_dve(dve)
            a3_dve(dve)
            f3_dve(dve)

        @block.gpsimd
        def _(pool):
            a0_pool(pool)
            f0_pool(pool)
            f1_pool(pool)
            f2_pool(pool)
            a3_pool(pool)
            f3_pool(pool)


def constants():
    out = np.zeros((P, CONST_W), np.float32)
    r = np.arange(P)

    def put(name, v):
        a, b = CONSTS[name]
        out[:, a:b] = v
    put("ident", np.eye(P))
    put("mean", 1.0 / D)
    put("headones", r[:, None] // 64 == r[None, :] // 64)
    put("expo", np.arange(EMIN, EMAX + 1)[None])
    put("expo_r", np.arange(EMAX, EMIN - 1, -1)[None])
    seen = np.concatenate([np.arange(N)[None] >= r[:, None], np.arange(P, N)[None] >= r[:, None] + P], 1)
    put("causal", seen)
    put("hide", np.where(seen, 0.0, -BIG))
    un = np.zeros((P, 2, 64))
    for p in range(P):
        if p % 32 < 16:
            un[p, 0, 16 * (p // 32) + p % 32] = 1
    un[:, 1] = un[:, 0]
    put("unpad", un.reshape(P, -1))
    put("block4", r[:, None] // 32 == np.arange(4)[None])
    return out


def by_part(a):
    a = np.asarray(a)
    return np.ascontiguousarray(a.reshape((-1, P) + a.shape[1:]).swapaxes(0, 1))


def pack(*parts):
    return np.concatenate([np.asarray(p, np.float32).reshape(P, -1) for p in parts], 1)


def layouts(i):
    i = {k: np.asarray(v) for k, v in i.items()}
    a = {"consts": constants()}
    x = i["x"].reshape(B, 5, 16, 8, 16, 8).transpose(0, 2, 4, 1, 3, 5).reshape(B * D, PF)
    a["xt"] = by_part(np.concatenate([x.T, np.zeros((3 * P - PF, B * D), np.float32)]))
    a["wtok"] = by_part(np.concatenate([i["L0_tok_W"], np.zeros((3 * P - PF, D), np.float32)]))

    def col(v):
        return by_part(v.reshape(-1))

    a["vecs"] = pack(col(i["cls_tok"]), col(i["L0_tok_gamma"]), col(i["L0_attn_ln_gamma"]), col(i["L0_attn_ln_beta"]),
                     col(i["L0_attn_bO"]), col(i["L1_attn_b_o"]), col(i["L0_attn_alpha_logit"]), col(i["L3_attn_b_delta"]),
                     by_part(i["L3_attn_A_log"]), col(i["L3_attn_D_param"]),
                     np.repeat(i["L3_ffn_gate_b"][None], P, 0), np.repeat(i["L2_ffn_e_score_correction_bias"][None], P, 0))
    pairs = []
    for m in range(HP):
        rows = slice(m * P, (m + 1) * P)
        pairs.append(pack(*[by_part(i["L0_attn_W" + n][rows].T) for n in ("Q", "K", "V", "g")],
                          i["L0_attn_WO"][:, rows].T, *[col(i["L0_attn_b" + n][rows]) for n in ("Q", "K", "V", "g")]))
    a["w_a0"] = np.stack(pairs)
    w, bq = i["L1_attn_W_qkv"].reshape(1024, 3, D), i["L1_attn_b_qkv"].reshape(1024, 3)
    pairs = []
    for m in range(HP):
        rows = slice(m * P, (m + 1) * P)
        pairs.append(pack(*[by_part(w[rows, n].T) for n in range(3)], i["L1_attn_W_o"][:, rows].T,
                          *[col(bq[rows, n]) for n in range(3)]))
    a["w_a1"] = np.stack(pairs)
    quads = []
    for m in range(4):
        parts = []
        for n in "qkv":
            wt = np.zeros((D, 4, 32), np.float32)
            wt[:, :, 0:16] = i["L2_attn_W" + n][64 * m:64 * m + 64].T.reshape(D, 4, 16)
            parts.append(by_part(wt.reshape(D, P)))
        quads.append(pack(*parts))
    a["w_a2"] = np.stack(quads)
    def ups(mats, biases=()):
        return pack(*[by_part(m) for m in mats], *[col(b) for b in biases])
    f0 = [(i["L0_ffn_w1_shared"], i["L0_ffn_w2_shared"])] + list(zip(i["L0_ffn_w1_routed"], i["L0_ffn_w2_routed"]))
    a["up_f0"] = np.stack([ups([w1]) for w1, _ in f0])
    a["dn_f0"] = np.stack([pack(by_part(w2)) for _, w2 in f0])
    a["up_f1"] = np.stack([ups([i["L1_ffn_W1"][e].T, i["L1_ffn_W3"][e].T], [i["L1_ffn_b1"][e], i["L1_ffn_b3"][e], i["L1_ffn_b2"][e]]) for e in range(16)])
    a["dn_f1"] = np.stack([pack(by_part(i["L1_ffn_W2"][e].T)) for e in range(16)])
    gu = i["L2_ffn_gate_up_proj"]
    a["up_f2"] = np.stack([ups([gu[e, 0:P].T, gu[e, P:].T]) for e in range(32)])
    a["dn_f2"] = np.stack([pack(by_part(i["L2_ffn_down_proj"][e].T)) for e in range(32)])
    a["up_f3"] = np.stack([ups([i["L3_ffn_w1"][e].T], [i["L3_ffn_b1"][e], i["L3_ffn_b2"][e]]) for e in range(8)])
    a["dn_f3"] = np.stack([pack(by_part(i["L3_ffn_w2"][e].T)) for e in range(8)])
    a["wr_f0"] = by_part(i["L0_ffn_w_router"])
    a["wr_f1"] = by_part(i["L1_ffn_Wg"].T)
    a["wr_f2"] = by_part(i["L2_ffn_classifier_weight"].T)
    a["wr_f3"] = by_part(i["L3_ffn_gate_w"].T)
    a["w3_in"] = by_part(i["L3_attn_W_in"])
    a["w3_delta"] = by_part(i["L3_attn_W_delta"])
    a["w3_bc"] = by_part(np.concatenate([i["L3_attn_W_B"], i["L3_attn_W_C"]], 1))
    a["w3_out"] = by_part(i["L3_attn_W_out"])
    return a


def kernel(**inputs):
    import concourse.bacc as bacc
    from concourse.bass_utils import run_bass_kernel_spmd

    nc = bacc.Bacc("TRN2", target_bir_lowering=False, num_devices=1)
    arrays = {f"in_{n}": a for n, a in layouts(inputs).items()}
    dram = {n[3:]: nc.dram_tensor(n, a.shape, mybir.dt.float32, kind="ExternalInput").ap() for n, a in arrays.items()}
    out = nc.dram_tensor("out_0", (D, T), mybir.dt.float32, kind="ExternalOutput").ap()
    build(nc, dram, out)
    r = run_bass_kernel_spmd(nc, [arrays], core_ids=[0])
    return np.ascontiguousarray(np.asarray(r.results[0]["out_0"]).T).reshape(B, N, D)
```

```python
from contextlib import ExitStack

import numpy as np
import concourse.bass as bass
from concourse import mybir

P = 128
D = 256
C = D // P
B = 4
N = 257
T = B * N
PF = 320
EPS = 1e-5
RMS_EPS = 1.1920929e-07
BANK = 512
CHUNKS = [(0, 344), (344, 342), (686, 342)]
CW = 344
NC = len(CHUNKS)
TILES = [128 * j for j in range(8)] + [T - 128]
NT = len(TILES)
SC0, SC1 = N, N - P
SCW = SC0 + SC1
EMIN, EMAX = -8, 128
NEXP = EMAX - EMIN + 1
BIG = 1e30


class Ffn:
    def __init__(self, name, units, mt, gated, act, has_bias):
        self.name, self.units, self.mt, self.gated, self.act, self.has_bias = name, units, mt, gated, act, has_bias
        self.up_mats = 2 if gated else 1
        self.up_w = self.up_mats * C * mt * P
        self.biases = self.up_mats * mt + C if has_bias else 0
        self.up_words = self.up_w + self.biases
        self.dn_w = mt * D
        self.psums = self.up_mats
        self.depth = 4 // self.psums


FFNS = [Ffn("f0", 9, 8, False, "Silu", False), Ffn("f1", 16, 2, True, "Silu", True),
        Ffn("f2", 32, 1, True, "Silu", False), Ffn("f3", 8, 8, False, "Relu", True)]

CONSTS = {}
_at = 0
for _n, _w in (("ident", P), ("mean", P), ("headones", P), ("expo", NEXP), ("expo_r", NEXP), ("causal", SCW), ("hide", SCW),
               ("unpad", 2 * 64), ("block4", 4)):
    CONSTS[_n] = (_at, _at + _w)
    _at += _w
CONST_W = _at


VECS = {}
_at = 0
for _n, _w in (("cls", C), ("tok_gamma", C), ("ln_gamma", C), ("ln_beta", C), ("bO0", C), ("bO1", C), ("alpha", 8),
               ("b_delta", 4), ("A_log", 64), ("D_param", 4), ("gate_b", 8), ("score_b", 40)):
    VECS[_n] = (_at, _at + _w)
    _at += _w
VEC_W = _at
HP = 8
A0_W = 4 * C * P + D + 4 + P
NE = N + 1
A1_W = 3 * C * P + D + 3 + P
A2_W = 3 * C * P
ARENA_W = 34000


def build(nc, dram, out):
    f32 = mybir.dt.float32
    u32 = mybir.dt.uint32
    ALU = mybir.AluOpType
    ACT = mybir.ActivationFunctionType
    AX = mybir.AxisListType
    ctx = ExitStack()
    with ctx:
        def sb(name, shape):
            return ctx.enter_context(nc.sbuf_tensor(name, shape, f32))

        sems = {}

        def sem(name):
            if name not in sems:
                sems[name] = ctx.enter_context(nc.semaphore(name))
            return sems[name]

        HT = sb("HT", [P, C, T])
        XN = sb("XN", [P, C, T])
        XN2 = sb("XN2", [P, C, T + 2])
        XC = sb("XC", [P, C, T])
        SQ = sb("SQ", [P, C, T])
        consts = sb("consts", [P, CONST_W])
        vecs = sb("vecs", [P, VEC_W])
        watt = [sb(f"watt{s}", [P, A0_W]) for s in range(2)]
        epsc = sb("epsc", [P, 2])
        region = (nc.sbuf_base + 31) // 32 * 32

        def at(name, shape, offset, dtype=f32):
            t = nc.alloc_sbuf_tensor_at(name, [P] + shape, dtype, offset=region + 4 * offset)
            return t, offset + (int(np.prod(shape)) + 7) // 8 * 8

        arena, _ = at("arena", [ARENA_W], 0)
        ps = ctx.enter_context(nc.psum_tensor("ps", [P, 8, BANK], f32))

        class Arena:
            def __init__(self):
                self.at = 0

            def take(self, *shape, rows=P):
                w = int(np.prod(shape))
                v = arena[0:rows, self.at:self.at + w]
                self.at += w
                assert self.at <= ARENA_W, self.at
                if len(shape) == 2:
                    v = v.rearrange("p (a b) -> p a b", b=shape[1])
                elif len(shape) == 3:
                    v = v.rearrange("p (a b c) -> p a b c", b=shape[1], c=shape[2])
                return v

        def const(name):
            a, b = CONSTS[name]
            return consts[:, a:b]

        def vec(name):
            a, b = VECS[name]
            return vecs[:, a:b]

        ident, mean_mat = const("ident"), const("mean")

        def spread(col, w):
            return col.unsqueeze(2).broadcast_to([col.shape[0], col.shape[1], w])

        def over(row, n):
            return row.unsqueeze(1).broadcast_to([row.shape[0], n, row.shape[1]])

        class Norm:
            count = 0

            def __init__(self, src, dst, ready, centred=True, eps=EPS, gamma=None, beta=None):
                self.src, self.dst, self.ready = src, dst, ready
                self.centred, self.eps, self.gamma, self.beta = centred, eps, gamma, beta
                self.base = NC * Norm.count
                self.cbase = NC * Norm.centred_before if centred else None
                Norm.count += 1
                Norm.centred_before += centred
                self.gbase = 2 * NC * Norm.gamma_before
                Norm.gamma_before += gamma is not None

            centred_before = 0
            gamma_before = 0

            def done(self, c=NC - 1):
                return sem("ln_out"), self.base + c + 1

            def pe(self, pe):
                if self.centred:
                    for c, (t0, w) in enumerate(CHUNKS):
                        for s, v in self.ready(c):
                            pe.wait_ge(s, v)
                        for k in range(C):
                            mm = pe.matmul(ps[:, c, 0:w], mean_mat, self.src[:, k, t0:t0 + w], start=(k == 0), stop=(k == C - 1))
                        mm.then_inc(sem("ln_mean"), 1)
                for c, (t0, w) in enumerate(CHUNKS):
                    pe.wait_ge(sem("ln_sq"), self.base + c + 1)
                    for k in range(C):
                        mm = pe.matmul(ps[:, NC + c, 0:w], mean_mat, SQ[:, k, t0:t0 + w], start=(k == 0), stop=(k == C - 1))
                    mm.then_inc(sem("ln_var"), 1)

            def act(self, act):
                for c, (t0, w) in enumerate(CHUNKS):
                    if self.centred:
                        act.wait_ge(sem("ln_cent"), self.cbase + c + 1)
                        x = XC
                    else:
                        for s, v in self.ready(c):
                            act.wait_ge(s, v)
                        x = self.src
                    act.activation(SQ[:, :, t0:t0 + w], x[:, :, t0:t0 + w], ACT.Square).then_inc(sem("ln_sq"), 1)
                for c, (t0, w) in enumerate(CHUNKS):
                    act.wait_ge(sem("ln_var"), self.base + c + 1)
                    act.wait_ge(sem("ln_eps"), 2)
                    eps = epsc[:, 0:1] if self.eps == EPS else epsc[:, 1:2]
                    act.activation(SQ[:, 0, t0:t0 + w], ps[:, NC + c, 0:w], ACT.Sqrt, bias=eps).then_inc(sem("ln_std"), 1)

            def dve(self, dve):
                if self.centred:
                    for c, (t0, w) in enumerate(CHUNKS):
                        dve.wait_ge(sem("ln_mean"), self.cbase + c + 1)
                        dve.tensor_tensor(XC[:, :, t0:t0 + w], self.src[:, :, t0:t0 + w], over(ps[:, c, 0:w], C),
                                          ALU.subtract).then_inc(sem("ln_cent"), 1)
                x = XC if self.centred else self.src
                for c, (t0, w) in enumerate(CHUNKS):
                    n = self.base + c + 1
                    dve.wait_ge(sem("ln_std"), n)
                    dve.reciprocal(SQ[:, 1, t0:t0 + w], SQ[:, 0, t0:t0 + w]).then_inc(sem("ln_rstd"), 1)
                    dve.wait_ge(sem("ln_rstd"), n)
                    last = dve.tensor_tensor(self.dst[:, :, t0:t0 + w], x[:, :, t0:t0 + w], over(SQ[:, 1, t0:t0 + w], C), ALU.mult)
                    if self.gamma is not None:
                        for k in range(C):
                            last.then_inc(sem("ln_scaled"), 1)
                            dve.wait_ge(sem("ln_scaled"), self.gbase + C * c + k + 1)
                            v = self.dst[:, k, t0:t0 + w]
                            if self.beta is None:
                                last = dve.tensor_scalar(v, v, self.gamma[:, k:k + 1], None, ALU.mult)
                            else:
                                last = dve.tensor_scalar(v, v, self.gamma[:, k:k + 1], self.beta[:, k:k + 1], ALU.mult, ALU.add)
                    last.then_inc(sem("ln_out"), 1)

        ar = Arena()
        xt = ar.take(3, B * D)
        wtok = ar.take(3, D)

        def tok_sp(sp):
            sp.dma_start(xt, dram["xt"]).then_inc(sem("tok_in"), 16)
            sp.dma_start(wtok, dram["wtok"]).then_inc(sem("tok_in"), 16)
            sp.dma_start(consts[:, :], dram["consts"]).then_inc(sem("const_in"), 16)
            sp.dma_start(vecs[:, :], dram["vecs"]).then_inc(sem("const_in"), 16)

        def tok_pe(pe):
            pe.wait_ge(sem("tok_in"), 32)
            for b in range(B):
                for d in range(C):
                    for k in range(3):
                        r = min(P, PF - k * P)
                        mm = pe.matmul(ps[:, 2 * b + d, 0:D], wtok[0:r, k, d * P:(d + 1) * P], xt[0:r, k, b * D:(b + 1) * D],
                                       start=(k == 0), stop=(k == 2))
                mm.then_inc(sem("tok_ps"), 1)
            pe.wait_ge(sem("const_in"), 32)

        def cls_columns(dve):
            return dve.tensor_copy(HT[:, :, :].rearrange("p c (b n) -> p c b n", n=N)[:, :, :, 0], spread(vec("cls"), B))

        def tok_dve(dve):
            dve.memset(epsc[:, 0:1], EPS).then_inc(sem("ln_eps"), 1)
            dve.memset(epsc[:, 1:2], RMS_EPS).then_inc(sem("ln_eps"), 1)
            dve.wait_ge(sem("const_in"), 32)
            cls_columns(dve).then_inc(sem("tok_h"), 1)
            for b in range(B):
                dve.wait_ge(sem("tok_ps"), b + 1)
                dve.tensor_copy(HT[:, :, b * N + 1:(b + 1) * N], ps[:, 2 * b:2 * b + 2, 0:D]).then_inc(sem("tok_h"), 1)

        tok_norm = Norm(HT, HT, lambda c: [(sem("tok_h"), B + 1)], gamma=vec("tok_gamma"))

        def tok_cls(dve):
            dve.wait_ge(*tok_norm.done())
            cls_columns(dve).then_inc(sem("h0"), 1)

        n0a = Norm(HT, XN, lambda c: [(sem("h0"), 1)])
        n0b = Norm(XN, XN2, lambda c: [n0a.done(c)], gamma=vec("ln_gamma"), beta=vec("ln_beta"))
        ar = Arena()
        w0 = [w[:, 0:A0_W] for w in watt]
        powt = ar.take(HP, NEXP)
        powr = ar.take(HP, NEXP)
        tab = ar.take(2, NEXP)
        lga = ar.take(4, HP)
        q0, k0, g0 = ([ar.take(N) for _ in range(2)] for _ in range(3))
        q16, kA, kB = ar.take(16, 16), ar.take(8, 16), ar.take(8, 32)
        q32, k32 = ar.take(4, 32), ar.take(4, 32)
        q64, k64 = ar.take(2, 64), ar.take(2, 64)
        q128, k128 = ar.take(P + 1), ar.take(2, P)
        at0 = [ar.take(SCW) for _ in range(2)]
        vt0 = [ar.take(2, P) for _ in range(2)]
        og0 = ar.take(N)
        lastp, lastv, vl0 = ar.take(2), ar.take(1), ar.take(2)
        U = 2 * B
        LOOPS = HP // 2 - 1
        E0 = -EMIN
        fr = mybir.dt.float32r
        off = (ar.at + 7) // 8 * 8
        xh, off = at("xh", [C, B, NE], off, fr)
        xl, off = at("xl", [C, B, NE], off, fr)
        wh, wl = [None, None], [None, None]
        for s_ in range(2):
            wh[s_], off = at(f"wh{s_}", [4 * C * P], off, fr)
            wl[s_], off = at(f"wl{s_}", [4 * C * P], off, fr)
        assert off <= ARENA_W
        a0_end = ar.at

        def R(e):
            return EMAX - e

        def images(x):
            return x[:, :, 0:T].rearrange("p c (b n) -> p c b n", n=N)

        def split3(pe, out, w, x, first, last):
            for n, (i, j) in enumerate(((0, 0), (0, 1), (1, 0))):
                mm = pe.matmul(out, w[i], x[j], start=(first and n == 0), stop=(last and n == 2))
            return mm

        def split_tokens_act(act, done):
            act.copy(xh[:, :, :, 0:N], images(XN2))
            act.copy(xh[:, :, :, N:NE], images(XN2)[:, :, :, N - 1:N]).then_inc(done, 1)

        def split_tokens_dve(dve, done):
            dve.tensor_tensor(xl[:, :, :, 0:N], images(XN2), xh[:, :, :, 0:N].bitcast(f32), ALU.subtract)
            dve.tensor_tensor(xl[:, :, :, N:NE], images(XN2)[:, :, :, N - 1:N], xh[:, :, :, N:NE].bitcast(f32), ALU.subtract).then_inc(done, 1)

        def a0_load(sp, m, s):
            return sp.dma_start(w0[s], m).then_inc(sem(f"a0_w{s}"), 16)

        def a0_sp(sp):
            for s in range(2):
                a0_load(sp, dram["w_a0"][s], s)
            with sp.Fori(1, HP // 2) as mm:
                for s in range(2):
                    sp.wait_ge(sem("a0_y"), mm * U + (s - 1) * B)
                    a0_load(sp, dram["w_a0"][bass.ds(2 * mm + s, 1), :, :].rearrange("a p w -> p (a w)"), s)

        def a0_pe(pe):
            n0a.pe(pe)
            n0b.pe(pe)
            pe.wait_ge(sem("split_xl"), 1)

            def project(mm, j):
                n, s, b = mm * U + j, (j // B) % 2, j % B
                if b == 0:
                    pe.wait_ge(sem("split_wl"), 2 * mm + j // B + 1)
                if not (isinstance(n, int) and n == 0):
                    pe.wait_ge(sem("a0_vg"), n)
                    pe.wait_ge(sem("a0_vsb"), n)
                w = (wh[s], wl[s])

                def feature_major(bank, i):
                    for k in range(C):
                        mmul = split3(pe, ps[:, bank, 0:NE], [x[:, (i * C + k) * P:(i * C + k + 1) * P] for x in w],
                                      [x[:, k, b, :] for x in (xh, xl)], k == 0, k == C - 1)
                    return mmul

                feature_major(0, 0)
                feature_major(1, 1).then_inc(sem("a0_proj"), 1)
                for t in range(2):
                    for k in range(C):
                        split3(pe, ps[:, 7, t * P:(t + 1) * P], [x[:, k, b, t * P:(t + 1) * P] for x in (xh, xl)],
                               [x[:, (2 * C + k) * P:(2 * C + k + 1) * P] for x in w], k == 0, k == C - 1)
                for k in range(C):
                    mmul = split3(pe, ps[:, 7, 2 * P:2 * P + 2], [x[:, (2 * C + k) * P:(2 * C + k + 1) * P] for x in w],
                                  [x[:, k, b, N - 1:NE] for x in (xh, xl)], k == 0, k == C - 1)
                mmul.then_inc(sem("a0_vt"), 1)
                feature_major(2, 3).then_inc(sem("a0_proj"), 1)

            def scores(mm, j):
                n = mm * U + j
                pe.wait_ge(sem("a0_prep"), n + 1)
                pe.wait_ge(sem("a0_prepg"), n + 1)
                pe.nop(nofuse=True)
                for h in range(2):
                    rows = slice(64 * h, 64 * h + 64)

                    def block(r0, r1, c0, lhs, rhs):
                        return pe.matmul(ps[r0:r1, 4 + h, c0:c0 + rhs.shape[1]], lhs, rhs, start=True, stop=True)

                    for i in range(2):
                        cb = i * SC0
                        for m in range(4):
                            g = 4 * i + m
                            block(32 * m, 32 * m + 16, cb + 32 * m, kA[rows, g, :], q16[rows, 2 * g, :])
                            block(32 * m, 32 * m + 32, cb + 32 * m + 16, kB[rows, g, :], q16[rows, 2 * g + 1, :])
                        for m in range(2):
                            g = 2 * i + m
                            block(64 * m, 64 * m + 32, cb + 64 * m + 32, k32[rows, g, :], q32[rows, g, :])
                        block(0, 64, cb + 64, k64[rows, i, :], q64[rows, i, :])
                    block(0, P, P, k128[rows, 0, :], q128[rows, :])
                    block(0, P, SC0 + P, k128[rows, 1, :], q0[j % 2][rows, 2 * P:N]).then_inc(sem("a0_s"), 1)

            def mix(mm, j):
                n = mm * U + j
                pe.wait_ge(sem("a0_vsb"), n + 1)
                pe.wait_ge(sem("a0_added"), n + 1)
                pe.nop(nofuse=True)
                pe.matmul(ps[:, 3, 0:1], const("headones"), lastp[:, j % 2:j % 2 + 1], start=True, stop=True).then_inc(sem("a0_last"), 1)
                for h in range(2):
                    pe.wait_ge(sem("a0_at"), 2 * n + h + 1)
                    o, v = ps[64 * h:64 * h + 64, 6, :], vt0[j % 2][:, :, 64 * h:64 * h + 64]
                    pe.matmul(o[:, 0:N], v[:, 0, :], at0[h][:, 0:SC0], start=True, stop=False)
                    mmul = pe.matmul(o[:, P:N], v[:, 1, :], at0[h][:, SC0:SCW], start=False, stop=True)
                mmul.then_inc(sem("a0_o"), 1)

            def output(mm, j):
                pe.wait_ge(sem("a0_og"), mm * U + j + 1)
                for d in range(C):
                    mmul = pe.matmul(ps[:, 3 + 3 * d, 0:N], w0[j // B][:, 1024 + d * P:1024 + (d + 1) * P], og0, start=True, stop=True)
                mmul.then_inc(sem("a0_y"), 1)

            def body(mm, last):
                for j in range(U):
                    mix(mm, j)
                    if j + 1 < U or not last:
                        scores(mm, j + 1)
                    output(mm, j)
                    if j + 2 < U or not last:
                        project(mm, j + 2)

            project(0, 0)
            scores(0, 0)
            project(0, 1)
            with pe.Fori(0, LOOPS) as mm:
                body(mm, False)
            body(LOOPS, True)

        def a0_act(act):
            n0a.act(act)
            n0b.act(act)
            act.wait_ge(sem("a0_lg"), 2)
            act.activation(lga[:, 1, :], lga[:, 0, :], ACT.Exp).then_inc(sem("a0_lga"), 1)
            act.wait_ge(sem("a0_lga"), 1)
            act.activation(lga[:, 2, :], lga[:, 1, :], ACT.Ln, bias=1.0).then_inc(sem("a0_lga"), 1)
            act.wait_ge(*n0b.done())
            split_tokens_act(act, sem("split_xh"))

            def split(pair, s):
                act.wait_ge(sem(f"a0_w{s}"), 16 * pair + 16)
                act.copy(wh[s][:, :], w0[s][:, 0:4 * C * P]).then_inc(sem("split_wh"), 1)

            split(0, 0)
            act.wait_ge(sem("a0_lg"), 4)
            for m in range(HP):
                act.activation(powt[:, m, :], const("expo")[:, 0:NEXP], ACT.Exp, scale=lga[:, 3, m:m + 1])
                ins = act.activation(powr[:, m, :], const("expo_r"), ACT.Exp, scale=lga[:, 3, m:m + 1])
                ins.then_inc(sem("a0_pow"), 1)

            def body(mm, last):
                for j in range(U):
                    n, w = mm * U + j, w0[j // B]
                    act.wait_ge(sem("a0_proj"), 2 * n + 1)
                    act.activation(q0[j % 2], ps[:, 0, 0:N], ACT.Identity, bias=w[:, 1280:1281])
                    act.activation(k0[j % 2], ps[:, 1, 0:N], ACT.Identity, bias=w[:, 1281:1282]).then_inc(sem("a0_qk"), 1)
                    act.wait_ge(sem("a0_proj"), 2 * n + 2)
                    act.activation(g0[j % 2], ps[:, 2, 0:N], ACT.Silu, bias=w[:, 1283:1284]).then_inc(sem("a0_vg"), 1)
                    if j % B == 1 and not (last and j > B):
                        split(mm + j // B, 1 - j // B)

            with act.Fori(0, LOOPS) as mm:
                body(mm, False)
            body(LOOPS, True)

        def a0_dve(dve):
            n0a.dve(dve)
            n0b.dve(dve)
            dve.tensor_scalar(lga[:, 0, :], vec("alpha"), -1.0, None, ALU.mult).then_inc(sem("a0_lg"), 1)
            dve.wait_ge(sem("a0_lg"), 1)
            dve.tensor_tensor(lga[:, 0, :], lga[:, 0, :], vec("alpha"), ALU.min).then_inc(sem("a0_lg"), 1)
            dve.tensor_scalar(lga[:, 3, :], vec("alpha"), 0.0, None, ALU.min).then_inc(sem("a0_lg"), 1)
            dve.wait_ge(sem("a0_lga"), 2)
            dve.wait_ge(sem("a0_lg"), 3)
            dve.tensor_tensor(lga[:, 3, :], lga[:, 3, :], lga[:, 2, :], ALU.subtract).then_inc(sem("a0_lg"), 1)
            dve.wait_ge(*n0b.done())
            for c in range(C):
                dve.scalar_tensor_tensor(HT[:, c, :], XN[:, c, :], vec("bO0")[:, c:c + 1], HT[:, c, :], ALU.add, ALU.add).then_inc(sem("a0_res"), 1)
            for h in range(2):
                dve.memset(at0[h], 0.0).then_inc(sem("a0_zero"), 1)
            dve.memset(ps[:, 4:6, 0:SCW], 0.0).then_inc(sem("a0_added"), 1)
            dve.wait_ge(sem("split_xh"), 1)
            split_tokens_dve(dve, sem("split_xl"))

            def split(n, s):
                dve.wait_ge(sem("split_wh"), n + 1)
                dve.tensor_tensor(wl[s][:, :], w0[s][:, 0:4 * C * P], wh[s][:, :].bitcast(f32), ALU.subtract).then_inc(sem("split_wl"), 1)

            split(0, 0)
            dve.wait_ge(sem("a0_zero"), 2)
            dve.wait_ge(sem("a0_res"), C)
            dve.wait_ge(sem("a0_pow"), HP)

            def prep(mm, j):
                n, b = mm * U + j, j % B
                up, down = tab[:, 0, :], tab[:, 1, :]
                dve.wait_ge(sem("a0_qk"), n + 1)
                if b == 0:
                    m = 2 * mm + j // B
                    dve.nop(nofuse=True)
                    dve.tensor_copy(up, powt[:, bass.ds(m, 1), :].rearrange("p a e -> p (a e)")).then_inc(sem("a0_tab"), 1)
                    dve.tensor_copy(down, powr[:, bass.ds(m, 1), :].rearrange("p a e -> p (a e)")).then_inc(sem("a0_tab"), 1)
                    dve.wait_ge(sem("a0_tab"), 2 * m + 2)
                q, k = q0[j % 2], k0[j % 2]

                def view(x, n):
                    return x[:, 0:2 * P].rearrange("p (a b) -> p a b", b=n)

                dve.tensor_tensor(lastp[:, j % 2:j % 2 + 1], q[:, N - 1:N], k[:, N - 1:N], ALU.mult)
                dve.tensor_tensor(q16, view(q, 16), over(up[:, E0 - 8:E0 + 8], 16), ALU.mult)
                dve.tensor_tensor(kA, view(k, 32)[:, :, 0:16], over(down[:, R(8):R(8) + 16], 8), ALU.mult)
                dve.tensor_tensor(kB, view(k, 32), over(down[:, R(24):R(24) + 32], 8), ALU.mult)
                dve.tensor_tensor(q32, view(q, 64)[:, :, 32:64], over(up[:, E0:E0 + 32], 4), ALU.mult)
                dve.tensor_tensor(k32, view(k, 64)[:, :, 0:32], over(down[:, R(32):R(32) + 32], 4), ALU.mult).then_inc(sem("a0_prep"), 1)

            def tokens(mm, j):
                dve.wait_ge(sem("a0_vt"), mm * U + j + 1)
                w = w0[(j // B) % 2]
                bv = w[:, 1284:1284 + P]
                dve.tensor_scalar(vl0[:, j % 2:j % 2 + 1], ps[:, 7, 2 * P:2 * P + 1], w[:, 1282:1283], None, ALU.add)
                dve.tensor_tensor(vt0[j % 2], ps[:, 7, 0:2 * P].rearrange("p (a b) -> p a b", b=P), over(bv, 2), ALU.add)\
                    .then_inc(sem("a0_vsb"), 1)

            def mask(mm, j):
                for h in range(2):
                    dve.wait_ge(sem("a0_s"), 2 * (mm * U + j) + h + 1)
                    dve.nop(nofuse=True)
                    dve.copy_predicated(at0[h], const("causal").bitcast(u32), ps[:, 4 + h, 0:SCW]).then_inc(sem("a0_at"), 1)

            def gate(mm, j):
                n, g = mm * U + j, g0[j % 2]
                dve.wait_ge(sem("a0_last"), n + 1)
                dve.tensor_tensor(lastv, vl0[:, j % 2:j % 2 + 1], ps[:, 3, 0:1], ALU.mult).then_inc(sem("a0_lastv"), 1)
                dve.wait_ge(sem("a0_o"), n + 1)
                dve.wait_ge(sem("a0_vg"), n + 1)
                dve.tensor_tensor(og0[:, 0:N - 1], ps[:, 6, 0:N - 1], g[:, 0:N - 1], ALU.mult)
                dve.wait_ge(sem("a0_lastv"), n + 1)
                dve.scalar_tensor_tensor(og0[:, N - 1:N], ps[:, 6, N - 1:N], lastv, g[:, N - 1:N], ALU.add, ALU.mult).then_inc(sem("a0_og"), 1)

            def add(mm, j):
                h = HT[:, :, (j % B) * N:(j % B + 1) * N]
                dve.wait_ge(sem("a0_y"), mm * U + j + 1)
                for d in range(C):
                    ins = dve.tensor_tensor(h[:, d, :], h[:, d, :], ps[:, 3 + 3 * d, 0:N], ALU.add)
                ins.then_inc(sem("a0_added"), 1)

            def body(mm, last):
                for j in range(U):
                    gate(mm, j)
                    if j + 1 < U or not last:
                        mask(mm, j + 1)
                    add(mm, j)
                    if j + 2 < U or not last:
                        prep(mm, j + 2)
                        tokens(mm, j + 2)
                    if j % B == 1 and not (last and j > B):
                        split(2 * mm + j // B + 1, 1 - j // B)

            prep(0, 0)
            tokens(0, 0)
            mask(0, 0)
            prep(0, 1)
            tokens(0, 1)
            with dve.Fori(0, LOOPS) as mm:
                body(mm, False)
            body(LOOPS, True)

        def a0_pool(pool):
            with pool.Fori(0, HP // 2) as mm:
                base = mm * U
                for j in range(U):
                    pool.wait_ge(sem("a0_qk"), base + j + 1)
                    if j % B == 0:
                        pool.wait_ge(sem("a0_tab"), 4 * mm + 2 * (j // B) + 2)
                    q, k = q0[j % 2], k0[j % 2]
                    up, down = tab[:, 0, :], tab[:, 1, :]
                    pool.tensor_tensor(q64, q[:, 0:2 * P].rearrange("p (a b) -> p a b", b=P)[:, :, 64:P], over(up[:, E0:E0 + 64], 2), ALU.mult)
                    pool.tensor_tensor(k64, k[:, 0:2 * P].rearrange("p (a b) -> p a b", b=P)[:, :, 0:64], over(down[:, R(64):R(64) + 64], 2), ALU.mult)
                    pool.tensor_tensor(q128, q[:, P:N], up[:, E0:E0 + P + 1], ALU.mult)
                    pool.tensor_tensor(k128, k[:, 0:2 * P].rearrange("p (a b) -> p a b", b=P), over(down[:, R(P):R(P) + P], 2), ALU.mult)\
                        .then_inc(sem("a0_prepg"), 1)

        h_a0 = [(sem("a0_added"), HP * B + 1)]

        at_ = 0

        def take(name, shape, dtype=f32):
            nonlocal at_
            t, at_ = at(name, shape, at_, dtype)
            return t

        wu = [[take(f"wu{s}{x}", [2 * 8 * P], fr) for x in ("hi", "lo")] for s in range(2)]
        wd = [[take(f"wd{s}{x}", [8 * D], fr) for x in ("hi", "lo")] for s in range(2)]
        xs = [take(f"xs{x}", [C, T], fr) for x in ("hi", "lo")]
        hid = [[take(f"hid{u}{x}", [8, CW], fr) for x in ("hi", "lo")] for u in range(2)]
        raw_h = take("raw_h", [4, CW])
        sig = take("sig", [2, CW])
        scaled = [take(f"scaled{u}", [C, CW]) for u in range(2)]
        bias = [take(f"bias{s}", [16]) for s in range(2)]
        cwt = take("cwt", [T])
        wr = take("wr", [C, 40])
        lg, prob, cw = take("lg", [NT, 40]), take("prob", [NT, 40]), take("cw", [NT, 40])
        vals, repl = take("vals", [NT, 48]), take("repl", [NT, 48])
        top8, red = take("top8", [NT, 8]), take("red", [4, NT])
        grp, grpr = take("grp", [NT, 10]), take("grpr", [NT, 10])
        assert region + 4 * at_ <= nc.sbuf_usable_end
        raw_up = XN2[:, :, :].rearrange("p c t -> p (c t)")
        raw_dn = XC[:, :, :].rearrange("p c t -> p (c t)")
        cwb = [w[:, 0:T] for w in watt]

        def mm3(pe, out, w, x, first, last):
            for n, (i, j) in enumerate(((0, 0), (0, 1), (1, 0))):
                mm = pe.matmul(out, w[i], x[j], start=(first and n == 0), stop=(last and n == 2))
            return mm

        class Units:
            def __init__(self, f, i, s, c):
                self.f, self.i, self.s, self.c = f, i, s, c
                self.n = 6 * i + 3 * s + c
                self.par = (3 * s + c) % 2

            def expert(self):
                return 2 * self.i + self.s

            def last(self):
                return isinstance(self.i, int) and 2 * self.i + self.s == self.f.units - 1

            def next(self):
                if self.c + 1 < NC:
                    return Units(self.f, self.i, self.s, self.c + 1)
                return Units(self.f, self.i + self.s, 1 - self.s, 0)

            def tile(self, m):
                return self.n * self.f.mt + m, ((3 * self.s + self.c) * self.f.mt + m) % self.f.depth

        def sweep(eng, f, hidden, outputs, after_first=None):
            loops = (f.units - 1) // 2
            hidden(Units(f, 0, 0, 0))
            if after_first:
                after_first()
            with eng.Fori(0, loops) as i:
                for s in range(2):
                    for c in range(NC):
                        u = Units(f, i, s, c)
                        hidden(u.next())
                        outputs(u)
            rest = f.units - 2 * loops
            for s in range(rest):
                for c in range(NC):
                    u = Units(f, loops, s, c)
                    if s < rest - 1 or c < NC - 1:
                        hidden(u.next())
                    outputs(u)

        class Layer:
            def __init__(self, f, ready, src=None):
                self.f, self.p = f, f.name
                self.norm = Norm(HT, XN, ready)
                self.rows = {"f0": 9, "f1": 16, "f2": 33, "f3": 8}[f.name]
                self.experts = {"f0": 8, "f1": 16, "f2": 40, "f3": 8}[f.name]
                self.cwd = nc.dram_tensor(f"cw_{f.name}", (self.rows, T), f32, kind="Internal").ap()
                self.extra = 1 if f.name == "f2" else 0
                self.index = FFNS.index(f)
                Layer.all.append(self)

            all = []
            steps = 0

            def sem(self, n):
                return sem(f"ff_{n}")

            def counts(self, n):
                u = self.f.units
                tiles, units = NC * u * self.f.mt, NC * (u + self.extra)
                return {"upraw": 16 * u, "dnraw": 16 * u, "cw0": 16 * ((u + 1) // 2 + self.extra), "cw1": 16 * (u // 2),
                        "wuhi": u, "wdhi": u, "wu": u, "wd": u, "hps": tiles, "sig": tiles * self.f.gated,
                        "got": tiles, "hhi": tiles, "hid": tiles, "out": NC * u,
                        "taken": units, "added": units, "xs": 2}[n]

            def at(self, n, v):
                return self.sem(n), sum(x.counts(n) for x in Layer.all[:self.index]) + v

            def once(self, n, v):
                each = {"wr": 16, "logits": 1, "shifted": 1, "prob": 1, "cw": 1, "cwps": 1, "cwt": 3, "cwd": 16}[n]
                before = self.index
                if n == "shifted":
                    before = self.index // 2
                return sem(f"route_{n}"), each * before + v

            def done(self):
                return [self.at("added", 2 + NC * (self.f.units + self.extra))]

            def load_up(self, sp, src):
                sp.dma_start(raw_up[:, 0:self.f.up_words], src).then_inc(self.sem("upraw"), 16)

            def load_dn(self, sp, src):
                sp.dma_start(raw_dn[:, 0:self.f.dn_w], src).then_inc(self.sem("dnraw"), 16)

            def load_cw(self, sp, src, s):
                sp.dma_start(cwb[s], src.broadcast_to([P, T])).then_inc(self.sem(f"cw{s}"), 16)

            def sp(self, sp):
                for sm, v in self.norm.ready(0):
                    sp.wait_ge(sm, v)
                sp.dma_start(wr[:, :, 0:self.experts], dram["wr_" + self.p]).then_inc(sem("route_wr"), 16)
                self.load_up(sp, dram["up_" + self.p][0])
                sp.wait_ge(*self.norm.done())
                self.load_dn(sp, dram["dn_" + self.p][0])
                sp.wait_ge(*self.once("cwt", 3))
                sp.dma_start(self.cwd, cwt[0:self.rows, :]).then_inc(sem("route_cwd"), 16)
                sp.wait_ge(*self.once("cwd", 16))
                self.load_cw(sp, self.cwd[0:1, :], 0)

                def more(g, i, s):
                    sp.wait_ge(*self.at("wu", g))
                    self.load_up(sp, dram["up_" + self.p][bass.ds(g, 1), :, :].rearrange("a p w -> p (a w)"))
                    sp.wait_ge(*self.at("wd", g))
                    self.load_dn(sp, dram["dn_" + self.p][bass.ds(g, 1), :, :].rearrange("a p w -> p (a w)"))
                    if not (isinstance(g, int) and g == 1):
                        sp.wait_ge(*self.at("taken", 2 + 6 * i + 3 * s - 3))
                    self.load_cw(sp, self.cwd[bass.ds(g, 1), :], s)

                more(1, 0, 1)
                pairs = self.f.units // 2
                with sp.Fori(1, pairs) as i:
                    for s in range(2):
                        more(2 * i + s, i, s)
                if self.f.units % 2:
                    more(2 * pairs, pairs, 0)
                if self.extra:
                    sp.wait_ge(*self.at("taken", 2 + NC * (self.f.units - 1)))
                    self.load_cw(sp, self.cwd[self.f.units:self.f.units + 1, :], 0)

            def pe(self, pe):
                f = self.f
                self.norm.pe(pe)
                pe.wait_ge(*self.norm.done())
                pe.wait_ge(*self.once("wr", 16))
                for j, t0 in enumerate(TILES):
                    for k in range(C):
                        mm = pe.matmul(ps[:, 4, j * 40:j * 40 + self.experts], XN[:, k, t0:t0 + P], wr[:, k, 0:self.experts],
                                       start=(k == 0), stop=(k == C - 1))
                mm.then_inc(sem("route_logits"), 1)
                pe.wait_ge(*self.at("xs", 2))

                def turn():
                    pe.wait_ge(*self.once("cw", 1))
                    for j in range(NT):
                        mm = pe.transpose(ps[0:self.rows, 5 + j // 4, (j % 4) * P:(j % 4 + 1) * P], cw[:, j, 0:self.rows], ident)
                    mm.then_inc(sem("route_cwps"), 1)

                def hidden(u):
                    if u.c == 0:
                        pe.wait_ge(*self.at("wu", u.expert() + 1))
                    t0, w = CHUNKS[u.c]
                    for m in range(f.mt):
                        t, slot = u.tile(m)
                        pe.wait_ge(*self.at("got", 4 - f.depth + t + 1))
                        for a in range(f.up_mats):
                            for k in range(C):
                                col = ((a * C + k) * f.mt + m) * P
                                mm = mm3(pe, ps[:, slot * f.psums + a, 0:w], [x[:, col:col + P] for x in wu[u.s]],
                                         [x[:, k, t0:t0 + w] for x in xs], k == 0, k == C - 1)
                        mm.then_inc(self.sem("hps"), 1)

                def outputs(u):
                    if u.c == 0:
                        pe.wait_ge(*self.at("wd", u.expert() + 1))
                    w = CHUNKS[u.c][1]
                    if u.s == 0 and u.c == 0:
                        pe.wait_ge(*self.once("cwt", 3))
                    pe.wait_ge(*self.at("taken", u.n + 1))
                    pe.wait_ge(*self.at("hid", 4 + (u.n + 1) * f.mt))
                    for d in range(C):
                        for m in range(f.mt):
                            col = m * D + d * P
                            mm = mm3(pe, ps[:, 4 + 2 * u.par + d, 0:w], [x[:, col:col + P] for x in wd[u.s]],
                                     [x[:, m, 0:w] for x in hid[u.par]], m == 0, m == f.mt - 1)
                    mm.then_inc(self.sem("out"), 1)

                sweep(pe, f, hidden, outputs, turn)

            def split_act(self, act, g, c, spare=None):
                s, raw, words, name = (g[1], raw_up, self.f.up_w, "wu") if c == 0 else (g[1], raw_dn, self.f.dn_w, "wd")
                g = g[0]
                act.wait_ge(*self.at("upraw" if c == 0 else "dnraw", 16 * g + 16))
                if spare is not None:
                    act.wait_ge(*spare)
                act.copy((wu if c == 0 else wd)[s][0][:, 0:words], raw[:, 0:words]).then_inc(self.sem(name + "hi"), 1)

            def split_dve(self, dve, g, c):
                s, raw, words, name = (g[1], raw_up, self.f.up_w, "wu") if c == 0 else (g[1], raw_dn, self.f.dn_w, "wd")
                g = g[0]
                dve.wait_ge(*self.at(name + "hi", g + 1))
                hi, lo = (wu if c == 0 else wd)[s]
                if c == 0 and self.f.biases:
                    dve.tensor_copy(bias[s][:, 0:self.f.biases], raw[:, words:words + self.f.biases])
                dve.tensor_tensor(lo[:, 0:words], raw[:, 0:words], hi[:, 0:words].bitcast(f32), ALU.subtract).then_inc(self.sem(name), 1)

            def act(self, act):
                f = self.f
                self.norm.act(act)
                act.wait_ge(*self.norm.done())
                act.copy(xs[0][:, :, :], XN[:, :, :]).then_inc(self.sem("xs"), 1)
                self.split_act(act, (0, 0), 0)
                self.route_act(act)
                self.split_act(act, (0, 0), 1)
                if self.index == 0:
                    act.sem_inc(self.sem("got"), 4)
                func = ACT.Silu if f.act == "Silu" else ACT.Relu

                def hidden(u):
                    w = CHUNKS[u.c][1]
                    if u.c == 0 and f.biases:
                        act.wait_ge(*self.at("wu", u.expert() + 1))
                    for m in range(f.mt):
                        t, slot = u.tile(m)
                        act.wait_ge(*self.at("hps", t + 1))
                        b = bias[u.s][:, m:m + 1] if f.has_bias else 0.0
                        if f.gated:
                            act.activation(sig[:, slot, 0:w], ps[:, slot * 2, 0:w], func, bias=b).then_inc(self.sem("sig"), 1)
                        else:
                            act.wait_ge(*self.at("hid", t + 1))
                            act.activation(raw_h[:, slot, 0:w], ps[:, slot, 0:w], func, bias=b).then_inc(self.sem("got"), 1)

                def ahead(u):
                    if u.c < 2 and not u.last():
                        self.split_act(act, (u.expert() + 1, 1 - u.s), u.c, self.at("taken", 2 + NC * u.expert()))

                sweep(act, f, hidden, ahead)

            def dve(self, dve):
                f = self.f
                self.norm.dve(dve)
                dve.wait_ge(*self.at("xs", 1))
                dve.tensor_tensor(xs[1][:, :, :], XN[:, :, :], xs[0][:, :, :].bitcast(f32), ALU.subtract).then_inc(self.sem("xs"), 1)
                self.split_dve(dve, (0, 0), 0)
                if self.index == 0:
                    dve.sem_inc(self.sem("taken"), 2)
                    dve.sem_inc(self.sem("hid"), 4)
                self.route_dve(dve)
                self.split_dve(dve, (0, 0), 1)

                def turned():
                    dve.wait_ge(*self.once("cwps", 1))
                    for n in range(2):
                        dve.tensor_copy(cwt[0:self.rows, 4 * P * n:4 * P * (n + 1)], ps[0:self.rows, 5 + n, 0:4 * P]).then_inc(sem("route_cwt"), 1)
                    dve.tensor_copy(cwt[0:self.rows, 8 * P:T], ps[0:self.rows, 7, P - (T - 8 * P):P]).then_inc(sem("route_cwt"), 1)

                def hidden(u):
                    w = CHUNKS[u.c][1]
                    for m in range(f.mt):
                        t, slot = u.tile(m)
                        if f.gated:
                            dve.wait_ge(*self.at("sig", t + 1))
                            x = ps[:, slot * 2 + 1, 0:w]
                            raw = raw_h[:, slot, 0:w]
                            if f.has_bias:
                                ins = dve.scalar_tensor_tensor(raw, x, bias[u.s][:, f.mt + m:f.mt + m + 1], sig[:, slot, 0:w], ALU.add, ALU.mult)
                            else:
                                ins = dve.tensor_tensor(raw, x, sig[:, slot, 0:w], ALU.mult)
                            ins.then_inc(self.sem("got"), 1)
                        raw = raw_h[:, slot, 0:w]
                        hi, lo = (x[:, m, 0:w] for x in hid[u.par])
                        dve.wait_ge(*self.at("got", 4 + t + 1))
                        dve.tensor_copy(hi, raw).then_inc(self.sem("hhi"), 1)
                        dve.wait_ge(*self.at("hhi", t + 1))
                        dve.tensor_tensor(lo, raw, hi.bitcast(f32), ALU.subtract).then_inc(self.sem("hid"), 1)

                def outputs(u):
                    t0, w = CHUNKS[u.c]
                    if u.c == 0:
                        dve.wait_ge(*self.at(f"cw{u.s}", 16 * u.i + 16))
                    dve.wait_ge(*self.at("added", u.n + 1))
                    dve.wait_ge(*self.at("out", u.n + 1))
                    o, src, k = scaled[u.par], ps[:, 4 + 2 * u.par:6 + 2 * u.par, 0:w], cwb[u.s][:, t0:t0 + w]
                    if f.has_bias:
                        for d in range(C):
                            b = bias[u.s][:, f.up_mats * f.mt + d:f.up_mats * f.mt + d + 1]
                            ins = dve.scalar_tensor_tensor(o[:, d, 0:w], src[:, d, :], b, k, ALU.add, ALU.mult)
                    else:
                        ins = dve.tensor_tensor(o[:, :, 0:w], src, over(k, C), ALU.mult)
                    ins.then_inc(self.sem("taken"), 1)
                    if u.c < 2 and not u.last():
                        self.split_dve(dve, (u.expert() + 1, 1 - u.s), u.c)

                sweep(dve, f, hidden, outputs, turned)
                if self.extra:
                    dve.wait_ge(*self.at("cw0", 16 * (f.units // 2) + 16))
                    for c, (t0, w) in enumerate(CHUNKS):
                        u = NC * f.units + c
                        dve.wait_ge(*self.at("added", u + 1))
                        dve.tensor_tensor(scaled[u % 2][:, :, 0:w], XN[:, :, t0:t0 + w], over(cwb[0][:, t0:t0 + w], C), ALU.mult)\
                            .then_inc(self.sem("taken"), 1)

            def pool(self, pool):
                if self.index == 0:
                    pool.sem_inc(self.sem("added"), 2)

                def outputs(u):
                    t0, w = CHUNKS[u.c]
                    pool.wait_ge(*self.at("added", u.n + 2))
                    pool.wait_ge(*self.at("taken", u.n + 3))
                    h = HT[:, :, t0:t0 + w]
                    pool.tensor_tensor(h, h, scaled[u.par][:, :, 0:w], ALU.add).then_inc(self.sem("added"), 1)

                sweep(pool, self.f, lambda u: None, outputs)
                for c in range(NC * self.extra):
                    outputs(Units(self.f, self.f.units // 2, 0, c))

            def step(self, dve, ins):
                Layer.steps += 1
                ins.then_inc(sem("route_step"), 1)
                dve.wait_ge(sem("route_step"), Layer.steps)

            def top(self, dve, k, e, v, r):
                s = 8 - k
                for n in range(s):
                    self.step(dve, dve.memset(v[:, :, e + n:e + n + 1], -2e38 - n * 1e37))
                for j in range(NT):
                    ins = dve.max(top8[:, j, :], v[:, j, 0:e + s])
                self.step(dve, ins)
                self.step(dve, dve.tensor_copy(top8[:, :, k:8], v[:, :, e:e + s]))
                for j in range(NT):
                    ins = dve.match_replace(r[:, j, 0:e + s], top8[:, j, :], v[:, j, 0:e + s], 3e38)
                self.step(dve, ins)
                self.step(dve, dve.tensor_tensor(r[:, :, 0:e], r[:, :, 0:e], v[:, :, 0:e], ALU.not_equal))

            def normalise(self, dve, x, e):
                self.step(dve, dve.tensor_reduce(red[:, 1, :], x, AX.X, ALU.add))
                self.step(dve, dve.reciprocal(red[:, 2, :], red[:, 1, :]))
                return dve.tensor_tensor(x, x, spread(red[:, 2, :], e), ALU.mult)

            def route_act(self, act):
                e = self.experts
                if self.p in ("f0", "f2"):
                    act.wait_ge(*self.once("shifted", 1))
                    act.activation(prob[:, :, 0:e], lg[:, :, 0:e], ACT.Exp).then_inc(sem("route_prob"), 1)
                if self.p == "f1":
                    act.wait_ge(*self.once("logits", 1))
                    act.activation(prob[:, :, 0:e], ps[:, 4, 0:NT * 40].rearrange("p (a b) -> p a b", b=40)[:, :, 0:e], ACT.Sigmoid)\
                        .then_inc(sem("route_prob"), 1)

            def route_dve(self, dve):
                e, st = self.experts, self.step
                logits = ps[:, 4, 0:NT * 40].rearrange("p (a b) -> p a b", b=40)[:, :, 0:e]
                pr, v, r, x = prob[:, :, 0:e], vals, repl, cw
                dve.wait_ge(*self.once("logits", 1))
                if self.p in ("f0", "f2"):
                    st(dve, dve.tensor_reduce(red[:, 0, :], logits, AX.X, ALU.max))
                    dve.tensor_tensor(lg[:, :, 0:e], logits, spread(red[:, 0, :], e), ALU.subtract).then_inc(sem("route_shifted"), 1)
                if self.p != "f3":
                    dve.wait_ge(*self.once("prob", 1))
                if self.p == "f0":
                    st(dve, self.normalise(dve, pr, e))
                    st(dve, dve.tensor_copy(v[:, :, 0:e], pr))
                    self.top(dve, 2, e, v, r)
                    st(dve, dve.memset(x[:, :, 0:1], 1.0))
                    st(dve, dve.tensor_tensor(x[:, :, 1:e + 1], pr, r[:, :, 0:e], ALU.mult))
                    last = self.normalise(dve, x[:, :, 1:e + 1], e)
                if self.p == "f1":
                    st(dve, dve.tensor_reduce(grp[:, :, 0:4], pr.rearrange("p a (g b) -> p a g b", b=4), AX.X, ALU.max))
                    for n in range(4):
                        st(dve, dve.memset(grp[:, :, 4 + n:5 + n], -1e38 - n * 1e37))
                    self.top_groups(dve)
                    g4 = grpr[:, :, 0:4].unsqueeze(3).broadcast_to([P, NT, 4, 4])
                    v4 = v[:, :, 0:e].rearrange("p a (g b) -> p a g b", b=4)
                    st(dve, dve.tensor_tensor(v4, pr.rearrange("p a (g b) -> p a g b", b=4), g4, ALU.mult))
                    st(dve, dve.tensor_scalar(grpr[:, :, 0:4], grpr[:, :, 0:4], -1.0, BIG, ALU.add, ALU.mult))
                    st(dve, dve.tensor_tensor(v4, v4, g4, ALU.add))
                    self.top(dve, 4, e, v, r)
                    st(dve, dve.tensor_tensor(x[:, :, 0:e], pr, r[:, :, 0:e], ALU.mult))
                    st(dve, self.normalise(dve, x[:, :, 0:e], e))
                    last = dve.tensor_scalar(x[:, :, 0:e], x[:, :, 0:e], 2.5, None, ALU.mult)
                if self.p == "f2":
                    st(dve, self.normalise(dve, pr, e))
                    st(dve, dve.tensor_tensor(v[:, :, 0:e], pr, over(vec("score_b"), NT), ALU.add))
                    self.top(dve, 6, e, v, r)
                    st(dve, dve.scalar_tensor_tensor(x[:, :, 0:e], pr, 2.5, r[:, :, 0:e], ALU.mult, ALU.mult))
                    st(dve, dve.tensor_reduce(red[:, 0, :], x[:, :, 32:40], AX.X, ALU.add))
                    last = dve.tensor_copy(x[:, :, 32:33], red[:, 0, :].unsqueeze(2))
                if self.p == "f3":
                    st(dve, dve.tensor_tensor(v[:, :, 0:e], logits, over(vec("gate_b"), NT), ALU.add))
                    self.top(dve, 1, e, v, r)
                    last = dve.tensor_copy(x[:, :, 0:e], r[:, :, 0:e])
                last.then_inc(sem("route_cw"), 1)

            def top_groups(self, dve):
                for n in range(2):
                    self.step(dve, dve.memset(grp[:, :, 8 + n:9 + n], -2e38 - n * 1e37))
                for j in range(NT):
                    ins = dve.max(top8[:, j, :], grp[:, j, :])
                self.step(dve, ins)
                self.step(dve, dve.tensor_copy(top8[:, :, 2:8], grp[:, :, 4:10]))
                for j in range(NT):
                    ins = dve.match_replace(grpr[:, j, :], top8[:, j, :], grp[:, j, :], 3e38)
                self.step(dve, ins)
                self.step(dve, dve.tensor_tensor(grpr[:, :, 0:4], grpr[:, :, 0:4], grp[:, :, 0:4], ALU.not_equal))

        f0 = Layer(FFNS[0], lambda c: h_a0)
        h_f0 = f0.done()

        def f0_sp(sp):
            f0.sp(sp)

        def f0_pe(pe):
            f0.pe(pe)

        def f0_act(act):
            f0.act(act)

        def f0_dve(dve):
            f0.dve(dve)

        def f0_pool(pool):
            f0.pool(pool)

        n1a = Norm(HT, XN, lambda c: h_f0)
        n1b = Norm(XN, XN2, lambda c: [n1a.done(c)], centred=False, eps=RMS_EPS)
        ar = Arena()
        w1 = [w[:, 0:A1_W] for w in watt]
        q1, k1 = ([ar.take(N) for _ in range(2)] for _ in range(2))
        sm1 = [ar.take(SCW) for _ in range(2)]
        nmax1 = ar.take(2, 2)
        sum1, rs1 = ar.take(2, 2), ar.take(2, 2)
        at1 = [ar.take(SCW) for _ in range(2)]
        vt1 = [ar.take(2, P) for _ in range(2)]
        vl1 = ar.take(2)
        vs1 = ar.take(2, P)
        og1 = ar.take(N)
        assert ar.at <= a0_end

        def a1_sp(sp):
            sp.wait_ge(*h_f0[0])
            for s in range(2):
                sp.dma_start(w1[s], dram["w_a1"][s]).then_inc(sem(f"a1_w{s}"), 16)
            with sp.Fori(1, HP // 2) as mm:
                for s in range(2):
                    sp.wait_ge(sem("a1_y"), mm * U + (s - 1) * B)
                    sp.dma_start(w1[s], dram["w_a1"][bass.ds(2 * mm + s, 1), :, :].rearrange("a p w -> p (a w)")).then_inc(sem(f"a1_w{s}"), 16)

        def a1_pe(pe):
            n1a.pe(pe)
            n1b.pe(pe)
            pe.wait_ge(sem("split_xl"), 2)

            def project(mm, j):
                n, s, b = mm * U + j, (j // B) % 2, j % B
                if b == 0:
                    pe.wait_ge(sem("split_wl"), HP + 2 * mm + j // B + 1)
                if not (isinstance(n, int) and n == 0):
                    pe.wait_ge(sem("a1_vsb"), n)
                w = (wh[s], wl[s])
                for i in range(2):
                    for k in range(C):
                        mmul = split3(pe, ps[:, i, 0:NE], [x[:, (i * C + k) * P:(i * C + k + 1) * P] for x in w],
                                      [x[:, k, b, :] for x in (xh, xl)], k == 0, k == C - 1)
                mmul.then_inc(sem("a1_proj"), 1)
                for t in range(2):
                    for k in range(C):
                        split3(pe, ps[:, 7, t * P:(t + 1) * P], [x[:, k, b, t * P:(t + 1) * P] for x in (xh, xl)],
                               [x[:, (2 * C + k) * P:(2 * C + k + 1) * P] for x in w], k == 0, k == C - 1)
                for k in range(C):
                    mmul = split3(pe, ps[:, 7, 2 * P:2 * P + 2], [x[:, (2 * C + k) * P:(2 * C + k + 1) * P] for x in w],
                                  [x[:, k, b, N - 1:NE] for x in (xh, xl)], k == 0, k == C - 1)
                mmul.then_inc(sem("a1_vt"), 1)

            def scores(mm, j):
                pe.wait_ge(sem("a1_qk"), mm * U + j + 1)
                for h in range(2):
                    rows = slice(64 * h, 64 * h + 64)
                    q, k = q1[j % 2][rows, :], k1[j % 2][rows, :]
                    pe.matmul(ps[:, 4 + h, 0:SC0], k[:, 0:P], q, start=True, stop=True)
                    pe.matmul(ps[:, 4 + h, SC0:SCW], k[:, P:2 * P], q[:, P:N], start=True, stop=True).then_inc(sem("a1_s"), 1)

            def mix(mm, j):
                n = mm * U + j
                pe.wait_ge(sem("a1_added"), n + 1)
                pe.wait_ge(sem("a1_vs"), n + 1)
                for h in range(2):
                    o = ps[64 * h:64 * h + 64, 6, :]
                    pe.matmul(o[:, 0:N], vs1[:, 0, 64 * h:64 * h + 64], at1[h][:, 0:SC0], start=True, stop=False)
                    mmul = pe.matmul(o[:, P:N], vs1[:, 1, 64 * h:64 * h + 64], at1[h][:, SC0:SCW], start=False, stop=True)
                mmul.then_inc(sem("a1_o"), 1)

            def output(mm, j):
                pe.wait_ge(sem("a1_og"), mm * U + j + 1)
                for d in range(C):
                    mmul = pe.matmul(ps[:, 3 + 3 * d, 0:N], w1[j // B][:, 768 + d * P:768 + (d + 1) * P], og1, start=True, stop=True)
                mmul.then_inc(sem("a1_y"), 1)

            def body(mm, last):
                for j in range(U):
                    mix(mm, j)
                    if j + 1 < U or not last:
                        scores(mm, j + 1)
                    output(mm, j)
                    if j + 2 < U or not last:
                        project(mm, j + 2)

            project(0, 0)
            scores(0, 0)
            project(0, 1)
            with pe.Fori(0, LOOPS) as mm:
                body(mm, False)
            body(LOOPS, True)

        def a1_act(act):
            n1a.act(act)
            n1b.act(act)
            act.wait_ge(*n1b.done())
            split_tokens_act(act, sem("split_xh"))

            def split(pair, s):
                act.wait_ge(sem(f"a1_w{s}"), 16 * pair + 16)
                act.copy(wh[s][:, 0:3 * C * P], w1[s][:, 0:3 * C * P]).then_inc(sem("split_wh"), 1)

            def take(mm, j):
                w = w1[(j // B) % 2]
                act.wait_ge(sem("a1_proj"), mm * U + j + 1)
                act.activation(q1[j % 2], ps[:, 0, 0:N], ACT.Identity, bias=w[:, 1024:1025])
                act.activation(k1[j % 2], ps[:, 1, 0:N], ACT.Identity, bias=w[:, 1025:1026]).then_inc(sem("a1_qk"), 1)

            def exps(mm, j):
                for h in range(2):
                    act.wait_ge(sem("a1_max"), 2 * (mm * U + j) + h + 1)
                    for i, (a, b) in enumerate(((0, SC0), (SC0, SCW))):
                        e = act.activation(at1[h][:, a:b], sm1[h][:, a:b], ACT.Exp, bias=nmax1[:, h, i:i + 1],
                                           accum_out=sum1[:, h, i:i + 1])
                    e.then_inc(sem("a1_exp"), 1)

            def body(mm, last):
                for j in range(U):
                    if j + 1 < U or not last:
                        exps(mm, j + 1)
                    if j + 2 < U or not last:
                        take(mm, j + 2)
                    if j % B == 1 and not (last and j > B):
                        split(mm + j // B, 1 - j // B)

            split(0, 0)
            take(0, 0)
            exps(0, 0)
            take(0, 1)
            with act.Fori(0, LOOPS) as mm:
                body(mm, False)
            body(LOOPS, True)

        def a1_dve(dve):
            n1a.dve(dve)
            n1b.dve(dve)
            dve.wait_ge(*n1b.done())
            for c in range(C):
                h = HT[:, c, :]
                dve.tensor_scalar(h, h, vec("bO1")[:, c:c + 1], None, ALU.add).then_inc(sem("a1_bias"), 1)
            dve.wait_ge(sem("a1_bias"), C)
            dve.sem_inc(sem("a1_added"), 1)
            dve.wait_ge(sem("split_xh"), 2)
            split_tokens_dve(dve, sem("split_xl"))

            def split(n, s):
                dve.wait_ge(sem("split_wh"), HP + n + 1)
                w = slice(0, 3 * C * P)
                dve.tensor_tensor(wl[s][:, w], w1[s][:, w], wh[s][:, w].bitcast(f32), ALU.subtract).then_inc(sem("split_wl"), 1)

            def tokens(mm, j):
                dve.wait_ge(sem("a1_vt"), mm * U + j + 1)
                w = w1[(j // B) % 2]
                dve.tensor_scalar(vl1[:, j % 2:j % 2 + 1], ps[:, 7, 2 * P:2 * P + 1], w[:, 1026:1027], None, ALU.add)
                dve.tensor_tensor(vt1[j % 2], ps[:, 7, 0:2 * P].rearrange("p (a b) -> p a b", b=P), over(w[:, 1027:1027 + P], 2), ALU.add)\
                    .then_inc(sem("a1_vsb"), 1)

            def hide(mm, j):
                for h in range(2):
                    n = 2 * (mm * U + j) + h
                    dve.wait_ge(sem("a1_s"), n + 1)
                    dve.tensor_tensor(sm1[h], ps[:, 4 + h, 0:SCW], const("hide"), ALU.add).then_inc(sem("a1_hid"), 1)
                    dve.wait_ge(sem("a1_hid"), n + 1)
                    dve.tensor_reduce(nmax1[:, h, 0:1], sm1[h][:, 0:SC0], AX.X, ALU.max, negate=True)
                    dve.tensor_reduce(nmax1[:, h, 1:2], sm1[h][:, SC0:SCW], AX.X, ALU.max, negate=True).then_inc(sem("a1_max"), 1)

            def values(mm, j):
                n = mm * U + j + 1
                dve.wait_ge(sem("a1_vsb"), n)
                dve.wait_ge(sem("a1_exp"), 2 * n)
                dve.reciprocal(rs1, sum1).then_inc(sem("a1_rs"), 1)
                dve.wait_ge(sem("a1_rs"), n)
                for h in range(2):
                    c = slice(64 * h, 64 * h + 64)
                    ins = dve.tensor_tensor(vs1[:, :, c], vt1[j % 2][:, :, c], spread(rs1[:, h, :], 64), ALU.mult)
                ins.then_inc(sem("a1_vs"), 1)

            def take(mm, j):
                dve.wait_ge(sem("a1_o"), mm * U + j + 1)
                dve.tensor_copy(og1[:, 0:N - 1], ps[:, 6, 0:N - 1])
                dve.tensor_tensor(og1[:, N - 1:N], ps[:, 6, N - 1:N], vl1[:, j % 2:j % 2 + 1], ALU.add).then_inc(sem("a1_og"), 1)

            def add(mm, j):
                h = HT[:, :, (j % B) * N:(j % B + 1) * N]
                dve.wait_ge(sem("a1_y"), mm * U + j + 1)
                for d in range(C):
                    ins = dve.tensor_tensor(h[:, d, :], h[:, d, :], ps[:, 3 + 3 * d, 0:N], ALU.add)
                ins.then_inc(sem("a1_added"), 1)

            def body(mm, last):
                for j in range(U):
                    take(mm, j)
                    if j + 1 < U or not last:
                        hide(mm, j + 1)
                    add(mm, j)
                    if j + 1 < U or not last:
                        values(mm, j + 1)
                    if j + 2 < U or not last:
                        tokens(mm, j + 2)
                    if j % B == 1 and not (last and j > B):
                        split(2 * mm + j // B + 1, 1 - j // B)

            split(0, 0)
            tokens(0, 0)
            hide(0, 0)
            values(0, 0)
            tokens(0, 1)
            with dve.Fori(0, LOOPS) as mm:
                body(mm, False)
            body(LOOPS, True)

        h_a1 = [(sem("a1_added"), HP * B + 1)]

        f1 = Layer(FFNS[1], lambda c: h_a1)
        h_f1 = f1.done()

        def f1_sp(sp):
            f1.sp(sp)

        def f1_pe(pe):
            f1.pe(pe)

        def f1_act(act):
            f1.act(act)

        def f1_dve(dve):
            f1.dve(dve)

        def f1_pool(pool):
            f1.pool(pool)

        n2 = Norm(HT, XN, lambda c: h_f1)
        ar = Arena()
        H4 = 4
        w2 = [w[:, 0:A2_W] for w in watt]
        q2, k2, v2 = ([ar.take(N) for _ in range(2)] for _ in range(3))
        pr2 = [ar.take(H4, N) for _ in range(2)]
        mx2, nm2 = ar.take(2, H4), ar.take(2, H4)
        sm2, rs2 = ar.take(2, H4), ar.take(2, H4)
        pt2 = ar.take(2, H4 * N)
        vt2 = [ar.take(2, P) for _ in range(2)]
        ql2 = ar.take(H4)
        vl2 = ar.take(H4)
        pl2 = ar.take(N, rows=H4)
        ml2 = ar.take(4, rows=H4)
        pk2 = [ar.take(N, rows=H4) for _ in range(2)]
        vr2 = [ar.take(P, rows=H4) for _ in range(2)]
        os2 = ar.take(N)
        QS = 1.0 / 16
        pt2v = pt2.rearrange("p t (h q) -> p t h q", q=N)
        UA2 = 2 * B

        def a2_sp(sp):
            sp.wait_ge(*h_f1[0])
            for s in range(2):
                sp.dma_start(w2[s], dram["w_a2"][s]).then_inc(sem(f"a2_w{s}"), 16)
            for s in range(2):
                sp.wait_ge(sem("a2_qk"), B * (s + 1))
                sp.wait_ge(sem("a2_v"), B * (s + 1))
                sp.dma_start(w2[s], dram["w_a2"][2 + s]).then_inc(sem(f"a2_w{s}"), 16)

        def a2_pe(pe):
            n2.pe(pe)
            pe.wait_ge(*n2.done())
            with pe.Fori(0, 2) as mm:
                base = mm * UA2

                def project(j):
                    s, b = j // B, j % B
                    if b == 0:
                        pe.wait_ge(sem(f"a2_w{s}"), 16 * mm + 16)
                    if j >= 2:
                        pe.wait_ge(sem("a2_g1"), base + j - 1)
                        pe.wait_ge(sem("a2_k1"), base + j - 1)
                    for i in range(3):
                        for k in range(C):
                            mmul = pe.matmul(ps[:, i, 0:N], w2[s][:, (i * C + k) * P:(i * C + k + 1) * P],
                                             XN[:, k, b * N:(b + 1) * N], start=(k == 0), stop=(k == C - 1))
                        if i:
                            mmul.then_inc(sem("a2_proj"), 1)

                def score(j, i):
                    if i:
                        pe.wait_ge(sem("a2_e0"), base + j + 1)
                    else:
                        pe.wait_ge(sem("a2_qk"), base + j + 1)
                        if j:
                            pe.wait_ge(sem("a2_e1"), base + j)
                    pe.nop(nofuse=True)
                    for h in range(H4):
                        r = slice(32 * h, 32 * h + 32)
                        mmul = pe.matmul(ps[:, 4 + h, 0:N], q2[j % 2][r, i * P:(i + 1) * P], k2[j % 2][r, :], start=True, stop=True)
                    mmul.then_inc(sem(f"a2_s{i}"), 1)

                def values(j):
                    pe.wait_ge(sem("a2_v"), base + j + 1)
                    pe.wait_ge(sem("a2_last"), base + j + 1)
                    if j >= 2:
                        pe.wait_ge(sem("a2_taken"), base + j - 1)
                    for t in range(2):
                        pe.transpose(ps[:, 3, t * P:(t + 1) * P], v2[j % 2][:, t * P:(t + 1) * P], ident)
                    pe.transpose(ps[0:H4, 3, 2 * P:3 * P], vl2, ident).then_inc(sem("a2_vt"), 1)

                def last(j):
                    pe.wait_ge(sem("a2_vsb"), base + j + 1)
                    pe.matmul(ps[0:H4, 3, 0:N], ql2, k2[j % 2], start=True, stop=True).then_inc(sem("a2_sl"), 1)

                def turn(j, i):
                    pe.wait_ge(sem(f"a2_p{i}"), base + j + 1)
                    if i:
                        pe.wait_ge(sem("a2_g0"), base + j + 1)
                        pe.wait_ge(sem("a2_k0"), base + j + 1)
                    elif j + 1 < UA2:
                        pe.wait_ge(sem("a2_v"), base + j + 2)
                    for h in range(H4):
                        for t in range(2):
                            pe.transpose(ps[:, t, h * P:(h + 1) * P], pr2[i][:, h, t * P:(t + 1) * P], ident)
                    if i == 0:
                        pe.wait_ge(sem("a2_pl"), base + j + 1)
                        pe.nop(nofuse=True)
                        for t in range(2):
                            pe.transpose(ps[:, 2, 300 + H4 * t:300 + H4 * (t + 1)], pl2[:, t * P:(t + 1) * P], ident[0:H4, 0:H4])
                    pe.transpose(ps[0:H4, 2, i * P:(i + 1) * P], pr2[i][:, :, N - 1], ident).then_inc(sem(f"a2_t{i}"), 1)

                def mix(j):
                    pe.wait_ge(sem("a2_g1"), base + j + 1)
                    pe.wait_ge(sem("a2_k1"), base + j + 1)
                    if j + 1 < UA2:
                        pe.wait_ge(sem("a2_el"), base + j + 2)
                    for h in range(H4):
                        for t in range(2):
                            pe.matmul(ps[32 * h:32 * h + 32, 3, 0:N], vt2[j % 2][:, t, 32 * h:32 * h + 32], pt2v[:, t, h, :],
                                      start=(t == 0), stop=(t == 1))
                    pe.matmul(ps[:, 3, 0:N], vr2[j % 2], pk2[j % 2], start=False, stop=True, skip_group_check=True).then_inc(sem("a2_o"), 1)

                def output(j):
                    c = j // B
                    pe.wait_ge(sem("a2_os"), base + j + 1)
                    pe.matmul(ps[64 * c:64 * c + 64, 3, 0:N], const("unpad")[:, 0:64], os2, start=True, stop=True).then_inc(sem("a2_y"), 1)

                project(0)
                values(0)
                score(0, 0)
                last(0)
                for j in range(UA2):
                    if j + 1 < UA2:
                        project(j + 1)
                    score(j, 1)
                    if j:
                        mix(j - 1)
                    turn(j, 0)
                    if j:
                        output(j - 1)
                    if j + 1 < UA2:
                        score(j + 1, 0)
                    turn(j, 1)
                    if j + 1 < UA2:
                        values(j + 1)
                        last(j + 1)
                mix(UA2 - 1)
                output(UA2 - 1)
                pe.wait_ge(sem("a2_taken"), base + UA2)

        def a2_act(act):
            n2.act(act)
            with act.Fori(0, 2) as mm:
                base = mm * UA2

                def take(j):
                    act.wait_ge(sem("a2_proj"), 2 * base + 2 * j + 1)
                    act.copy(q2[j % 2], ps[:, 0, 0:N])
                    act.copy(k2[j % 2], ps[:, 1, 0:N]).then_inc(sem("a2_qk"), 1)
                    act.wait_ge(sem("a2_proj"), 2 * base + 2 * j + 2)
                    act.copy(v2[j % 2], ps[:, 2, 0:N]).then_inc(sem("a2_v"), 1)

                def exps(j, i):
                    act.wait_ge(sem(f"a2_m{i}"), base + j + 1)
                    for h in range(H4):
                        e = act.activation(pr2[i][:, h, :], ps[:, 4 + h, 0:N], ACT.Exp, bias=nm2[:, i, h:h + 1], scale=QS,
                                           accum_out=sm2[:, i, h:h + 1])
                    e.then_inc(sem(f"a2_e{i}"), 1)

                def take_keys(j, i):
                    act.wait_ge(sem(f"a2_t{i}"), base + j + 1)
                    act.copy(pt2v[:, 1, :, i * P:(i + 1) * P], ps[:, 1, :].rearrange("p (h q) -> p h q", q=P)).then_inc(sem(f"a2_k{i}"), 1)

                def exp_last(j):
                    act.wait_ge(sem("a2_ml"), base + j + 1)
                    act.activation(pl2, ps[0:H4, 3, 0:N], ACT.Exp, bias=ml2[:, 1:2], scale=QS, accum_out=ml2[:, 2:3])\
                        .then_inc(sem("a2_el"), 1)

                take(0)
                exps(0, 0)
                exp_last(0)
                for j in range(UA2):
                    if j + 1 < UA2:
                        take(j + 1)
                    exps(j, 1)
                    take_keys(j, 0)
                    if j + 1 < UA2:
                        exps(j + 1, 0)
                    take_keys(j, 1)
                    if j + 1 < UA2:
                        exp_last(j + 1)

        def a2_dve(dve):
            n2.dve(dve)
            dve.wait_ge(*n2.done())
            with dve.Fori(0, 2) as mm:
                base = mm * UA2

                def by_head(j):
                    dve.wait_ge(sem("a2_v"), base + j + 1)
                    dve.tensor_scalar(ql2, const("block4"), q2[j % 2][:, N - 1:N], None, ALU.mult)
                    dve.tensor_scalar(vl2, const("block4"), v2[j % 2][:, N - 1:N], None, ALU.mult).then_inc(sem("a2_last"), 1)

                def values(j):
                    dve.wait_ge(sem("a2_vt"), base + j + 1)
                    dve.tensor_copy(vt2[j % 2], ps[:, 3, 0:2 * P].rearrange("p (a b) -> p a b", b=P))
                    dve.tensor_copy(vr2[j % 2], ps[0:H4, 3, 2 * P:3 * P]).then_inc(sem("a2_vsb"), 1)

                def maxima(j, i):
                    dve.wait_ge(sem(f"a2_s{i}"), base + j + 1)
                    dve.tensor_reduce(mx2[:, i, :], ps[:, 4:8, 0:N], AX.X, ALU.max, negate=True).then_inc(sem(f"a2_x{i}"), 1)
                    dve.wait_ge(sem(f"a2_x{i}"), base + j + 1)
                    dve.tensor_scalar(nm2[:, i, :], mx2[:, i, :], QS, None, ALU.mult).then_inc(sem(f"a2_m{i}"), 1)

                def max_last(j):
                    dve.wait_ge(sem("a2_sl"), base + j + 1)
                    dve.tensor_reduce(ml2[:, 0:1], ps[0:H4, 3, 0:N], AX.X, ALU.max, negate=True).then_inc(sem("a2_xl"), 1)
                    dve.wait_ge(sem("a2_xl"), base + j + 1)
                    dve.tensor_scalar(ml2[:, 1:2], ml2[:, 0:1], QS, None, ALU.mult).then_inc(sem("a2_ml"), 1)

                def normalise(j, i):
                    dve.wait_ge(sem(f"a2_e{i}"), base + j + 1)
                    dve.reciprocal(rs2[:, i, :], sm2[:, i, :]).then_inc(sem(f"a2_r{i}"), 1)
                    dve.wait_ge(sem(f"a2_r{i}"), base + j + 1)
                    dve.tensor_tensor(pr2[i], pr2[i], spread(rs2[:, i, :], N), ALU.mult).then_inc(sem(f"a2_p{i}"), 1)

                def normalise_last(j):
                    dve.wait_ge(sem("a2_el"), base + j + 1)
                    dve.reciprocal(ml2[:, 3:4], ml2[:, 2:3]).then_inc(sem("a2_rl"), 1)
                    dve.wait_ge(sem("a2_rl"), base + j + 1)
                    dve.tensor_scalar(pl2, pl2, ml2[:, 3:4], None, ALU.mult).then_inc(sem("a2_pl"), 1)
                    dve.wait_ge(sem("a2_pl"), base + j + 1)
                    dve.tensor_copy(pk2[j % 2][:, N - 1:N], pl2[:, N - 1:N])

                def take(j, i):
                    dve.wait_ge(sem(f"a2_t{i}"), base + j + 1)
                    dve.tensor_copy(pt2v[:, 0, :, i * P:(i + 1) * P], ps[:, 0, :].rearrange("p (h q) -> p h q", q=P))
                    if i == 0:
                        dve.tensor_copy(pt2v[:, :, :, N - 1], ps[:, 2, 300:300 + 2 * H4].rearrange("p (t h) -> p t h", h=H4))
                    dve.tensor_copy(pk2[j % 2][:, i * P:(i + 1) * P], ps[0:H4, 2, i * P:(i + 1) * P]).then_inc(sem(f"a2_g{i}"), 1)

                def heads_out(j):
                    dve.wait_ge(sem("a2_o"), base + j + 1)
                    dve.tensor_copy(os2, ps[:, 3, 0:N]).then_inc(sem("a2_os"), 1)

                def add(j):
                    c, b = j // B, j % B
                    r = slice(64 * c, 64 * c + 64)
                    dve.wait_ge(sem("a2_y"), base + j + 1)
                    h = HT[r, bass.ds(mm, 1), b * N:(b + 1) * N].rearrange("p a n -> p (a n)")
                    dve.tensor_tensor(h, h, ps[r, 3, 0:N], ALU.add).then_inc(sem("a2_taken"), 1)

                by_head(0)
                values(0)
                maxima(0, 0)
                max_last(0)
                normalise(0, 0)
                normalise_last(0)
                for j in range(UA2):
                    maxima(j, 1)
                    if j + 1 < UA2:
                        by_head(j + 1)
                    if j:
                        heads_out(j - 1)
                    take(j, 0)
                    normalise(j, 1)
                    if j:
                        add(j - 1)
                    if j + 1 < UA2:
                        maxima(j + 1, 0)
                    take(j, 1)
                    if j + 1 < UA2:
                        values(j + 1)
                        max_last(j + 1)
                        normalise(j + 1, 0)
                        normalise_last(j + 1)
                heads_out(UA2 - 1)
                add(UA2 - 1)

        h_a2 = [(sem("a2_taken"), 4 * B)]

        f2 = Layer(FFNS[2], lambda c: h_a2)
        h_f2 = f2.done()

        def f2_sp(sp):
            f2.sp(sp)

        def f2_pe(pe):
            f2.pe(pe)

        def f2_act(act):
            f2.act(act)

        def f2_dve(dve):
            f2.dve(dve)

        def f2_pool(pool):
            f2.pool(pool)

        n3 = Norm(HT, XN, lambda c: h_f2)
        DI, NS, KT = 512, 16, 4
        NH = NS // 2
        ar = Arena()
        u3, r3, d3 = ar.take(KT, T), ar.take(KT, T), ar.take(KT, T)
        at_bufs = ar.at
        hb3 = [ar.take(NH * N) for _ in range(4)]
        bc3 = [[x[:, :, :].rearrange("p c t -> p (c t)")[:, 0:NH * N] for x in (XN, XN2, XC, SQ)],
               [ar.take(NH * N) for _ in range(4)]]
        al = Arena()
        al.at = at_bufs
        win3, wde3, wbc3 = al.take(C, 2 * DI), al.take(KT, DI), al.take(KT, 2 * NS)
        ab3 = al.take(KT, T)
        bct3 = al.take(T, rows=2 * NS)
        dA3 = [ar.take(NH * N) for _ in range(2)]
        wo3 = watt[0][:, 0:KT * D].rearrange("p (k d) -> p k d", d=D)
        a3c = watt[0][:, KT * D:KT * D + 64]
        a3e = watt[0][:, KT * D + 64:KT * D + 128]
        du3 = [watt[1][:, N * i:N * (i + 1)] for i in range(2)]
        y3 = [watt[1][:, N * (2 + i):N * (3 + i)] for i in range(2)]
        bcd = nc.dram_tensor("state_rows", (2 * NS, T), f32, kind="Internal").ap()
        UB = 4 * KT

        def bc_load(sp, b, s):
            for i in range(4):
                src = bcd[NH * i:NH * (i + 1), b * N:(b + 1) * N] if isinstance(b, int) else bcd[NH * i:NH * (i + 1), bass.ds(b * N, N)]
                dst = bc3[s][i].rearrange("p (n t) -> p n t", t=N)
                sp.dma_start(dst, src.unsqueeze(0).broadcast_to([P, NH, N])).then_inc(sem(f"a3_bc{s}"), 16)

        def a3_sp(sp):
            sp.wait_ge(*h_f2[0])
            sp.dma_start(win3, dram["w3_in"]).then_inc(sem("a3_w"), 16)
            sp.dma_start(wde3, dram["w3_delta"]).then_inc(sem("a3_w"), 16)
            sp.dma_start(wbc3, dram["w3_bc"]).then_inc(sem("a3_w"), 16)
            sp.dma_start(wo3, dram["w3_out"]).then_inc(sem("a3_w"), 16)
            sp.wait_ge(sem("a3_bct"), NC)
            sp.dma_start(bcd, bct3).then_inc(sem("a3_bcd"), 16)
            sp.wait_ge(sem("a3_bcd"), 16)
            bc_load(sp, 0, 0)
            sp.wait_ge(sem("a3_delta"), 2)
            bc_load(sp, 1, 1)
            for s in range(2):
                sp.wait_ge(sem("a3_hc"), 2 * KT * (s + 1))
                bc_load(sp, 2 + s, s)

        def a3_pe(pe):
            n3.pe(pe)
            pe.wait_ge(*n3.done())
            pe.wait_ge(sem("a3_w"), 64)
            n = 0
            for m in range(2 * KT):
                for t0, w in CHUNKS:
                    if n >= 4:
                        pe.wait_ge(sem("a3_in"), n - 3)
                    for k in range(C):
                        mmul = pe.matmul(ps[:, n % 4, 0:w], win3[:, k, m * P:(m + 1) * P], XN[:, k, t0:t0 + w], start=(k == 0), stop=(k == C - 1))
                    mmul.then_inc(sem("a3_inps"), 1)
                    n += 1
            for c, (t0, w) in enumerate(CHUNKS):
                for k in range(KT):
                    mmul = pe.matmul(ps[0:2 * NS, 4 + c, 0:w], wbc3[:, k, :], u3[:, k, t0:t0 + w], start=(k == 0), stop=(k == KT - 1))
                mmul.then_inc(sem("a3_bcps"), 1)
            n = 0
            pe.wait_ge(sem("a3_in"), 2 * KT * NC)
            for m in range(KT):
                for t0, w in CHUNKS:
                    if n >= 4:
                        pe.wait_ge(sem("a3_pre"), n - 3)
                    for k in range(KT):
                        mmul = pe.matmul(ps[:, n % 4, 0:w], wde3[:, k, m * P:(m + 1) * P], u3[:, k, t0:t0 + w], start=(k == 0), stop=(k == KT - 1))
                    mmul.then_inc(sem("a3_deps"), 1)
                    n += 1
            pe.wait_ge(sem("a3_pre"), KT * NC)
            pe.wait_ge(sem("a3_bct"), NC)
            pe.sem_inc(sem("a3_sum"), 4)
            with pe.Fori(0, 2) as bb:
                base = UB * bb

                def total(s, ct, hf):
                    n = 8 * s + 2 * ct + hf
                    pe.wait_ge(sem("a3_hc"), base + n + 1)
                    if hf == 0:
                        pe.wait_ge(sem("a3_yfree"), 2 * KT * bb + KT * s + ct + 1)
                    for i in range(NH):
                        mmul = pe.matmul(ps[:, ct % 2, 0:N], ident, hb3[n % 4][:, i * N:(i + 1) * N],
                                         start=(hf == 0 and i == 0), stop=(hf == 1 and i == NH - 1))
                    mmul.then_inc(sem("a3_sum"), 1)

                def output(s, ct):
                    pe.wait_ge(sem("a3_y"), 2 * KT * bb + KT * s + ct + 1)
                    if ct == 0:
                        pe.wait_ge(sem("a3_added"), 2 * bb + s + 1)
                    for d in range(C):
                        mmul = pe.matmul(ps[:, 4 + 2 * s + d, 0:N], wo3[:, ct, d * P:(d + 1) * P], y3[ct % 2], start=(ct == 0), stop=(ct == KT - 1))
                    mmul.then_inc(sem("a3_o"), 1)

                last = None
                for s in range(2):
                    for ct in range(KT):
                        total(s, ct, 0)
                        if last:
                            output(*last)
                        total(s, ct, 1)
                        last = (s, ct)
                output(*last)

        def a3_act(act):
            n3.act(act)
            act.activation(a3e, vec("A_log"), ACT.Exp).then_inc(sem("a3_ae"), 1)
            n = 0
            for m in range(2 * KT):
                dst = u3[:, m, :] if m < KT else r3[:, m - KT, :]
                for t0, w in CHUNKS:
                    act.wait_ge(sem("a3_inps"), n + 1)
                    act.activation(dst[:, t0:t0 + w], ps[:, n % 4, 0:w], ACT.Silu).then_inc(sem("a3_in"), 1)
                    n += 1
            for c, (t0, w) in enumerate(CHUNKS):
                act.wait_ge(sem("a3_bcps"), c + 1)
                act.copy(bct3[:, t0:t0 + w], ps[0:2 * NS, 4 + c, 0:w]).then_inc(sem("a3_bct"), 1)
            for half in range(2):
                m = slice(2 * half, 2 * half + 2)
                act.wait_ge(sem("a3_pre"), 2 * NC * (half + 1))
                act.activation(ab3[:, m, :], d3[:, m, :], ACT.Abs).then_inc(sem("a3_abs"), 1)
                act.wait_ge(sem("a3_abs"), half + 1)
                act.activation(ab3[:, m, :], ab3[:, m, :], ACT.Exp, scale=-1.0).then_inc(sem("a3_sp"), 1)
                act.wait_ge(sem("a3_sp"), 2 * half + 1)
                act.activation(ab3[:, m, :], ab3[:, m, :], ACT.Ln, bias=1.0).then_inc(sem("a3_sp"), 1)
            act.wait_ge(sem("a3_delta"), 2)
            act.wait_ge(sem("a3_a"), 3)
            with act.Fori(0, 2) as bb:
                base = UB * bb
                for s in range(2):
                    for ct in range(KT):
                        for hf in range(2):
                            n = 8 * s + 2 * ct + hf
                            act.wait_ge(sem("a3_dafree"), base + n + 1)
                            act.nop(nofuse=True)
                            d = d3[:, ct, bass.ds((2 * bb + s) * N + 1, N - 1)]
                            for i in range(NH):
                                col = ct * NS + hf * NH + i
                                e = act.activation(dA3[n % 2][:, i * N + 1:(i + 1) * N], d, ACT.Exp, scale=a3c[:, col:col + 1])
                            e.then_inc(sem("a3_da"), 1)

        def a3_dve(dve):
            n3.dve(dve)
            dve.wait_ge(sem("a3_ae"), 1)
            dve.tensor_scalar(a3c, a3e, -1.0, None, ALU.mult).then_inc(sem("a3_a"), 1)
            for i in range(2):
                dve.memset(dA3[i].rearrange("p (n t) -> p n t", t=N)[:, :, 0:1], 0.0).then_inc(sem("a3_a"), 1)
            n = 0
            for half in range(2):
                for t in range(2 * half, 2 * half + 2):
                    for t0, w in CHUNKS:
                        dve.wait_ge(sem("a3_deps"), n + 1)
                        dve.tensor_scalar(d3[:, t, t0:t0 + w], ps[:, n % 4, 0:w], vec("b_delta")[:, t:t + 1], None, ALU.add)\
                            .then_inc(sem("a3_pre"), 1)
                        n += 1
            for half in range(2):
                m = slice(2 * half, 2 * half + 2)
                dve.wait_ge(sem("a3_sp"), 2 * half + 2)
                dve.scalar_tensor_tensor(d3[:, m, :], d3[:, m, :], 0.0, ab3[:, m, :], ALU.max, ALU.add).then_inc(sem("a3_delta"), 1)
            dve.sem_inc(sem("a3_dafree"), 2)
            dve.sem_inc(sem("a3_yfree"), 2)
            dve.sem_inc(sem("a3_added"), 2)
            with dve.Fori(0, 2) as bb:
                base = UB * bb

                def scan(s, ct, hf):
                    n = 8 * s + 2 * ct + hf
                    h = hb3[n % 4]
                    dve.wait_ge(sem("a3_da"), base + n + 1)
                    dve.wait_ge(sem("a3_dbu"), base + n + 1)
                    dve.tensor_tensor_scan(h, dA3[n % 2], h, 0.0, ALU.mult, ALU.add).then_inc(sem("a3_dafree"), 1)
                    dve.wait_ge(sem("a3_dafree"), base + n + 3)
                    dve.tensor_tensor(h, h, bc3[s][2 + hf], ALU.mult).then_inc(sem("a3_hc"), 1)

                def finish(s, ct):
                    n = 2 * KT * bb + KT * s + ct
                    cols = bass.ds((2 * bb + s) * N, N)
                    dve.wait_ge(sem("a3_sum"), 2 * n + 6)
                    dve.scalar_tensor_tensor(y3[ct % 2], u3[:, ct, cols], vec("D_param")[:, ct:ct + 1], ps[:, ct % 2, 0:N], ALU.mult, ALU.add)\
                        .then_inc(sem("a3_yfree"), 1)
                    dve.wait_ge(sem("a3_yfree"), n + 3)
                    dve.tensor_tensor(y3[ct % 2], y3[ct % 2], r3[:, ct, cols], ALU.mult).then_inc(sem("a3_y"), 1)

                def add(s):
                    h = HT[:, :, bass.ds((2 * bb + s) * N, N)]
                    dve.wait_ge(sem("a3_o"), 2 * KT * bb + KT * (s + 1))
                    dve.tensor_tensor(h, h, ps[:, 4 + 2 * s:6 + 2 * s, 0:N], ALU.add).then_inc(sem("a3_added"), 1)

                last = None
                for s in range(2):
                    for ct in range(KT):
                        scan(s, ct, 0)
                        if last:
                            finish(*last)
                        scan(s, ct, 1)
                        if last and last[1] == KT - 1:
                            add(last[0])
                        last = (s, ct)
                finish(*last)
                add(last[0])

        def a3_pool(pool):
            pool.wait_ge(sem("a3_delta"), 2)
            pool.sem_inc(sem("a3_du"), 1)
            with pool.Fori(0, 2) as bb:
                base = UB * bb
                for s in range(2):
                    cols = bass.ds((2 * bb + s) * N, N)
                    for ct in range(KT):
                        for hf in range(2):
                            n = 8 * s + 2 * ct + hf
                            d = du3[ct % 2]
                            if hf == 0:
                                if ct == 0:
                                    pool.wait_ge(sem(f"a3_bc{s}"), 64 * bb + 64)
                                pool.nop(nofuse=True)
                                pool.tensor_tensor(d, d3[:, ct, cols], u3[:, ct, cols], ALU.mult).then_inc(sem("a3_du"), 1)
                                pool.wait_ge(sem("a3_du"), 2 * KT * bb + KT * s + ct + 2)
                            pool.wait_ge(sem("a3_sum"), base + n + 1)
                            pool.tensor_tensor(hb3[n % 4].rearrange("p (n t) -> p n t", t=N), bc3[s][hf].rearrange("p (n t) -> p n t", t=N),
                                               over(d, NH), ALU.mult).then_inc(sem("a3_dbu"), 1)

        h_a3 = [(sem("a3_added"), B + 2)]

        f3 = Layer(FFNS[3], lambda c: h_a3)
        h_f3 = f3.done()

        def f3_sp(sp):
            f3.sp(sp)

        def f3_pe(pe):
            f3.pe(pe)

        def f3_act(act):
            f3.act(act)

        def f3_dve(dve):
            f3.dve(dve)

        def f3_pool(pool):
            f3.pool(pool)

        def store_sp(sp):
            for s, v in h_f3:
                sp.wait_ge(s, v)
            sp.dma_start(out.rearrange("(c p) t -> p c t", p=P), HT[:, :, :]).then_inc(sem("stored"), 16)
            sp.wait_ge(sem("stored"), 16)

        block = ctx.enter_context(nc.Block())

        @block.sync
        def _(sp):
            tok_sp(sp)
            a0_sp(sp)
            f0_sp(sp)
            a1_sp(sp)
            f1_sp(sp)
            a2_sp(sp)
            f2_sp(sp)
            a3_sp(sp)
            f3_sp(sp)
            store_sp(sp)

        @block.tensor
        def _(pe):
            tok_pe(pe)
            tok_norm.pe(pe)
            a0_pe(pe)
            f0_pe(pe)
            a1_pe(pe)
            f1_pe(pe)
            a2_pe(pe)
            f2_pe(pe)
            a3_pe(pe)
            f3_pe(pe)

        @block.scalar
        def _(act):
            tok_norm.act(act)
            a0_act(act)
            f0_act(act)
            a1_act(act)
            f1_act(act)
            a2_act(act)
            f2_act(act)
            a3_act(act)
            f3_act(act)

        @block.vector
        def _(dve):
            tok_dve(dve)
            tok_norm.dve(dve)
            tok_cls(dve)
            a0_dve(dve)
            f0_dve(dve)
            a1_dve(dve)
            f1_dve(dve)
            a2_dve(dve)
            f2_dve(dve)
            a3_dve(dve)
            f3_dve(dve)

        @block.gpsimd
        def _(pool):
            a0_pool(pool)
            f0_pool(pool)
            f1_pool(pool)
            f2_pool(pool)
            a3_pool(pool)
            f3_pool(pool)


def constants():
    out = np.zeros((P, CONST_W), np.float32)
    r = np.arange(P)

    def put(name, v):
        a, b = CONSTS[name]
        out[:, a:b] = v
    put("ident", np.eye(P))
    put("mean", 1.0 / D)
    put("headones", r[:, None] // 64 == r[None, :] // 64)
    put("expo", np.arange(EMIN, EMAX + 1)[None])
    put("expo_r", np.arange(EMAX, EMIN - 1, -1)[None])
    seen = np.concatenate([np.arange(N)[None] >= r[:, None], np.arange(P, N)[None] >= r[:, None] + P], 1)
    put("causal", seen)
    put("hide", np.where(seen, 0.0, -BIG))
    un = np.zeros((P, 2, 64))
    for p in range(P):
        if p % 32 < 16:
            un[p, 0, 16 * (p // 32) + p % 32] = 1
    un[:, 1] = un[:, 0]
    put("unpad", un.reshape(P, -1))
    put("block4", r[:, None] // 32 == np.arange(4)[None])
    return out


def by_part(a):
    a = np.asarray(a)
    return np.ascontiguousarray(a.reshape((-1, P) + a.shape[1:]).swapaxes(0, 1))


def pack(*parts):
    return np.concatenate([np.asarray(p, np.float32).reshape(P, -1) for p in parts], 1)


def layouts(i):
    i = {k: np.asarray(v) for k, v in i.items()}
    a = {"consts": constants()}
    x = i["x"].reshape(B, 5, 16, 8, 16, 8).transpose(0, 2, 4, 1, 3, 5).reshape(B * D, PF)
    a["xt"] = by_part(np.concatenate([x.T, np.zeros((3 * P - PF, B * D), np.float32)]))
    a["wtok"] = by_part(np.concatenate([i["L0_tok_W"], np.zeros((3 * P - PF, D), np.float32)]))

    def col(v):
        return by_part(v.reshape(-1))

    a["vecs"] = pack(col(i["cls_tok"]), col(i["L0_tok_gamma"]), col(i["L0_attn_ln_gamma"]), col(i["L0_attn_ln_beta"]),
                     col(i["L0_attn_bO"]), col(i["L1_attn_b_o"]), col(i["L0_attn_alpha_logit"]), col(i["L3_attn_b_delta"]),
                     by_part(i["L3_attn_A_log"]), col(i["L3_attn_D_param"]),
                     np.repeat(i["L3_ffn_gate_b"][None], P, 0), np.repeat(i["L2_ffn_e_score_correction_bias"][None], P, 0))
    pairs = []
    for m in range(HP):
        rows = slice(m * P, (m + 1) * P)
        pairs.append(pack(*[by_part(i["L0_attn_W" + n][rows].T) for n in ("Q", "K", "V", "g")],
                          i["L0_attn_WO"][:, rows].T, *[col(i["L0_attn_b" + n][rows]) for n in ("Q", "K", "V", "g")],
                          np.repeat(i["L0_attn_bV"][None, rows], P, 0)))
    a["w_a0"] = np.stack(pairs)
    w, bq = i["L1_attn_W_qkv"].reshape(1024, 3, D), i["L1_attn_b_qkv"].reshape(1024, 3)
    pairs = []
    for m in range(HP):
        rows = slice(m * P, (m + 1) * P)
        pairs.append(pack(*[by_part(w[rows, n].T) for n in range(3)], i["L1_attn_W_o"][:, rows].T,
                          *[col(bq[rows, n]) for n in range(3)], np.repeat(bq[None, rows, 2], P, 0)))
    a["w_a1"] = np.stack(pairs)
    quads = []
    for m in range(4):
        parts = []
        for n in "qkv":
            wt = np.zeros((D, 4, 32), np.float32)
            wt[:, :, 0:16] = i["L2_attn_W" + n][64 * m:64 * m + 64].T.reshape(D, 4, 16)
            parts.append(by_part(wt.reshape(D, P)))
        quads.append(pack(*parts))
    a["w_a2"] = np.stack(quads)
    def ups(mats, biases=()):
        return pack(*[by_part(m) for m in mats], *[col(b) for b in biases])
    f0 = [(i["L0_ffn_w1_shared"], i["L0_ffn_w2_shared"])] + list(zip(i["L0_ffn_w1_routed"], i["L0_ffn_w2_routed"]))
    a["up_f0"] = np.stack([ups([w1]) for w1, _ in f0])
    a["dn_f0"] = np.stack([pack(by_part(w2)) for _, w2 in f0])
    a["up_f1"] = np.stack([ups([i["L1_ffn_W1"][e].T, i["L1_ffn_W3"][e].T], [i["L1_ffn_b1"][e], i["L1_ffn_b3"][e], i["L1_ffn_b2"][e]]) for e in range(16)])
    a["dn_f1"] = np.stack([pack(by_part(i["L1_ffn_W2"][e].T)) for e in range(16)])
    gu = i["L2_ffn_gate_up_proj"]
    a["up_f2"] = np.stack([ups([gu[e, 0:P].T, gu[e, P:].T]) for e in range(32)])
    a["dn_f2"] = np.stack([pack(by_part(i["L2_ffn_down_proj"][e].T)) for e in range(32)])
    a["up_f3"] = np.stack([ups([i["L3_ffn_w1"][e].T], [i["L3_ffn_b1"][e], i["L3_ffn_b2"][e]]) for e in range(8)])
    a["dn_f3"] = np.stack([pack(by_part(i["L3_ffn_w2"][e].T)) for e in range(8)])
    a["wr_f0"] = by_part(i["L0_ffn_w_router"])
    a["wr_f1"] = by_part(i["L1_ffn_Wg"].T)
    a["wr_f2"] = by_part(i["L2_ffn_classifier_weight"].T)
    a["wr_f3"] = by_part(i["L3_ffn_gate_w"].T)
    a["w3_in"] = by_part(i["L3_attn_W_in"])
    a["w3_delta"] = by_part(i["L3_attn_W_delta"])
    a["w3_bc"] = by_part(np.concatenate([i["L3_attn_W_B"], i["L3_attn_W_C"]], 1))
    a["w3_out"] = by_part(i["L3_attn_W_out"])
    return a


def kernel(**inputs):
    import concourse.bacc as bacc
    from concourse.bass_utils import run_bass_kernel_spmd

    nc = bacc.Bacc("TRN2", target_bir_lowering=False, num_devices=1)
    arrays = {f"in_{n}": a for n, a in layouts(inputs).items()}
    dram = {n[3:]: nc.dram_tensor(n, a.shape, mybir.dt.float32, kind="ExternalInput").ap() for n, a in arrays.items()}
    out = nc.dram_tensor("out_0", (D, T), mybir.dt.float32, kind="ExternalOutput").ap()
    build(nc, dram, out)
    r = run_bass_kernel_spmd(nc, [arrays], core_ids=[0])
    return np.ascontiguousarray(np.asarray(r.results[0]["out_0"]).T).reshape(B, N, D)
```
